# Optimizing a Trainium2 kernel written in Bass

```python
import numpy as np
import jax
import jax.numpy as jnp

def _softmax(x, axis=-1):
    return jax.nn.softmax(x, axis=axis)

def _gelu(x):
    return jax.nn.gelu(x, approximate=True)

def _silu(x):
    return jax.nn.silu(x)

def _sigmoid(x):
    return jax.nn.sigmoid(x)

def _layernorm(x, axis=-1, eps=1e-05):
    m = jnp.mean(x, axis=axis, keepdims=True)
    v = jnp.var(x, axis=axis, keepdims=True)
    return (x - m) / jnp.sqrt(v + eps)

def _scatter_add(tgt, idx, src, axis=0):
    return tgt.at[idx].add(src)

def _segment_sum(src, seg, n):
    return jax.ops.segment_sum(src, seg, n)
kernel_name = 'mk_decoder_preln_d1_seqx_r4_77ce01'

def setup_inputs(seed: int=0):
    np.random.seed(seed)
    _w = jnp.asarray

    def _rec_inputs():
        import jax
        import jax.numpy as jnp
        _rk = jax.random.key(seed)
        x = -0.0003929 + 0.9999 * jax.random.normal(jax.random.fold_in(_rk, 1), (8, 256, 512), jnp.float32)
        _lenS = 256 - jax.random.randint(jax.random.fold_in(_rk, 7), (8,), 0, max(1, 256 // 4) + 1, jnp.int32)
        _lenS2 = 256 - jax.random.randint(jax.random.fold_in(_rk, 8), (8,), 0, max(1, 256 // 4) + 1, jnp.int32)
        _ctx_2048P = jax.random.normal(jax.random.fold_in(_rk, 11), (8, 16, 512), jnp.float32)
        _ctx_2048c = jax.random.dirichlet(jax.random.fold_in(_rk, 511), 0.3 * jnp.ones((16,), jnp.float32), (8, 256))
        _ctx_2048t = jnp.einsum('bsk,bkd->bsd', _ctx_2048c, _ctx_2048P)
        _ctx_2048t = _ctx_2048t * jax.lax.rsqrt(jnp.mean(jnp.square(_ctx_2048t)) + 1e-12) * 0.953939
        ctx_2048 = -1.39393e-06 + 0.999914 * (_ctx_2048t + 0.3 * jax.random.normal(jax.random.fold_in(_rk, 611), (8, 256, 512), jnp.float32))
        itok_BxS_0_1023 = jax.random.randint(jax.random.fold_in(_rk, 12), (8, 256), 0, 256, jnp.int32)
        return (x, ctx_2048, itok_BxS_0_1023)
    x, ctx_2048, itok_BxS_0_1023 = _rec_inputs()

    def _L0_attn_setup():
        import jax, jax.numpy as jnp
        import numpy as np
        B, S, D = (2, 1024, 512)
        H, DK, DV = (16, 128, 128)
        SEG = 128
        UPDATE = 'delta'
        CAUSAL = True
        key = jax.random.key(seed)
        ks = jax.random.split(key, 6)
        s = 0.02
        return {'x': jax.random.normal(ks[0], (B, S, D), jnp.float32), 'Wq': jax.random.normal(ks[1], (D, H * DK), jnp.float32) * s, 'Wk': jax.random.normal(ks[2], (D, H * DK), jnp.float32) * s, 'Wv': jax.random.normal(ks[3], (D, H * DV), jnp.float32) * s, 'Wo': jax.random.normal(ks[4], (H * DV, D), jnp.float32) * s, 'betas': jax.random.normal(ks[5], (1, H, 1, DV), jnp.float32)}
    _L0_attn_all = _L0_attn_setup()
    _L0_attn_in = {k: v for k, v in _L0_attn_all.items() if k in ('Wq', 'Wk', 'Wv', 'Wo', 'betas')}
    del _L0_attn_all

    def _L0_xattn_setup():
        import jax, jax.numpy as jnp
        import numpy as np
        B, Lq, Lk = (2, 1024, 256)
        Q_DIM, KV_DIM = (512, 512)
        H, HD = (16, 128)
        KVC, QC, R = (128, 192, 64)
        LOOKBACK = 8
        NEG = -1e+30

        def _rope(x, L):
            half = x.shape[-1] // 2
            inv_freq = 1.0 / 10000.0 ** (jnp.arange(half, dtype=jnp.float32) / half)
            ang = jnp.arange(L, dtype=jnp.float32)[:, None] * inv_freq
            cos, sin = (jnp.cos(ang), jnp.sin(ang))
            x1, x2 = (x[..., :half], x[..., half:])
            return jnp.concatenate([x1 * cos - x2 * sin, x1 * sin + x2 * cos], axis=-1)
        key = jax.random.key(seed)
        ks = jax.random.split(key, 11)

        def w(k, shape, fan_in):
            return jax.random.normal(k, shape, jnp.float32) / np.sqrt(fan_in).astype(np.float32)
        return {'q': jax.random.normal(ks[0], (B, Lq, Q_DIM), jnp.float32), 'kv': jax.random.normal(ks[1], (B, Lk, KV_DIM), jnp.float32), 'seg_id': jnp.sort(jax.random.randint(ks[2], (B, Lq), 0, Lk), axis=-1), 'W_kvc': w(ks[3], (KV_DIM, KVC), KV_DIM), 'W_dq': w(ks[4], (Q_DIM, QC), Q_DIM), 'W_uq': w(ks[5], (QC, H * HD), QC), 'W_qr': w(ks[6], (QC, H * R), QC), 'W_uk': w(ks[7], (KVC, H * HD), KVC), 'W_kr': w(ks[8], (KVC, R), KVC), 'W_uv': w(ks[9], (KVC, H * HD), KVC), 'W_o': w(ks[10], (H * HD, Q_DIM), H * HD)}
    _L0_xattn_all = _L0_xattn_setup()
    _L0_xattn_in = {k: v for k, v in _L0_xattn_all.items() if k in ('W_kvc', 'W_dq', 'W_uq', 'W_qr', 'W_uk', 'W_kr', 'W_uv', 'W_o')}
    del _L0_xattn_all

    def _L0_ffn_setup():
        import jax, jax.numpy as jnp
        import numpy as np

        def fwht(x):
            n = x.shape[-1]
            orig_shape = x.shape
            x = x.reshape(-1, n)
            h = 1
            while h < n:
                x = x.reshape(-1, n // (2 * h), 2, h)
                a = x[:, :, 0, :]
                b = x[:, :, 1, :]
                x = jnp.stack([a + b, a - b], axis=2)
                h *= 2
            x = x.reshape(orig_shape)
            return x * (1.0 / jnp.sqrt(jnp.asarray(n, dtype=x.dtype)))

        def act_quant(x, bits):
            qb = 2.0 ** (bits - 1) - 1.0
            scale = qb / jnp.clip(jnp.max(jnp.abs(x), axis=-1, keepdims=True), 1e-05, None)
            q = jnp.clip(jnp.round(x * scale), -qb, qb) / scale
            return x + jax.lax.stop_gradient(q - x)

        def weight_quant(w):
            scale = jnp.clip(jnp.mean(jnp.abs(w)), 1e-05, None)
            q = jnp.clip(jnp.round(w / scale), -1.0, 1.0) * scale
            return w + jax.lax.stop_gradient(q - w)

        def hbitlinear(x, w, bits):
            xh = fwht(x)
            xq = act_quant(xh, bits)
            wq = weight_quant(w)
            return jnp.einsum('bsh,oh->bso', xq, wq)
        key = jax.random.key(seed)
        k1, k2, k3 = jax.random.split(key, 3)
        B, S, H = (4, 512, 512)
        I = 1024
        hidden_states = jax.random.normal(k1, (B, S, H), dtype=jnp.float32)
        w_up = jax.random.normal(k2, (I, H), dtype=jnp.float32) * 0.02
        w_down = jax.random.normal(k3, (H, I), dtype=jnp.float32) * 0.02
        return {'hidden_states': hidden_states, 'w_up': w_up, 'w_down': w_down}
    _L0_ffn_all = _L0_ffn_setup()
    _L0_ffn_in = {k: v for k, v in _L0_ffn_all.items() if k in ('w_up', 'w_down')}
    del _L0_ffn_all
    return {'x': x, 'ctx_2048': ctx_2048, 'itok_BxS_0_1023': itok_BxS_0_1023, 'L0_attn_Wq': _L0_attn_in['Wq'], 'L0_attn_Wk': _L0_attn_in['Wk'], 'L0_attn_Wv': _L0_attn_in['Wv'], 'L0_attn_Wo': _L0_attn_in['Wo'], 'L0_attn_betas': _L0_attn_in['betas'], 'L0_xattn_W_kvc': _L0_xattn_in['W_kvc'], 'L0_xattn_W_dq': _L0_xattn_in['W_dq'], 'L0_xattn_W_uq': _L0_xattn_in['W_uq'], 'L0_xattn_W_qr': _L0_xattn_in['W_qr'], 'L0_xattn_W_uk': _L0_xattn_in['W_uk'], 'L0_xattn_W_kr': _L0_xattn_in['W_kr'], 'L0_xattn_W_uv': _L0_xattn_in['W_uv'], 'L0_xattn_W_o': _L0_xattn_in['W_o'], 'L0_ffn_w_up': _L0_ffn_in['w_up'], 'L0_ffn_w_down': _L0_ffn_in['w_down']}

def reference(x, ctx_2048, itok_BxS_0_1023, L0_attn_Wq, L0_attn_Wk, L0_attn_Wv, L0_attn_Wo, L0_attn_betas, L0_xattn_W_kvc, L0_xattn_W_dq, L0_xattn_W_uq, L0_xattn_W_qr, L0_xattn_W_uk, L0_xattn_W_kr, L0_xattn_W_uv, L0_xattn_W_o, L0_ffn_w_up, L0_ffn_w_down):
    import jax
    import jax.numpy as jnp

    def _L0_attn_ref(x, Wq, Wk, Wv, Wo, betas):
        import jax, jax.numpy as jnp
        import numpy as np
        B, S, D = (2, 1024, 512)
        H, DK, DV = (16, 128, 128)
        SEG = 128
        UPDATE = 'delta'
        CAUSAL = True
        Bsz, seq, _ = x.shape
        nseg = seq // SEG
        q = (x @ Wq).reshape(Bsz, seq, H, DK).transpose(0, 2, 1, 3)
        k = (x @ Wk).reshape(Bsz, seq, H, DK).transpose(0, 2, 1, 3)
        v = (x @ Wv).reshape(Bsz, seq, H, DV).transpose(0, 2, 1, 3)
        qs = q.reshape(Bsz, H, nseg, SEG, DK).transpose(2, 0, 1, 3, 4)
        ks_ = k.reshape(Bsz, H, nseg, SEG, DK).transpose(2, 0, 1, 3, 4)
        vs = v.reshape(Bsz, H, nseg, SEG, DV).transpose(2, 0, 1, 3, 4)
        causal_mask = jnp.tril(jnp.ones((SEG, SEG), bool))
        scale = DK ** 0.5
        beta = jax.nn.sigmoid(betas)

        def step(carry, seg):
            mem, z = carry
            qq, kk, vv = seg
            sigma_q = jax.nn.elu(qq) + 1.0
            scores = jnp.einsum('bhsk,bhtk->bhst', qq, kk) / scale
            if CAUSAL:
                scores = jnp.where(causal_mask, scores, -jnp.inf)
            att_dot = jax.nn.softmax(scores, axis=-1) @ vv
            att_mem = sigma_q @ mem / (sigma_q @ z)
            sigma_k = jax.nn.elu(kk) + 1.0
            if UPDATE == 'linear':
                mem_new = mem + jnp.einsum('bhsk,bhsv->bhkv', sigma_k, vv)
            else:
                delta = vv - sigma_k @ mem / (sigma_k @ z)
                mem_new = mem + jnp.einsum('bhsk,bhsv->bhkv', sigma_k, delta)
            z_new = z + sigma_k.sum(axis=-2, keepdims=True).transpose(0, 1, 3, 2)
            att = beta * att_mem + (1.0 - beta) * att_dot
            out = att.reshape(Bsz, SEG, H * DV) @ Wo
            return ((mem_new, z_new), out)
        mem0 = jnp.zeros((Bsz, H, DK, DV), x.dtype)
        z0 = jnp.ones((Bsz, H, DK, 1), x.dtype) / DK
        _, outs = jax.lax.scan(step, (mem0, z0), (qs, ks_, vs))
        return outs.transpose(1, 0, 2, 3).reshape(Bsz, seq, D)

    def _L0_xattn_ref(q, kv, seg_id, W_kvc, W_dq, W_uq, W_qr, W_uk, W_kr, W_uv, W_o):
        import jax, jax.numpy as jnp
        import numpy as np
        B, Lq, Lk = (2, 1024, 256)
        Q_DIM, KV_DIM = (512, 512)
        H, HD = (16, 128)
        KVC, QC, R = (128, 192, 64)
        LOOKBACK = 8
        NEG = -1e+30

        def _rope(x, L):
            half = x.shape[-1] // 2
            inv_freq = 1.0 / 10000.0 ** (jnp.arange(half, dtype=jnp.float32) / half)
            ang = jnp.arange(L, dtype=jnp.float32)[:, None] * inv_freq
            cos, sin = (jnp.cos(ang), jnp.sin(ang))
            x1, x2 = (x[..., :half], x[..., half:])
            return jnp.concatenate([x1 * cos - x2 * sin, x1 * sin + x2 * cos], axis=-1)
        b, lq, _ = q.shape
        lk = kv.shape[1]
        kv_c = kv @ W_kvc
        q_c = q @ W_dq
        q_nope = (q_c @ W_uq).reshape(b, lq, H, HD).transpose(0, 2, 1, 3)
        q_rope = (q_c @ W_qr).reshape(b, lq, H, R).transpose(0, 2, 1, 3)
        k_nope = (kv_c @ W_uk).reshape(b, lk, H, HD)
        v = (kv_c @ W_uv).reshape(b, lk, H, HD)
        k_rope = kv_c @ W_kr
        q_rope = _rope(q_rope, lq)
        k_rope = _rope(k_rope, lk)
        scale = 1.0 / np.sqrt(HD + R).astype(np.float32)
        scores = (jnp.einsum('bhqd,bkhd->bhqk', q_nope, k_nope) + jnp.einsum('bhqr,bkr->bhqk', q_rope, k_rope)) * scale
        k_ids = jnp.arange(lk)[None, None, :]
        qs = seg_id[:, :, None]
        good = (k_ids <= qs) & (k_ids >= qs - LOOKBACK)
        scores = jnp.where(good[:, None, :, :], scores, NEG)
        attn = jax.nn.softmax(scores, axis=-1)
        out = jnp.einsum('bhqk,bkhd->bqhd', attn, v).reshape(b, lq, H * HD)
        return out @ W_o

    def _L0_ffn_ref(hidden_states, w_up, w_down):
        import jax, jax.numpy as jnp
        import numpy as np

        def fwht(x):
            n = x.shape[-1]
            orig_shape = x.shape
            x = x.reshape(-1, n)
            h = 1
            while h < n:
                x = x.reshape(-1, n // (2 * h), 2, h)
                a = x[:, :, 0, :]
                b = x[:, :, 1, :]
                x = jnp.stack([a + b, a - b], axis=2)
                h *= 2
            x = x.reshape(orig_shape)
            return x * (1.0 / jnp.sqrt(jnp.asarray(n, dtype=x.dtype)))

        def act_quant(x, bits):
            qb = 2.0 ** (bits - 1) - 1.0
            scale = qb / jnp.clip(jnp.max(jnp.abs(x), axis=-1, keepdims=True), 1e-05, None)
            q = jnp.clip(jnp.round(x * scale), -qb, qb) / scale
            return x + jax.lax.stop_gradient(q - x)

        def weight_quant(w):
            scale = jnp.clip(jnp.mean(jnp.abs(w)), 1e-05, None)
            q = jnp.clip(jnp.round(w / scale), -1.0, 1.0) * scale
            return w + jax.lax.stop_gradient(q - w)

        def hbitlinear(x, w, bits):
            xh = fwht(x)
            xq = act_quant(xh, bits)
            wq = weight_quant(w)
            return jnp.einsum('bsh,oh->bso', xq, wq)
        ACT_BITS = 8
        h = hbitlinear(hidden_states, w_up, ACT_BITS)
        h = jnp.square(jax.nn.relu(h))
        out = hbitlinear(h, w_down, ACT_BITS)
        return out
    x = x + _L0_attn_ref(_layernorm(x, axis=-1), L0_attn_Wq, L0_attn_Wk, L0_attn_Wv, L0_attn_Wo, L0_attn_betas)
    x = x + _L0_xattn_ref(_layernorm(x, axis=-1), ctx_2048, itok_BxS_0_1023, L0_xattn_W_kvc, L0_xattn_W_dq, L0_xattn_W_uq, L0_xattn_W_qr, L0_xattn_W_uk, L0_xattn_W_kr, L0_xattn_W_uv, L0_xattn_W_o)
    x = x + _L0_ffn_ref(_layernorm(x, axis=-1), L0_ffn_w_up, L0_ffn_w_down)
    return x

_drawn_inputs = setup_inputs


def setup_inputs(seed=0):
    import zlib

    import numpy as np

    out = dict(_drawn_inputs(seed))
    spreads = {}
    factors = {'L0_attn_Wq': 7.932, 'L0_attn_Wk': 7.889, 'L0_attn_betas': 3.339}
    for name, (base, spread) in spreads.items():
        noise = np.random.default_rng([zlib.crc32(name.encode()), seed]).standard_normal(out[name].shape)
        drawn = base * np.exp(spread * noise) if base else spread * noise
        out[name] = jnp.asarray(drawn.astype(out[name].dtype))
    for name, factor in factors.items():
        out[name] = (out[name] * factor).astype(out[name].dtype)
    return out
```

```python
from contextlib import ExitStack

import numpy as np

import concourse.bass as bass
from concourse import mybir

F32 = mybir.dt.float32
F32R = mybir.dt.float32r
BF16 = mybir.dt.bfloat16
I32 = mybir.dt.int32
ACT = mybir.ActivationFunctionType
ALU = mybir.AluOpType
AX = mybir.AxisListType

P = 128
TOKENS = 2048
TILES = TOKENS // P
D = 512
KD = D // P
HEADS = 16
PAIRS = HEADS // 2
CHUNK = 512
CHUNKS = TOKENS // CHUNK
CT = CHUNK // P
STEPS = PAIRS * CHUNKS
EPS = 1e-5
NEG = -1e30
ATT_SCALE = float(np.float32(128.0) ** np.float32(-0.5))


def r3(ap, n):
    return ap.rearrange("p (a b) -> p a b", b=n)


def mm3(pe, out, lhs, rhs, first=True, last=True):
    (lh, ll), (rh, rl) = lhs, rhs
    pe.matmul(out, lh, rh, start=first, stop=False)
    pe.matmul(out, lh, rl, start=False, stop=False)
    return pe.matmul(out, ll, rh, start=False, stop=last)


def reuse_semaphores(nc):
    over = sorted(nc.released_uncleared_semaphores)
    with nc.Block() as block:
        @block.gpsimd
        def _(pool):
            pool.sem_clear(range(over[0], over[-1] + 1))


def alone(eng, sem):
    eng.sem_inc(sem, 1)


def statistics(nc, ctx, tag, mv, rstd):
    def sb(name, shape):
        return ctx.enter_context(nc.sbuf_tensor(tag + name, shape, F32))

    S = {n: ctx.enter_context(nc.semaphore(tag + n)) for n in
         ("stats_done", "aggr_done", "var_ready", "std_ready", "rstd_ready")}
    S.update(mv=mv, rstd=rstd, st=sb("st", [P, TILES, 6]), var_eps=sb("var_eps", [P, TILES]),
             std=sb("std", [P, TILES]))
    return S


def statistics_vector(dve, X, S, x_loaded, x_loads):
    for t in range(TILES):
        if x_loaded is not None:
            dve.wait_ge(x_loaded[t // (TILES // x_loads)], 16)
        dve.bn_stats(S["st"][:, t, :], X[:, t, :]).then_inc(S["stats_done"], 1)
    for t in range(TILES):
        dve.wait_ge(S["stats_done"], t + 1)
        dve.bn_aggr(S["mv"][:, t, :], S["st"][:, t, :]).then_inc(S["aggr_done"], 1)
    std, rstd, done = S["std"], S["rstd"], S["rstd_ready"]
    dve.wait_ge(S["aggr_done"], TILES)
    dve.tensor_scalar(S["var_eps"][:, :], S["mv"][:, :, 1], EPS, None, ALU.add).then_inc(S["var_ready"], 1)
    dve.wait_ge(S["std_ready"], 1)
    dve.reciprocal(rstd[:, :], std[:, :]).then_inc(done, 1)
    dve.wait_ge(done, 1)
    dve.tensor_tensor(std[:, :], rstd[:, :], rstd[:, :], ALU.mult).then_inc(done, 1)
    dve.wait_ge(done, 2)
    dve.tensor_tensor(std[:, :], std[:, :], S["var_eps"][:, :], ALU.mult).then_inc(done, 1)
    dve.wait_ge(done, 3)
    dve.tensor_scalar(std[:, :], std[:, :], -0.5, 1.5, ALU.mult, ALU.add).then_inc(done, 1)
    dve.wait_ge(done, 4)
    dve.tensor_tensor(rstd[:, :], rstd[:, :], std[:, :], ALU.mult).then_inc(done, 1)
    dve.wait_ge(done, 5)


def statistics_scalar(act, S):
    act.wait_ge(S["var_ready"], 1)
    act.activation(S["std"][:, :], S["var_eps"][:, :], ACT.Sqrt).then_inc(S["std_ready"], 1)


def layernorm_transposed(nc, X, x_loaded, x_loads, ident, tag, hi, lo):
    with ExitStack() as ctx:
        def sb(name, shape, dt=F32):
            return ctx.enter_context(nc.sbuf_tensor(tag + name, shape, dt))

        def sem(name):
            return ctx.enter_context(nc.semaphore(tag + name))

        mv = sb("mv", [P, TILES, 2])
        rstd = sb("rstd", [P, TILES])
        S = statistics(nc, ctx, tag, mv, rstd)
        xn = sb("xn", [P, 2, D])
        turned = [ctx.enter_context(nc.psum_tensor(f"{tag}turned{i}", [P, D], F32)) for i in range(2)]
        xn_ready = sem("xn_ready")
        lone = sem("lone")
        turned_ready = sem("turned_ready")
        hi_written = sem("hi_written")
        lo_written = sem("lo_written")
        block = ctx.enter_context(nc.Block())

        @block.vector
        def _(dve):
            statistics_vector(dve, X, S, x_loaded, x_loads)

            def normalize(t, i):
                dve.tensor_scalar(xn[:, i, :], X[:, bass.ds(t, 1), :].rearrange("p a n -> p (a n)"),
                                  mv[:, bass.ds(t, 1), 0], rstd[:, bass.ds(t, 1)],
                                  ALU.subtract, ALU.mult).then_inc(xn_ready, 1)

            normalize(0, 0)
            normalize(1, 1)
            with dve.Fori(0, TILES // 2) as it:
                for i in range(2):
                    t = 2 * it + i
                    dve.wait_ge(hi_written, t + 1)
                    dve.tensor_tensor(lo[:, :, bass.ds(t * P, P)], r3(turned[i][:, :], P),
                                      hi[:, :, bass.ds(t * P, P)].bitcast(F32),
                                      ALU.subtract).then_inc(lo_written, 1)
                    normalize((t + 2) % TILES, i)

        @block.scalar
        def _(act):
            statistics_scalar(act, S)
            with act.Fori(0, TILES // 2) as it:
                for i in range(2):
                    t = 2 * it + i
                    act.wait_ge(turned_ready, t + 1)
                    alone(act, lone)
                    act.activation(hi[:, :, bass.ds(t * P, P)], r3(turned[i][:, :], P),
                                   ACT.Copy).then_inc(hi_written, 1)

        @block.tensor
        def _(pe):
            def turn(t, i):
                pe.wait_ge(xn_ready, t + 1)
                for k in range(KD):
                    mm = pe.transpose(turned[i][:, k * P:(k + 1) * P], xn[:, i, k * P:(k + 1) * P],
                                      ident[:, :])
                mm.then_inc(turned_ready, 1)

            turn(0, 0)
            turn(1, 1)
            with pe.Fori(1, TILES // 2) as it:
                for i in range(2):
                    pe.wait_ge(lo_written, 2 * it + i - 1)
                    turn(2 * it + i, i)


def segment_attention(nc, X, ident, xT, d, consts_loaded, attT):
    with ExitStack() as ctx:
        def sb(name, shape, dt=F32):
            return ctx.enter_context(nc.sbuf_tensor("a_" + name, shape, dt))

        def parts(name, shape):
            return sb(name + "_hi", shape, F32R), sb(name + "_lo", shape, F32R)

        def sem(name):
            return ctx.enter_context(nc.semaphore("a_" + name))

        def psum(name):
            return ctx.enter_context(nc.psum_tensor("a_" + name, [P, 512], F32))

        def both(pair, *index):
            return pair[0][index], pair[1][index]

        ones = sb("ones", [P, P])
        ones_r = sb("ones_r", [P, P], F32R)
        z_start = sb("z_start", [P, P], F32R)
        mask = sb("mask", [P, P])
        betas = sb("betas", [P, HEADS])
        beta_e = sb("beta_e", [P, HEADS])
        gate = sb("gate", [P, HEADS, 2])
        gate_p = sb("gate_p", [P, 2, 2])
        w_raw = {n: sb("raw_" + n, [P, 1024]) for n in "qkv"}
        w = {n: parts("w" + n, [P, KD, 256]) for n in "qkv"}
        qT = parts("qT", [P, 2, CHUNK])
        kT = parts("kT", [P, 2, CHUNK])
        v = parts("v", [P, CT, 256])
        e = sb("e", [P, 2, 256])
        sq = sb("sq", [P, 2, 256])
        sk = sb("sk", [P, 2, 256])
        sqp = [parts(f"sq{i}", [P, 2, 256]) for i in range(2)]
        skp = parts("skt", [P, 4, P])
        prob = sb("prob", [P, 2, CT, P])
        probT = parts("probT", [P, 2, CT * P])
        mx = sb("mx", [P, 2, CT])
        nb = sb("nb", [P, 2, CT])
        rs = sb("rs", [P, 2, CT])
        rr = sb("rr", [P, 2, CT])
        mem = parts("mem", [P, 2, 512])
        att = sb("att", [P, 2, CHUNK])
        rec = sb("rec", [P, 256])
        amr = sb("amr", [P, 256])

        bank = [psum("bank0"), psum("bank1")]
        s_ps = [psum("s0"), psum("s1")]
        mem_ps = [psum("mem0"), psum("mem1")]
        ad_ps = [psum("ad0"), psum("ad1")]

        raw_loaded = {n: sem("raw_loaded_" + n) for n in "qkv"}
        w_split = {n: sem("w_split_" + n) for n in "qkv"}
        w_hi = sem("w_hi")
        ones_ready = sem("ones_ready")
        beta_step = sem("beta_step")
        gate_ready = sem("gate_ready")
        filled = sem("filled")
        hi_done = sem("hi_done")
        freed = sem("freed")
        sig_done = sem("sig_done")
        sq_hi = sem("sq_hi")
        sq_ready = sem("sq_ready")
        s_done = sem("s_done")
        max_done = sem("max_done")
        nb_done = sem("nb_done")
        exp_done = sem("exp_done")
        rr_done = sem("rr_done")
        p_ready = sem("p_ready")
        pt_done = sem("pt_done")
        pt_hi = sem("pt_hi")
        pt_ready = sem("pt_ready")
        skt_done = sem("skt_done")
        skt_hi = sem("skt_hi")
        sk_ready = sem("sk_ready")
        mem_done = sem("mem_done")
        mem_hi = sem("mem_hi")
        mem_ready = sem("mem_ready")
        ad_done = sem("ad_done")
        ad_read = sem("ad_read")
        am_done = sem("am_done")
        rec_done = sem("rec_done")
        amr_done = sem("amr_done")
        att_done = sem("att_done")
        att_stored = sem("att_stored")
        wo_loaded = sem("wo_loaded")
        lone = {n: sem("lone_" + n) for n in ("dve", "pool")}
        block = ctx.enter_context(nc.Block())

        Q, K, V = 0, 2, 4

        def fill(chunk, kind, j):
            return 6 * chunk + kind + j

        def over_steps(eng, step):
            step(0, 0, True)
            with eng.Fori(0, PAIRS - 1) as p:
                for c in range(1, CHUNKS + 1):
                    step(CHUNKS * p + c, c % CHUNKS, True)
            for g in range(STEPS - CHUNKS + 1, STEPS):
                step(g, g % CHUNKS, g < STEPS - 1)

        def seg(ap, s):
            return ap.rearrange("p (b s t) -> p b s t", b=2, s=2)[:, :, s, :]

        @block.sync
        def _(sp):
            sp.dma_start(mask[:, :], d["causal"]).then_inc(consts_loaded, 16)
            sp.dma_start(betas[:, :], d["betas"]).then_inc(consts_loaded, 16)
            for n in "qkv":
                sp.dma_start(w_raw[n][:, :], d["w" + n][0]).then_inc(raw_loaded[n], 16)

            sp.dma_start(X[:, :, :], d["wo"]).then_inc(wo_loaded, 16)

            def store(g):
                sp.wait_ge(att_done, 2 * g + 2)
                sp.dma_start(attT[g], att[:, :, :]).then_inc(att_stored, 16)

            def load(n, p):
                sp.wait_ge(w_split[n], p + 1)
                sp.dma_start(w_raw[n][:, :], d["w" + n][p + 1]).then_inc(raw_loaded[n], 16)

            with sp.Fori(0, PAIRS - 1) as p:
                for n in "qkv":
                    load(n, p)
                for c in range(CHUNKS):
                    store(CHUNKS * p + c)
            for g in range(STEPS - CHUNKS, STEPS):
                store(g)
            sp.wait_ge(att_stored, 16 * STEPS)
            sp.wait_ge(wo_loaded, 16)

        @block.gpsimd
        def _(pool):
            pool.memset(ones[:, :], 1.0).then_inc(ones_ready, 1)
            pool.wait_ge(ones_ready, 1)
            pool.tensor_copy(ones_r[:, :], ones[:, :]).then_inc(ones_ready, 1)
            pool.tensor_scalar(z_start[:, :], ones[:, :], 1.0 / (P * P), None,
                               ALU.mult).then_inc(ones_ready, 1)

            def split(n, raw, loads, dst, p, splits):
                flat = [x[:, :, :].rearrange("p a b -> p (a b)") for x in dst]
                pool.wait_ge(raw_loaded[raw], 16 * loads)
                alone(pool, lone["pool"])
                pool.tensor_copy(flat[0], w_raw[raw][:, :]).then_inc(w_hi, 1)
                pool.wait_ge(w_hi, splits)
                pool.tensor_tensor(flat[1], w_raw[raw][:, :], flat[0].bitcast(F32),
                                   ALU.subtract).then_inc(w_split[n], 1)

            def take_gate(p):
                pool.wait_ge(gate_ready, 1)
                pool.tensor_copy(gate_p[:, :, :], gate[:, bass.ds(2 * p, 2), :]).then_inc(gate_ready, 1)

            for i, n in enumerate("qkv"):
                split(n, n, 1, w[n], 0, i + 1)

            def step(g, c, nxt):
                if c == 0:
                    if not (isinstance(g, int) and g == 0):
                        pool.wait_ge(att_done, 2 * g)
                    take_gate(pair_of[0])
                for h in range(2):
                    pool.wait_ge(rr_done, 2 * g + h + 1)
                    pool.tensor_tensor(prob[:, h], prob[:, h],
                                       rr[:, h, :].unsqueeze(2).to_broadcast([P, CT, P]),
                                       ALU.mult).then_inc(p_ready, 1)
                if nxt:
                    split_sq(g + 1, (c + 1) % 2)
                p = pair_of[0]
                if c == 2 and not (isinstance(p, int) and p == PAIRS - 1):
                    for i, (n, kind) in enumerate((("q", Q), ("k", K), ("v", V))):
                        pool.wait_ge(filled, fill(g + 1, kind, 1) + 1)
                        split(n, n, p + 2, w[n], p + 1, 3 * p + 4 + i)

            def split_sq(g, par):
                pool.wait_ge(sig_done, 4 * g + 2)
                alone(pool, lone["pool"])
                hi, lo = sqp[par]
                pool.tensor_copy(hi[:, :, :], sq[:, :, :]).then_inc(sq_hi, 1)
                pool.wait_ge(sq_hi, g + 1)
                pool.tensor_tensor(lo[:, :, :], sq[:, :, :], hi[:, :, :].bitcast(F32),
                                   ALU.subtract).then_inc(sq_ready, 1)

            split_sq(0, 0)
            pair_of = [0]
            step(0, 0, True)
            with pool.Fori(0, PAIRS - 1) as p:
                for c in range(1, CHUNKS + 1):
                    pair_of[0] = p + c // CHUNKS
                    step(CHUNKS * p + c, c % CHUNKS, True)
            pair_of[0] = PAIRS - 1
            for g in range(STEPS - CHUNKS + 1, STEPS):
                step(g, g % CHUNKS, g < STEPS - 1)

        @block.scalar
        def _(act):
            act.wait_ge(consts_loaded, 48)
            act.activation(beta_e[:, :], betas[:, :], ACT.Exp, scale=-1.0).then_inc(beta_step, 1)

            def project(gc, kind):
                for j in range(2):
                    act.wait_ge(filled, fill(gc, kind, j) + 1)
                    src = bank[j]
                    if kind == V:
                        dst = v[0][:, 2 * j:2 * j + 2, :].rearrange("p a n -> p (a n)")
                    else:
                        dst = (qT if kind == Q else kT)[0][:, j]
                        if not (isinstance(gc, int) and gc == 0):
                            act.wait_ge(sq_ready if kind == Q else skt_done, gc)
                        if kind == K:
                            act.wait_ge(sig_done, 4 * gc + 1 + j)
                        elif not (isinstance(gc, int) and gc == 0):
                            act.wait_ge(sig_done, 4 * gc - 1 + j)
                        half = seg(src[:, :], 1 if kind == Q else 0)
                        act.activation(r3(e[:, j], P), half, ACT.Exp)
                        act.activation(r3((sq if kind == Q else sk)[:, j], P), half, ACT.Relu)
                    act.activation(dst, src[:, :], ACT.Copy).then_inc(hi_done, 1)

            for kind in (Q, K, V):
                project(0, kind)

            def step(g, c, nxt):
                for h in range(2):
                    act.wait_ge(nb_done, 2 * g + h + 1)
                    for t in range(CT):
                        ins = act.activation(prob[:, h, t, :], prob[:, h, t, :], ACT.Exp,
                                             bias=nb[:, h, t:t + 1], scale=ATT_SCALE,
                                             accum_out=rs[:, h, t:t + 1])
                    ins.then_inc(exp_done, 1)
                act.wait_ge(skt_done, g + 1)
                act.activation(skp[0][:, :, :], r3(ad_ps[0][:, :], P), ACT.Copy).then_inc(skt_hi, 1)
                if nxt:
                    project(g + 1, Q)
                    project(g + 1, K)
                for h in range(2):
                    act.wait_ge(pt_done, 2 * g + h + 1)
                    act.activation(probT[0][:, h], s_ps[h][:, :], ACT.Copy).then_inc(pt_hi, 1)
                for h in range(2):
                    act.wait_ge(mem_done, 2 * g + h + 1)
                    act.activation(mem[0][:, h], mem_ps[h][:, :], ACT.Copy).then_inc(mem_hi, 1)
                for h in range(2):
                    act.wait_ge(ad_done, 2 * g + h + 1)
                    if not (isinstance(g, int) and g == 0):
                        act.wait_ge(att_stored, 16 * g)
                    act.wait_ge(gate_ready, pair_of[0] + 2)
                    act.activation(att[:, h], ad_ps[h][:, :], ACT.Copy,
                                   scale=gate_p[:, h, 1:2]).then_inc(ad_read, 1)
                if nxt:
                    project(g + 1, V)

            pair_of = [0]
            step(0, 0, True)
            with act.Fori(0, PAIRS - 1) as p:
                for c in range(1, CHUNKS + 1):
                    pair_of[0] = p + c // CHUNKS
                    step(CHUNKS * p + c, c % CHUNKS, True)
            pair_of[0] = PAIRS - 1
            for g in range(STEPS - CHUNKS + 1, STEPS):
                step(g, g % CHUNKS, g < STEPS - 1)

        @block.vector
        def _(dve):
            dve.wait_ge(beta_step, 1)
            dve.tensor_scalar(beta_e[:, :], beta_e[:, :], 1.0, None, ALU.add).then_inc(beta_step, 1)
            dve.wait_ge(beta_step, 2)
            dve.reciprocal(gate[:, :, 0], beta_e[:, :]).then_inc(beta_step, 1)
            dve.wait_ge(beta_step, 3)
            dve.tensor_scalar(gate[:, :, 1], gate[:, :, 0], -1.0, 1.0, ALU.mult,
                              ALU.add).then_inc(gate_ready, 1)

            def project(gc, kind):
                for j in range(2):
                    dst = (qT, kT, v)[kind // 2]
                    dst = [x[:, j] if kind != V else x[:, 2 * j:2 * j + 2, :].rearrange("p a n -> p (a n)")
                           for x in dst]
                    dve.wait_ge(hi_done, fill(gc, kind, j) + 1)
                    dve.tensor_tensor(dst[1], bank[j][:, :], dst[0].bitcast(F32),
                                      ALU.subtract).then_inc(freed, 1)
                    if kind != V:
                        s = sq if kind == Q else sk
                        dve.scalar_tensor_tensor(out=s[:, j], in0=e[:, j], scalar=1.0, in1=s[:, j],
                                                 op0=ALU.min, op1=ALU.add).then_inc(sig_done, 1)

            for kind in (Q, K, V):
                project(0, kind)

            def step(g, c, nxt):
                for h in range(2):
                    dve.wait_ge(s_done, 2 * g + h + 1)
                    alone(dve, lone["dve"])
                    for t in range(CT):
                        ins = dve.tensor_tensor_reduce(prob[:, h, t, :], s_ps[h][:, t * P:(t + 1) * P],
                                                       mask[:, :], 1.0, -3e38, ALU.add, ALU.max,
                                                       mx[:, h, t:t + 1])
                    ins.then_inc(max_done, 1)
                    dve.wait_ge(max_done, 2 * g + h + 1)
                    dve.tensor_scalar(nb[:, h, :], mx[:, h, :], -ATT_SCALE, None,
                                      ALU.mult).then_inc(nb_done, 1)
                dve.wait_ge(skt_hi, g + 1)
                dve.tensor_tensor(skp[1][:, :, :], r3(ad_ps[0][:, :], P), skp[0][:, :, :].bitcast(F32),
                                  ALU.subtract).then_inc(sk_ready, 1)
                for h in range(2):
                    dve.wait_ge(exp_done, 2 * g + h + 1)
                    dve.reciprocal(rr[:, h, :], rs[:, h, :]).then_inc(rr_done, 1)
                if nxt:
                    project(g + 1, Q)
                    project(g + 1, K)
                for h in range(2):
                    dve.wait_ge(pt_hi, 2 * g + h + 1)
                    dve.tensor_tensor(probT[1][:, h], s_ps[h][:, :], probT[0][:, h].bitcast(F32),
                                      ALU.subtract).then_inc(pt_ready, 1)
                for h in range(2):
                    dve.wait_ge(mem_hi, 2 * g + h + 1)
                    dve.tensor_tensor(mem[1][:, h], mem_ps[h][:, :], mem[0][:, h].bitcast(F32),
                                      ALU.subtract).then_inc(mem_ready, 1)
                for h in range(2):
                    dve.wait_ge(am_done, 2 * g + h + 1)
                    dve.reciprocal(rec[:, :], mem_ps[h][:, 256:512]).then_inc(rec_done, 1)
                    dve.wait_ge(rec_done, 2 * g + h + 1)
                    dve.tensor_tensor(amr[:, :], mem_ps[h][:, 0:256], rec[:, :],
                                      ALU.mult).then_inc(amr_done, 1)
                    dve.wait_ge(amr_done, 2 * g + h + 1)
                    dve.wait_ge(ad_read, 2 * g + h + 1)
                    half = seg(att[:, h], 1)
                    dve.scalar_tensor_tensor(out=half, in0=r3(amr[:, :], P), scalar=gate_p[:, h, 0:1],
                                             in1=half, op0=ALU.mult, op1=ALU.add).then_inc(att_done, 1)
                if nxt:
                    project(g + 1, V)

            dve.wait_ge(consts_loaded, 48)
            over_steps(dve, step)

        @block.tensor
        def _(pe):
            pe.wait_ge(ones_ready, 3)

            def project(gc, kind, p):
                c = project_chunk[0]
                n = "qkv"[kind // 2]
                for j in range(2):
                    f = fill(gc, kind, j)
                    if not (isinstance(f, int) and f < 2):
                        pe.wait_ge(freed, f - 1)
                    if j == 0:
                        pe.wait_ge(w_split[n], p + 1)
                    if kind == V:
                        for i in range(2):
                            t = 2 * j + i
                            tok = slice(c * CHUNK + t * P, c * CHUNK + (t + 1) * P)
                            for k in range(KD):
                                mm = mm3(pe, bank[j][:, i * 256:(i + 1) * 256],
                                         both(xT, slice(None), k, tok), both(w[n], slice(None), k),
                                         k == 0, k == KD - 1)
                    else:
                        for k in range(KD):
                            mm = mm3(pe, bank[j][:, :],
                                     both(w[n], slice(None), k, slice(j * P, (j + 1) * P)),
                                     both(xT, slice(None), k, slice(c * CHUNK, (c + 1) * CHUNK)),
                                     k == 0, k == KD - 1)
                    mm.then_inc(filled, 1)

            project_chunk = [0]
            for kind in (Q, K, V):
                project(0, kind, 0)

            def step(g, c, nxt, p_next):
                start = isinstance(g, int) and g == 0
                pe.wait_ge(freed, fill(g, V, 0))
                if not start:
                    pe.wait_ge(pt_ready, 2 * g)
                for h in range(2):
                    for t in range(CT):
                        tok = slice(t * P, (t + 1) * P)
                        mm = mm3(pe, s_ps[h][:, tok], both(qT, slice(None), h, tok),
                                 both(kT, slice(None), h, tok))
                    mm.then_inc(s_done, 1)
                pe.wait_ge(sig_done, 4 * g + 4)
                if not start:
                    pe.wait_ge(ad_read, 2 * g - 1)
                for h in range(2):
                    for b in range(2):
                        i = 2 * h + b
                        mm = pe.transpose(ad_ps[0][:, i * P:(i + 1) * P], sk[:, h, b * P:(b + 1) * P], ident[:, :])
                mm.then_inc(skt_done, 1)
                project_chunk[0] = (c + 1) % CHUNKS
                if nxt:
                    project(g + 1, Q, p_next)
                    project(g + 1, K, p_next)
                for h in range(2):
                    pe.wait_ge(p_ready, 2 * g + h + 1)
                    for t in range(CT):
                        mm = pe.transpose(s_ps[h][:, t * P:(t + 1) * P], prob[:, h, t, :], ident[:, :])
                    mm.then_inc(pt_done, 1)
                pe.wait_ge(sk_ready, g + 1)
                for h in range(2):
                    if not start:
                        pe.wait_ge(att_done, 2 * g - 1 + h)
                    for b in range(2):
                        s = both(skp, slice(None), 2 * h + b)
                        out = mem_ps[h][:, b * 256:b * 256 + P]
                        mm3(pe, out, s, both(v, slice(None), 2 * b, slice(h * P, (h + 1) * P)))
                        out = mem_ps[h][:, b * 256 + P:(b + 1) * 256]
                        pe.matmul(out, s[0], ones_r[:, :], start=True, stop=False)
                        pe.matmul(out, s[1], ones_r[:, :], start=False, stop=False)
                        mm = pe.matmul(out, ones_r[:, :], z_start[:, :], start=False, stop=True)
                    mm.then_inc(mem_done, 1)
                for h in range(2):
                    pe.wait_ge(pt_ready, 2 * g + h + 1)
                    if not start:
                        pe.wait_ge(ad_read, 2 * g - 1 + h)
                    for t in range(CT):
                        tok = slice(t * P, (t + 1) * P)
                        mm = mm3(pe, ad_ps[h][:, tok], both(v, slice(None), t, slice(h * P, (h + 1) * P)),
                                 both(probT, slice(None), h, tok))
                    mm.then_inc(ad_done, 1)
                pe.wait_ge(sq_ready, g + 1)
                for h in range(2):
                    pe.wait_ge(mem_ready, 2 * g + h + 1)
                    for b in range(2):
                        q_b = both(sqp[c % 2], slice(None), h, slice(b * P, (b + 1) * P))
                        mm3(pe, mem_ps[h][:, b * P:(b + 1) * P],
                            both(mem, slice(None), h, slice(b * 256, b * 256 + P)), q_b)
                        mm = mm3(pe, mem_ps[h][:, 256 + b * P:256 + (b + 1) * P],
                                 both(mem, slice(None), h, slice(b * 256 + P, (b + 1) * 256)), q_b)
                    mm.then_inc(am_done, 1)
                if nxt:
                    project(g + 1, V, p_next)

            step(0, 0, True, 0)
            with pe.Fori(0, PAIRS - 1) as p:
                for c in range(1, CHUNKS + 1):
                    step(CHUNKS * p + c, c % CHUNKS, True, p + (c + 1) // CHUNKS)
            for g in range(STEPS - CHUNKS + 1, STEPS):
                step(g, g % CHUNKS, g < STEPS - 1, PAIRS - 1)


def attention_output(nc, X, d, attT, x1):
    J = HEADS
    ROWS = P // J
    with ExitStack() as ctx:
        def sb(name, shape, dt=F32):
            return ctx.enter_context(nc.sbuf_tensor("o_" + name, shape, dt))

        def sem(name):
            return ctx.enter_context(nc.semaphore("o_" + name))

        wo = [sb("wo_" + n, [P, J, D], F32R) for n in ("hi", "lo")]
        raw = [sb(f"raw{i}", [P, TOKENS]) for i in range(2)]
        head = [[sb(f"head{i}_{n}", [P, J, P], F32R) for n in ("hi", "lo")] for i in range(2)]
        xrow = [sb(f"xrow{i}", [P, D]) for i in range(2)]
        row = [sb(f"row{i}", [P, D]) for i in range(2)]
        ps = [ctx.enter_context(nc.psum_tensor(f"o_ps{i}", [P, D], F32)) for i in range(2)]
        head_loaded = [sem(f"head_loaded{i}") for i in range(2)]
        x_loaded = [sem(f"x_loaded{i}") for i in range(2)]
        head_hi = sem("head_hi")
        head_split = sem("head_split")
        wo_hi = sem("wo_hi")
        wo_split = sem("wo_split")
        product = sem("product")
        row_ready = sem("row_ready")
        row_stored = [sem(f"row_stored{i}") for i in range(2)]
        x1_loaded = sem("x1_loaded")
        block = ctx.enter_context(nc.Block())
        heads = attT.rearrange("(p c) d h t -> p h d c t", c=CHUNKS)
        x_rows = d["x"].rearrange("(t h s) n -> h t s n", h=HEADS, s=ROWS)
        x1_rows = x1.rearrange("(t h s) n -> h t s n", h=HEADS, s=ROWS)

        @block.sync
        def _(sp):
            def load(p, i):
                sp.dma_start(r3(raw[i][:, :], CHUNK), heads[p, i]).then_inc(head_loaded[i], 16)

            def load_x(p, i):
                sp.dma_start(xrow[i][:, :], x_rows[2 * p + i]).then_inc(x_loaded[i], 16)

            def store(p, i):
                sp.wait_ge(row_ready, 2 * p + i + 1)
                sp.dma_start(x1_rows[2 * p + i], row[i][:, :]).then_inc(row_stored[i], 16)

            for i in range(2):
                load(0, i)
                load_x(0, i)
            with sp.Fori(0, HEADS // 2 - 1) as p:
                for i in range(2):
                    sp.wait_ge(head_split, 2 * p + i + 1)
                    load(p + 1, i)
                    store(p, i)
                    load_x(p + 1, i)
            for i in range(2):
                store(HEADS // 2 - 1, i)
            for i in range(2):
                sp.wait_ge(row_stored[i], 16 * HEADS // 2)
            sp.dma_start(X[:, :, :], x1.rearrange("(t p) n -> p t n", p=P)).then_inc(x1_loaded, 16)
            sp.wait_ge(x1_loaded, 16)

        @block.scalar
        def _(act):
            def head_part(h, i, p):
                act.wait_ge(head_loaded[i], 16 * (p + 1))
                if not (isinstance(p, int) and p == 0):
                    act.wait_ge(product, h - 1)
                act.activation(head[i][0][:, :, :], raw[i][:, :].rearrange("d (m j) -> d j m", j=J),
                               ACT.Copy).then_inc(head_hi, 1)

            head_part(0, 0, 0)
            for j in range(J):
                act.activation(wo[0][:, j, :], X[:, j, :], ACT.Copy).then_inc(wo_hi, 1)
            head_part(1, 1, 0)
            with act.Fori(1, HEADS // 2) as p:
                for i in range(2):
                    head_part(2 * p + i, i, p)

        @block.vector
        def _(dve):
            def head_part(h, i):
                dve.wait_ge(head_hi, h + 1)
                dve.tensor_tensor(head[i][1][:, :, :], raw[i][:, :].rearrange("d (m j) -> d j m", j=J),
                                  head[i][0][:, :, :].bitcast(F32), ALU.subtract).then_inc(head_split, 1)

            def finish(h, i, p):
                dve.wait_ge(product, h + 1)
                dve.wait_ge(x_loaded[i], 16 * (p + 1))
                if not (isinstance(p, int) and p == 0):
                    dve.wait_ge(row_stored[i], 16 * p)
                dve.tensor_tensor(row[i][:, :], ps[i][:, :], xrow[i][:, :], ALU.add).then_inc(row_ready, 1)

            head_part(0, 0)
            for j in range(J):
                dve.wait_ge(wo_hi, j + 1)
                dve.tensor_tensor(wo[1][:, j, :], X[:, j, :], wo[0][:, j, :].bitcast(F32),
                                  ALU.subtract).then_inc(wo_split, 1)
            head_part(1, 1)
            with dve.Fori(0, HEADS // 2 - 1) as p:
                for i in range(2):
                    finish(2 * p + i, i, p)
                    head_part(2 * p + i + 2, i)
            for i in range(2):
                finish(HEADS - 2 + i, i, HEADS // 2 - 1)

        @block.tensor
        def _(pe):
            def multiply(h, i):
                pe.wait_ge(head_split, h + 1)
                if not (isinstance(h, int) and h < 2):
                    pe.wait_ge(row_ready, h - 1)
                for j in range(J):
                    if isinstance(h, int) and h == 0:
                        pe.wait_ge(wo_split, j + 1)
                    mm = mm3(pe, ps[i][:, :], (head[i][0][:, j, :], head[i][1][:, j, :]),
                             (wo[0][:, j, :], wo[1][:, j, :]), j == 0, j == J - 1)
                mm.then_inc(product, 1)

            multiply(0, 0)
            multiply(1, 1)
            with pe.Fori(1, HEADS // 2) as p:
                for i in range(2):
                    multiply(2 * p + i, i)


QC = 2
KEYS = 256
SEQS = TOKENS // KEYS
LOOKBACK = 8
X_SCALE = float(np.float32(1.0) / np.sqrt(np.float32(192.0)))


def latents(nc, d, T):
    with ExitStack() as ctx:
        def sb(name, shape, dt=F32):
            return ctx.enter_context(nc.sbuf_tensor("k_" + name, shape, dt))

        def sem(name):
            return ctx.enter_context(nc.semaphore("k_" + name))

        w_raw = sb("w_raw", [P, KD + 1, P])
        w = [sb("w_" + n, [P, KD + 1, P], F32R) for n in ("hi", "lo")]
        raw = [sb(f"raw{i}", [P, KD, CHUNK]) for i in range(2)]
        cT = [[sb(f"c{i}_{n}", [P, KD, CHUNK], F32R) for n in ("hi", "lo")] for i in range(2)]
        kvf = sb("kvf", [P, CHUNK])
        rot = sb("rot", [P, CHUNK])
        rot_swap = sb("rot_swap", [P, CHUNK])
        kr = sb("kr", [P, CHUNK])
        kio = sb("kio", [P, KEYS])
        ids_i = sb("ids_i", [P, TILES], I32)
        ids = sb("ids", [P, TILES])
        ids_low = sb("ids_low", [P, TILES])
        above = sb("above", [P, KEYS])
        below = sb("below", [P, KEYS])
        rows_of = sb("rows_of", [P, 2])
        kv_ps, tok_ps, kr_ps = ([ctx.enter_context(nc.psum_tensor(f"k_{n}{i}", [P, 512], F32)) for i in range(2)]
                                for n in ("kv", "tok", "kr"))
        w_loaded = sem("w_loaded")
        small_loaded = sem("small_loaded")
        raw_loaded = [sem(f"raw_loaded{i}") for i in range(2)]
        w_hi = sem("w_hi")
        w_split = sem("w_split")
        c_hi = sem("c_hi")
        c_split = sem("c_split")
        kv_done = sem("kv_done")
        kv_hi = sem("kv_hi")
        kv_split = sem("kv_split")
        tok_done = sem("tok_done")
        tok_hi = sem("tok_hi")
        tok_split = sem("tok_split")
        kr_done = sem("kr_done")
        rot_done = sem("rot_done")
        kr_ready = sem("kr_ready")
        kr_hi = sem("kr_hi")
        kr_split = sem("kr_split")
        ids_step = sem("ids_step")
        mask_part = sem("mask_part")
        mask_done = sem("mask_done")
        block = ctx.enter_context(nc.Block())

        def cols(c):
            return slice(c * CHUNK, (c + 1) * CHUNK)

        @block.sync
        def _(sp):
            sp.dma_start(w_raw[:, :, :], d["wkv"]).then_inc(w_loaded, 16)
            for c in range(CHUNKS):
                if c >= 2:
                    sp.wait_ge(c_split, c - 1)
                sp.dma_start(raw[c % 2][:, :, :], d["ctxT"][c]).then_inc(raw_loaded[c % 2], 16)
                if c == 1:
                    sp.dma_start(T["cos"][:, :], d["cos"]).then_inc(small_loaded, 16)
                    sp.dma_start(T["sin"][:, :], d["sin"]).then_inc(small_loaded, 16)
                    sp.dma_start(kio[:, :], d["kio"]).then_inc(small_loaded, 16)
                    sp.dma_start(ids_i[:, :], d["ids"]).then_inc(small_loaded, 16)
                    sp.dma_start(rows_of[:, :], d["rows_of"]).then_inc(small_loaded, 16)

        @block.scalar
        def _(act):
            act.wait_ge(w_loaded, 16)
            act.activation(w[0][:, :, :], w_raw[:, :, :], ACT.Copy).then_inc(w_hi, 1)

            def context(c):
                act.wait_ge(raw_loaded[c % 2], 16 * (c // 2 + 1))
                if c >= 2:
                    act.wait_ge(kv_done, c - 1)
                act.activation(cT[c % 2][0][:, :, :], raw[c % 2][:, :, :], ACT.Copy).then_inc(c_hi, 1)

            context(0)
            act.wait_ge(small_loaded, 80)
            for c in range(CHUNKS):
                if c + 1 < CHUNKS:
                    context(c + 1)
                act.wait_ge(kv_done, c + 1)
                if c >= 1:
                    act.wait_ge(tok_done, c)
                act.activation(kvf[:, :], kv_ps[c % 2][:, :], ACT.Copy)
                act.activation(T["kvT"][0][:, cols(c)], kv_ps[c % 2][:, :], ACT.Copy).then_inc(kv_hi, 1)
                act.wait_ge(tok_done, c + 1)
                act.activation(T["kv"][0][:, c * CT:(c + 1) * CT, :], r3(tok_ps[c % 2][:, :], P),
                               ACT.Copy).then_inc(tok_hi, 1)
                act.wait_ge(kr_ready, c + 1)
                for h in range(2):
                    act.activation(T["kr"][0][:, 2 * c:2 * c + 2, h, :], r3(kr[:, :], KEYS), ACT.Copy,
                                   scale=rows_of[:, h:h + 1]).then_inc(kr_hi, 1)

        @block.vector
        def _(dve):
            dve.wait_ge(w_hi, 1)
            dve.tensor_tensor(w[1][:, :, :], w_raw[:, :, :], w[0][:, :, :].bitcast(F32),
                              ALU.subtract).then_inc(w_split, 1)

            def context(c):
                dve.wait_ge(c_hi, c + 1)
                dve.tensor_tensor(cT[c % 2][1][:, :, :], raw[c % 2][:, :, :],
                                  cT[c % 2][0][:, :, :].bitcast(F32), ALU.subtract).then_inc(c_split, 1)

            context(0)
            dve.wait_ge(small_loaded, 80)
            dve.tensor_copy(ids[:, :], ids_i[:, :]).then_inc(ids_step, 1)
            dve.wait_ge(ids_step, 1)
            dve.tensor_scalar(ids_low[:, :], ids[:, :], -float(LOOKBACK), None, ALU.add).then_inc(ids_step, 1)
            dve.wait_ge(ids_step, 2)

            def mask(t):
                if t:
                    dve.wait_ge(mask_done, t)
                dve.tensor_scalar(above[:, :], kio[:, :], ids[:, t:t + 1], NEG, ALU.is_gt, ALU.mult)
                dve.tensor_scalar(below[:, :], kio[:, :], ids_low[:, t:t + 1], NEG, ALU.is_lt,
                                  ALU.mult).then_inc(mask_part, 1)
                dve.wait_ge(mask_part, t + 1)
                dve.tensor_tensor(T["mask"][:, t, :], above[:, :], below[:, :], ALU.add).then_inc(mask_done, 1)

            for c in range(CHUNKS):
                if c + 1 < CHUNKS:
                    context(c + 1)
                dve.wait_ge(kv_hi, c + 1)
                dve.tensor_tensor(T["kvT"][1][:, cols(c)], kv_ps[c % 2][:, :],
                                  T["kvT"][0][:, cols(c)].bitcast(F32), ALU.subtract).then_inc(kv_split, 1)
                for t in range(c * CT, (c + 1) * CT):
                    mask(t)
                dve.wait_ge(tok_hi, c + 1)
                dve.tensor_tensor(T["kv"][1][:, c * CT:(c + 1) * CT, :], r3(tok_ps[c % 2][:, :], P),
                                  T["kv"][0][:, c * CT:(c + 1) * CT, :].bitcast(F32),
                                  ALU.subtract).then_inc(tok_split, 1)
                dve.wait_ge(kr_done, c + 1)
                rotate(dve, T, kr_ps[c % 2], rot, rot_swap).then_inc(rot_done, 1)
                dve.wait_ge(rot_done, c + 1)
                dve.tensor_tensor(kr[:, :], rot[:, :], rot_swap[:, :], ALU.add).then_inc(kr_ready, 1)
                for h in range(2):
                    dve.wait_ge(kr_hi, 2 * c + h + 1)
                    dve.scalar_tensor_tensor(
                        out=T["kr"][1][:, 2 * c:2 * c + 2, h, :], in0=r3(kr[:, :], KEYS),
                        scalar=rows_of[:, h:h + 1], in1=T["kr"][0][:, 2 * c:2 * c + 2, h, :].bitcast(F32),
                        op0=ALU.mult, op1=ALU.subtract).then_inc(kr_split, 1)

        @block.tensor
        def _(pe):
            pe.wait_ge(w_split, 1)
            for c in range(CHUNKS):
                pe.wait_ge(c_split, c + 1)
                if c >= 2:
                    pe.wait_ge(kv_split, c - 1)
                for k in range(KD):
                    mm = mm3(pe, kv_ps[c % 2][:, :], (w[0][:, k, :], w[1][:, k, :]),
                             (cT[c % 2][0][:, k, :], cT[c % 2][1][:, k, :]), k == 0, k == KD - 1)
                mm.then_inc(kv_done, 1)
                pe.wait_ge(kv_hi, c + 1)
                if c >= 2:
                    pe.wait_ge(tok_split, c - 1)
                for t in range(CT):
                    mm = pe.transpose(tok_ps[c % 2][:, t * P:(t + 1) * P], kvf[:, t * P:(t + 1) * P],
                                      T["ident"][:, :])
                mm.then_inc(tok_done, 1)
                pe.wait_ge(kv_split, c + 1)
                if c >= 2:
                    pe.wait_ge(rot_done, c - 1)
                mm3(pe, kr_ps[c % 2][:, :], (w[0][:, KD, :], w[1][:, KD, :]),
                    (T["kvT"][0][:, cols(c)], T["kvT"][1][:, cols(c)])).then_inc(kr_done, 1)


def rotate(dve, T, ps, rot, rot_swap):
    def table(name, rows):
        return T[name][rows, :].unsqueeze(1).to_broadcast([rows.stop - rows.start, 2, KEYS])

    H = P // 2
    dve.tensor_tensor(r3(rot[:, :], KEYS), r3(ps[:, :], KEYS), table("cos", slice(0, P)), ALU.mult)
    dve.tensor_tensor(r3(rot_swap[0:H, :], KEYS), r3(ps[H:P, :], KEYS), table("sin", slice(0, H)), ALU.mult)
    return dve.tensor_tensor(r3(rot_swap[H:P, :], KEYS), r3(ps[0:H, :], KEYS), table("sin", slice(H, P)),
                             ALU.mult)


def query_latent(nc, d, T, xT):
    with ExitStack() as ctx:
        def sb(name, shape, dt=F32):
            return ctx.enter_context(nc.sbuf_tensor("q_" + name, shape, dt))

        def sem(name):
            return ctx.enter_context(nc.semaphore("q_" + name))

        w_raw = sb("w_raw", [P, KD, QC * P])
        w = [sb("w_" + n, [P, KD, QC * P], F32R) for n in ("hi", "lo")]
        ps = [ctx.enter_context(nc.psum_tensor(f"q_ps{i}", [P, 512], F32)) for i in range(4)]
        w_loaded = sem("w_loaded")
        w_hi = sem("w_hi")
        w_split = sem("w_split")
        done = sem("done")
        hi = sem("hi")
        split = sem("split")
        block = ctx.enter_context(nc.Block())
        units = [(c, j) for c in range(CHUNKS) for j in range(QC)]

        @block.sync
        def _(sp):
            sp.dma_start(w_raw[:, :, :], d["wdq"]).then_inc(w_loaded, 16)

        @block.scalar
        def _(act):
            act.wait_ge(w_loaded, 16)
            act.activation(w[0][:, :, :], w_raw[:, :, :], ACT.Copy).then_inc(w_hi, 1)
            for n, (c, j) in enumerate(units):
                act.wait_ge(done, n + 1)
                act.activation(T["qc"][0][:, j, c * CHUNK:(c + 1) * CHUNK], ps[n % 4][:, :],
                               ACT.Copy).then_inc(hi, 1)

        @block.vector
        def _(dve):
            dve.wait_ge(w_hi, 1)
            dve.tensor_tensor(w[1][:, :, :], w_raw[:, :, :], w[0][:, :, :].bitcast(F32),
                              ALU.subtract).then_inc(w_split, 1)
            for n, (c, j) in enumerate(units):
                dve.wait_ge(hi, n + 1)
                tok = slice(c * CHUNK, (c + 1) * CHUNK)
                dve.tensor_tensor(T["qc"][1][:, j, tok], ps[n % 4][:, :], T["qc"][0][:, j, tok].bitcast(F32),
                                  ALU.subtract).then_inc(split, 1)

        @block.tensor
        def _(pe):
            pe.wait_ge(w_split, 1)
            for n, (c, j) in enumerate(units):
                if n >= 4:
                    pe.wait_ge(split, n - 3)
                tok = slice(c * CHUNK, (c + 1) * CHUNK)
                for k in range(KD):
                    mm = mm3(pe, ps[n % 4][:, :], (w[0][:, k, j * P:(j + 1) * P], w[1][:, k, j * P:(j + 1) * P]),
                             (xT[0][:, k, tok], xT[1][:, k, tok]), k == 0, k == KD - 1)
                mm.then_inc(done, 1)


def cross_attention(nc, X, d, T):
    with ExitStack() as ctx:
        def sb(name, shape, dt=F32):
            return ctx.enter_context(nc.sbuf_tensor("x_" + name, shape, dt))

        def parts(name, shape):
            return sb(name + "_hi", shape, F32R), sb(name + "_lo", shape, F32R)

        def sem(name):
            return ctx.enter_context(nc.semaphore("x_" + name))

        def psum(name):
            return ctx.enter_context(nc.psum_tensor("x_" + name, [P, 512], F32))

        def both(pair, *index):
            return pair[0][index], pair[1][index]

        ALL = slice(None)
        UQ, UK, UV, WO = 0, 256, 384, 512
        raw = sb("raw", [P, 2, WO + D])
        raw_r = sb("raw_r", [P, QC, P])
        wa = parts("wa", [P, 2, QC, P])
        wb = parts("wb", [P, 2, D])
        wr = parts("wr", [P, QC, P])
        qa = parts("qa", [P, 2, CHUNK])
        qr = parts("qr", [P, CHUNK])
        rot = sb("rot", [P, CHUNK])
        rot_swap = sb("rot_swap", [P, CHUNK])
        prob = sb("prob", [P, CT, 2, KEYS])
        probT = parts("probT", [P, 4, 512])
        ao = parts("ao", [P, 2, 512])
        mx = sb("mx", [P, CT, 2])
        nb = sb("nb", [P, CT, 2])
        rs = sb("rs", [P, CT, 2])
        rr = sb("rr", [P, CT, 2])
        bank = [psum("bank0"), psum("bank1")]
        s_ps = [psum("s0"), psum("s1")]
        pt_ps = [psum("pt0"), psum("pt1")]
        av_ps = [psum("av0"), psum("av1")]

        raw_loaded = sem("raw_loaded")
        raw_r_loaded = sem("raw_r_loaded")
        wr_hi, wr_split = sem("wr_hi"), sem("wr_split")
        a_done, a_hi, a_split = sem("a_done"), sem("a_hi"), sem("a_split")
        b_done, b_hi, b_split = sem("b_done"), sem("b_hi"), sem("b_split")
        qa_done, qa_hi, qa_split = sem("qa_done"), sem("qa_hi"), sem("qa_split")
        qr_done, rot_done, rot_sum = sem("qr_done"), sem("rot_done"), sem("rot_sum")
        qr_hi, qr_ready = sem("qr_hi"), sem("qr_ready")
        s_done, max_done, nb_done = sem("s_done"), sem("max_done"), sem("nb_done")
        exp_done, rr_done, p_ready = sem("exp_done"), sem("rr_done"), sem("p_ready")
        pt_done, pt_hi, pt_ready = sem("pt_done"), sem("pt_hi"), sem("pt_ready")
        av_done, av_hi, av_ready = sem("av_done"), sem("av_hi"), sem("av_ready")
        out_done, out_added = sem("out_done"), sem("out_added")
        lone = {n: sem("lone_" + n) for n in ("act", "dve", "pool")}
        block = ctx.enter_context(nc.Block())

        def over_steps(eng, step):
            step(0, 0, 0, True)
            with eng.Fori(0, PAIRS - 1) as p:
                for c in range(1, CHUNKS + 1):
                    step(CHUNKS * p + c, p + c // CHUNKS, c % CHUNKS, True)
            for g in range(STEPS - CHUNKS + 1, STEPS):
                step(g, PAIRS - 1, g % CHUNKS, g < STEPS - 1)

        def is_at(g, value):
            return isinstance(g, int) and g == value

        def folds_a(p, c):
            return c == 2 and not is_at(p, PAIRS - 1)

        @block.sync
        def _(sp):
            sp.dma_start(raw[:, :, :], d["xw"][0]).then_inc(raw_loaded, 16)
            sp.dma_start(raw_r[:, :, :], d["xwr"][0]).then_inc(raw_r_loaded, 16)
            with sp.Fori(0, PAIRS - 1) as p:
                sp.wait_ge(wr_split, p + 1)
                sp.dma_start(raw_r[:, :, :], d["xwr"][p + 1]).then_inc(raw_r_loaded, 16)
                sp.wait_ge(b_done, 2 * p + 2)
                sp.dma_start(raw[:, :, :], d["xw"][p + 1]).then_inc(raw_loaded, 16)

        @block.gpsimd
        def _(pool):
            def split_wr(p):
                pool.wait_ge(raw_r_loaded, 16 * (p + 1))
                alone(pool, lone["pool"])
                pool.tensor_copy(wr[0][:, :, :], raw_r[:, :, :]).then_inc(wr_hi, 1)
                pool.wait_ge(wr_hi, p + 1)
                pool.tensor_tensor(wr[1][:, :, :], raw_r[:, :, :], wr[0][:, :, :].bitcast(F32),
                                   ALU.subtract).then_inc(wr_split, 1)

            def rotary(gc):
                pool.wait_ge(rot_done, gc + 1)
                pool.tensor_tensor(rot[:, :], rot[:, :], rot_swap[:, :], ALU.add).then_inc(rot_sum, 1)
                pool.wait_ge(qr_hi, gc + 1)
                pool.tensor_tensor(qr[1][:, :], rot[:, :], qr[0][:, :].bitcast(F32),
                                   ALU.subtract).then_inc(qr_ready, 1)

            def step(g, p, c, nxt):
                for t in range(CT):
                    pool.wait_ge(rr_done, 4 * g + t + 1)
                    pool.tensor_tensor(prob[:, t], prob[:, t],
                                       rr[:, t, :].unsqueeze(2).to_broadcast([P, 2, KEYS]),
                                       ALU.mult).then_inc(p_ready, 1)
                if nxt:
                    rotary(g + 1)
                if folds_a(p, c):
                    split_wr(p + 1)

            split_wr(0)
            rotary(0)
            over_steps(pool, step)

        @block.scalar
        def _(act):
            def fold_a(p):
                act.wait_ge(a_done, p + 1)
                act.activation(wa[0][:, :, :, :].rearrange("p h k n -> p (h k n)"), av_ps[1][:, :],
                               ACT.Copy).then_inc(a_hi, 1)

            def queries(gc):
                for h in range(2):
                    act.wait_ge(qa_done, 2 * gc + h + 1)
                    act.activation(qa[0][:, h], bank[h][:, :], ACT.Copy).then_inc(qa_hi, 1)

            def rotary(gc):
                act.wait_ge(rot_sum, gc + 1)
                act.activation(qr[0][:, :], rot[:, :], ACT.Copy).then_inc(qr_hi, 1)

            def step(g, p, c, nxt):
                for t in range(CT):
                    act.wait_ge(nb_done, 4 * g + t + 1)
                    for h in range(2):
                        ins = act.activation(prob[:, t, h, :], prob[:, t, h, :], ACT.Exp,
                                             bias=nb[:, t, h:h + 1], scale=X_SCALE,
                                             accum_out=rs[:, t, h:h + 1])
                    ins.then_inc(exp_done, 1)
                if nxt:
                    queries(g + 1)
                if folds_a(p, c):
                    fold_a(p + 1)
                for i in range(4):
                    act.wait_ge(pt_done, 4 * g + i + 1)
                    act.activation(probT[0][:, i], pt_ps[i % 2][:, :], ACT.Copy).then_inc(pt_hi, 1)
                if nxt:
                    rotary(g + 1)
                for b in range(2):
                    act.wait_ge(av_done, 2 * g + b + 1)
                    act.activation(ao[0][:, b], av_ps[b][:, :], ACT.Copy).then_inc(av_hi, 1)
                if c == 0:
                    for h in range(2):
                        act.wait_ge(b_done, 2 * p + h + 1)
                        act.activation(wb[0][:, h], bank[h][:, :], ACT.Copy).then_inc(b_hi, 1)

            fold_a(0)
            queries(0)
            rotary(0)
            over_steps(act, step)

        @block.vector
        def _(dve):
            def fold_a(p):
                dve.wait_ge(a_hi, p + 1)
                dve.tensor_tensor(wa[1][:, :, :, :].rearrange("p h k n -> p (h k n)"), av_ps[1][:, :],
                                  wa[0][:, :, :, :].rearrange("p h k n -> p (h k n)").bitcast(F32),
                                  ALU.subtract).then_inc(a_split, 1)

            def queries(gc):
                for h in range(2):
                    dve.wait_ge(qa_hi, 2 * gc + h + 1)
                    dve.tensor_tensor(qa[1][:, h], bank[h][:, :], qa[0][:, h].bitcast(F32),
                                      ALU.subtract).then_inc(qa_split, 1)

            def rotary(gc):
                dve.wait_ge(qr_done, gc + 1)
                if not is_at(gc, 0):
                    dve.wait_ge(qr_ready, gc)
                rotate(dve, T, av_ps[0], rot, rot_swap).then_inc(rot_done, 1)

            def reciprocal(g, t):
                dve.wait_ge(exp_done, 4 * g + t + 1)
                dve.reciprocal(rr[:, t, :], rs[:, t, :]).then_inc(rr_done, 1)

            def output(m, c, tiles):
                for j in tiles:
                    dve.wait_ge(out_done, 4 * m + j + 1)
                    dve.tensor_tensor(X[:, c * CT + j, :], bank[j % 2][:, :], X[:, c * CT + j, :],
                                      ALU.add).then_inc(out_added, 1)

            def step(g, p, c, nxt):
                before = (c - 1) % CHUNKS
                for t in range(CT):
                    dve.wait_ge(s_done, 4 * g + t + 1)
                    alone(dve, lone["dve"])
                    for h in range(2):
                        ins = dve.tensor_tensor_reduce(prob[:, t, h, :], s_ps[t % 2][:, h * KEYS:(h + 1) * KEYS],
                                                       T["mask"][:, c * CT + t, :], 1.0, -3e38, ALU.add,
                                                       ALU.max, mx[:, t, h:h + 1])
                    ins.then_inc(max_done, 1)
                    dve.wait_ge(max_done, 4 * g + t + 1)
                    dve.tensor_scalar(nb[:, t, :], mx[:, t, :], -X_SCALE, None, ALU.mult).then_inc(nb_done, 1)
                    if t:
                        reciprocal(g, t - 1)
                reciprocal(g, CT - 1)
                if nxt:
                    queries(g + 1)
                if folds_a(p, c):
                    fold_a(p + 1)
                for i in range(4):
                    dve.wait_ge(pt_hi, 4 * g + i + 1)
                    dve.tensor_tensor(probT[1][:, i], pt_ps[i % 2][:, :], probT[0][:, i].bitcast(F32),
                                      ALU.subtract).then_inc(pt_ready, 1)
                if not is_at(g, 0):
                    output(g - 1, before, (0, 1))
                if nxt:
                    rotary(g + 1)
                if not is_at(g, 0):
                    output(g - 1, before, (2, 3))
                for b in range(2):
                    dve.wait_ge(av_hi, 2 * g + b + 1)
                    dve.tensor_tensor(ao[1][:, b], av_ps[b][:, :], ao[0][:, b].bitcast(F32),
                                      ALU.subtract).then_inc(av_ready, 1)
                if c == 0:
                    for h in range(2):
                        dve.wait_ge(b_hi, 2 * p + h + 1)
                        dve.tensor_tensor(wb[1][:, h], bank[h][:, :], wb[0][:, h].bitcast(F32),
                                          ALU.subtract).then_inc(b_split, 1)

            fold_a(0)
            queries(0)
            rotary(0)
            over_steps(dve, step)
            output(STEPS - 1, CHUNKS - 1, range(CT))

        @block.tensor
        def _(pe):
            def fold_a(p):
                pe.wait_ge(raw_loaded, 16 * (p + 1))
                for h in range(2):
                    for k in range(QC):
                        at = (2 * h + k) * P
                        mm = pe.matmul(av_ps[1][:, at:at + P], raw[:, h, UQ + k * P:UQ + (k + 1) * P],
                                       raw[:, h, UK:UK + P], start=True, stop=True)
                mm.then_inc(a_done, 1)

            def fold_b(g, p):
                for h in range(2):
                    if is_at(g, 0):
                        pe.wait_ge(qa_split, 2 + h + 1)
                    else:
                        pe.wait_ge(out_added, 4 * g + h - 1)
                    pe.matmul(bank[h][:, :], raw[:, h, UV:UV + P], raw[:, h, WO:WO + D],
                              start=True, stop=True).then_inc(b_done, 1)

            def queries(c, h):
                tok = slice(c * CHUNK, (c + 1) * CHUNK)
                for k in range(QC):
                    mm = mm3(pe, bank[h][:, :], both(wa, ALL, h, k), both(T["qc"], ALL, k, tok),
                             k == 0, k == QC - 1)
                mm.then_inc(qa_done, 1)

            def rotary(c):
                tok = slice(c * CHUNK, (c + 1) * CHUNK)
                for k in range(QC):
                    mm = mm3(pe, av_ps[0][:, :], both(wr, ALL, k), both(T["qc"], ALL, k, tok),
                             k == 0, k == QC - 1)
                mm.then_inc(qr_done, 1)

            def output(m, p, free):
                pe.wait_ge(av_ready, 2 * m + 2)
                pe.wait_ge(b_split, 2 * p + 2)
                for j in range(CT):
                    if j < 2:
                        free(j)
                    else:
                        pe.wait_ge(out_added, 4 * m + j - 1)
                    for h in range(2):
                        at = h * 256 + j % 2 * P
                        mm = mm3(pe, bank[j % 2][:, :], both(ao, ALL, j // 2, slice(at, at + P)),
                                 both(wb, ALL, h), h == 0, h == 1)
                    mm.then_inc(out_done, 1)

            def step(g, p, c, nxt):
                start = is_at(g, 0)
                pe.wait_ge(qa_split, 2 * g + 2)
                pe.wait_ge(qr_ready, g + 1)
                for t in range(CT):
                    if not (start and t < 2):
                        pe.wait_ge(max_done, 4 * g + t - 1)
                    seq = 2 * c + t // 2
                    tok = slice(t * P, (t + 1) * P)
                    mm3(pe, s_ps[t % 2][:, :], both(qr, ALL, tok),
                        [x[:, seq].rearrange("p h k -> p (h k)") for x in T["kr"]], True, False)
                    for h in range(2):
                        mm = mm3(pe, s_ps[t % 2][:, h * KEYS:(h + 1) * KEYS], both(qa, ALL, h, tok),
                                 both(T["kvT"], ALL, slice(seq * KEYS, (seq + 1) * KEYS)), False, h == 1)
                    mm.then_inc(s_done, 1)
                if nxt:
                    next_c = (c + 1) % CHUNKS
                    pe.wait_ge(a_split, (p + 2 if c == 3 else p + 1))
                    for h in range(2):
                        if start:
                            pe.wait_ge(qa_split, h + 1)
                        elif c == 1:
                            pe.wait_ge(b_split, 2 * p + h + 1)
                        else:
                            pe.wait_ge(out_added, 4 * g - 5 + h)
                        queries(next_c, h)
                    pe.wait_ge(wr_split, (p + 2 if c == 3 else p + 1))
                    if start:
                        pe.wait_ge(rot_done, 1)
                    else:
                        pe.wait_ge(av_ready, 2 * g - 1)
                    rotary(next_c)
                if folds_a(p, c):
                    pe.wait_ge(av_ready, 2 * g)
                    fold_a(p + 1)
                for i in range(4):
                    b, k = divmod(i, 2)
                    pe.wait_ge(p_ready, 4 * g + 2 * b + 2)
                    if not (start and i < 2):
                        pe.wait_ge(pt_ready, 4 * g + i - 1)
                    for h in range(2):
                        for t in range(2):
                            at = h * 256 + t * P
                            mm = pe.transpose(pt_ps[i % 2][:, at:at + P],
                                              prob[:, 2 * b + t, h, k * P:(k + 1) * P], T["ident"][:, :])
                    mm.then_inc(pt_done, 1)
                if not start:
                    def free(j):
                        if nxt:
                            pe.wait_ge(qa_split, 2 * g + 2 + j + 1)
                        else:
                            pe.wait_ge(out_added, 4 * g - 5 + j)

                    output(g - 1, (p - 1 if c == 0 else p), free)
                for b in range(2):
                    if not start:
                        pe.wait_ge(av_ready, 2 * g - 1 + b)
                    if b == 0 and nxt:
                        pe.wait_ge(rot_done, g + 2)
                    if b == 1 and folds_a(p, c):
                        pe.wait_ge(a_split, p + 2)
                    pe.wait_ge(pt_ready, 4 * g + 2 * b + 2)
                    for k in range(2):
                        mm = mm3(pe, av_ps[b][:, :], both(T["kv"], ALL, 4 * c + 2 * b + k),
                                 both(probT, ALL, 2 * b + k), k == 0, k == 1)
                    mm.then_inc(av_done, 1)
                if c == 0:
                    fold_b(g, p)

            fold_a(0)
            pe.wait_ge(a_split, 1)
            queries(0, 0)
            queries(0, 1)
            pe.wait_ge(wr_split, 1)
            rotary(0)
            over_steps(pe, step)
            output(STEPS - 1, PAIRS - 1, lambda j: pe.wait_ge(out_added, 4 * STEPS - 5 + j))


FF = 1024
KF = FF // P
QMAX = 127.0
MAGIC = 1.5 * 2.0 ** 23
H_IN = float(np.float32(1.0) / np.sqrt(np.float32(D)))
H_MID = float(np.float32(1.0) / np.sqrt(np.float32(FF)))


def ternary_weights(nc, X, d, F):
    with ExitStack() as ctx:
        def sb(name, shape, dt=F32):
            return ctx.enter_context(nc.sbuf_tensor("w_" + name, shape, dt))

        def sem(name):
            return ctx.enter_context(nc.semaphore("w_" + name))

        N = D * FF // P
        S = statistics(nc, ctx, "l3_", F["mv"], F["rstd"])
        raw = [sb("up_raw", [P, N]), sb("down_raw", [P, N])]
        h_raw = sb("h_raw", [P, KF * FF])
        ones = sb("ones", [P, P])
        magic = F["magic"]
        sums = sb("sums", [P, 2])
        inverse = sb("inverse", [P, 2])
        total_ps = ctx.enter_context(nc.psum_tensor("w_total", [P, 2], F32))
        loaded = [sem("up_loaded"), sem("down_loaded")]
        h_loaded = sem("h_loaded")
        h_copied = sem("h_copied")
        const_ready = sem("const_ready")
        summed = sem("summed")
        total_done = sem("total_done")
        mean_done = sem("mean_done")
        inverse_done = sem("inverse_done")
        rounded = sem("rounded")
        clipped = sem("clipped")
        written = sem("written")
        block = ctx.enter_context(nc.Block())
        PIECE = N // 4
        pieces = [(i, slice(j * PIECE, (j + 1) * PIECE)) for i in range(2) for j in range(4)]

        def h_scratch(i):
            return F["h"][:, i * N:(i + 1) * N]

        @block.sync
        def _(sp):
            sp.dma_start(raw[0][:, :], d["up"]).then_inc(loaded[0], 16)
            sp.dma_start(raw[1][:, :], d["down"]).then_inc(loaded[1], 16)
            sp.dma_start(h_raw[:, :], d["hadamard"]).then_inc(h_loaded, 16)

        @block.gpsimd
        def _(pool):
            pool.memset(ones[:, :], 1.0).then_inc(const_ready, 1)
            pool.memset(magic[:, :], MAGIC).then_inc(const_ready, 1)
            for n, (i, part) in enumerate(pieces):
                pool.wait_ge(clipped, n + 1)
                pool.tensor_scalar(F["t"][i][:, part], raw[i][:, part], -MAGIC, None,
                                   ALU.add).then_inc(written, 1)

        @block.scalar
        def _(act):
            statistics_scalar(act, S)
            for i in range(2):
                act.wait_ge(loaded[i], 16)
                act.activation(h_scratch(i), raw[i][:, :], ACT.Abs, accum_out=sums[:, i:i + 1]).then_inc(summed, 1)
            for n, (i, part) in enumerate(pieces):
                act.wait_ge(inverse_done, 1)
                act.wait_ge(const_ready, 2)
                act.activation(raw[i][:, part], raw[i][:, part], ACT.Identity, scale=inverse[:, i:i + 1],
                               bias=magic[:, 0:1]).then_inc(rounded, 1)
            act.wait_ge(h_loaded, 16)
            half = KF * FF // 2
            act.activation(F["h"][:, half:], h_raw[:, half:], ACT.Copy).then_inc(h_copied, 1)

        @block.vector
        def _(dve):
            statistics_vector(dve, X, S, None, 0)
            dve.wait_ge(total_done, 1)
            dve.tensor_scalar(F["scale_w"][:, :], total_ps[:, :], 1.0 / (D * FF), 1e-5, ALU.mult,
                              ALU.max).then_inc(mean_done, 1)
            dve.wait_ge(mean_done, 1)
            dve.reciprocal(inverse[:, :], F["scale_w"][:, :]).then_inc(inverse_done, 1)
            for n, (i, part) in enumerate(pieces):
                dve.wait_ge(rounded, n + 1)
                dve.tensor_scalar(raw[i][:, part], raw[i][:, part], MAGIC + 1.0, MAGIC - 1.0, ALU.min,
                                  ALU.max).then_inc(clipped, 1)
            dve.wait_ge(h_loaded, 16)
            dve.wait_ge(summed, 2)
            half = KF * FF // 2
            dve.tensor_copy(F["h"][:, 0:half], h_raw[:, 0:half]).then_inc(h_copied, 1)

        @block.tensor
        def _(pe):
            pe.wait_ge(const_ready, 2)
            pe.wait_ge(summed, 2)
            pe.matmul(total_ps[:, :], ones[:, :], sums[:, :], start=True, stop=True).then_inc(total_done, 1)


def feed_forward(nc, X, d, F, ident, out):
    with ExitStack() as ctx:
        def sb(name, shape, dt=F32):
            return ctx.enter_context(nc.sbuf_tensor("f_" + name, shape, dt))

        def sem(name):
            return ctx.enter_context(nc.semaphore("f_" + name))

        def psum(name, shape=(P, 512), dt=F32):
            return ctx.enter_context(nc.psum_tensor("f_" + name, list(shape), dt))

        ident_b = sb("ident_b", [P, P], BF16)
        xn = sb("xn", [P, D])
        xt = [sb("xt_" + n, [P, D], F32R) for n in ("hi", "lo")]
        y = sb("y", [P, D])
        xq = sb("xq", [P, D], BF16)
        xqT = sb("xqT", [P, KD, CHUNK], BF16)
        amax = sb("amax", [P, 1])
        bound = sb("bound", [P, TILES])
        rec = sb("rec", [P, 1])
        factor = sb("factor", [P, 1])
        r = [sb(f"r{i}", [P, CHUNK]) for i in range(2)]
        u = [sb("u_" + n, [P, KF, CHUNK], F32R) for n in ("hi", "lo")]
        amax2 = sb("amax2", [P, 2])
        unit = sb("unit", [P, 1])
        gain = sb("gain", [P, 1])
        top = sb("top", [P, 1])
        bound2 = sb("bound2", [P, 1])
        rec2 = sb("rec2", [P, 1])
        factor2 = sb("factor2", [P, 1])
        back = sb("back", [P, 2])
        y2 = sb("y2", [P, FF])
        q2 = sb("q2", [P, FF], BF16)
        q2T = sb("q2T", [P, KF, P], BF16)
        result = [sb(f"result{i}", [P, D]) for i in range(2)]
        t_ps, h_ps, down_ps = psum("t_ps"), psum("h_ps"), psum("down_ps")
        turn2_ps = psum("turn2_ps", (P, FF), BF16)
        up_ps = [psum(f"up_ps{i}") for i in range(2)]
        w_ps = [psum(f"w_ps{i}") for i in range(2)]
        turned_view = h_ps[:, 0:D // 2].bitcast(BF16)

        id_ready = sem("id_ready")
        xn_ready, t_done, t_hi, t_split = sem("xn_ready"), sem("t_done"), sem("t_hi"), sem("t_split")
        h_done, amax_done, bound_done = sem("h_done"), sem("amax_done"), sem("bound_done")
        rec_done, factor_done, y_done = sem("rec_done"), sem("factor_done"), sem("y_done")
        clip_done, xq_ready, turned, xq_copied = sem("clip_done"), sem("xq_ready"), sem("turned"), sem("xq_copied")
        up_done, relu_done, square_done = sem("up_done"), sem("relu_done"), sem("square_done")
        u_hi, u_split, w_done, amax2_done = sem("u_hi"), sem("u_split"), sem("w_done"), sem("amax2_done")
        small = sem("small")
        factor2_done, y2_done, clip2_done = sem("factor2_done"), sem("y2_done"), sem("clip2_done")
        q2_ready, turned2, q2_copied = sem("q2_ready"), sem("turned2"), sem("q2_copied")
        down_done, result_ready = sem("down_done"), sem("result_ready")
        stored = [sem(f"stored{i}") for i in range(2)]
        lone = {n: sem("lone_" + n) for n in ("dve", "pool")}
        block = ctx.enter_context(nc.Block())
        GROUPS = TILES // CT
        h3 = F["h"][:, :].rearrange("p (k n) -> p k n", k=KF)
        up3 = F["t"][0][:, :].rearrange("p (k n) -> p k n", k=KD)
        down3 = F["t"][1][:, :].rearrange("p (k n) -> p k n", k=KF)

        def is_at(g, value):
            return isinstance(g, int) and g == value

        def tile_of_X(s):
            return X[:, bass.ds(s, 1), :].rearrange("p a n -> p (a n)")

        def over_groups(eng, T, H, Q, U, W, D1, D2):
            T(0, 0)
            for i in range(CT):
                H(i, i)
                if i < CT - 1:
                    T(i + 1, i + 1)
                Q(i, i)
            U(0)

            def group(n, has_next):
                for i in range(CT):
                    if has_next:
                        if i == 0:
                            T(4 * n + 4, 0)
                        H(4 * n + 4 + i, i)
                        if i < CT - 1:
                            T(4 * n + 5 + i, i + 1)
                    if i >= 2:
                        D2(4 * n + i - 2, i - 2, n)
                    W(4 * n + i, i, n)
                    if has_next:
                        Q(4 * n + 4 + i, i)
                    if i >= 1:
                        D1(4 * n + i - 1, i - 1)
                D2(4 * n + 2, 2, n)
                if has_next:
                    U(n + 1)
                D1(4 * n + 3, 3)
                D2(4 * n + 3, 3, n)

            group(0, True)
            with eng.Fori(1, GROUPS - 1) as n:
                group(n, True)
            group(GROUPS - 1, False)

        def nothing(*_):
            pass

        @block.sync
        def _(sp):
            rows = out.rearrange("(s p) n -> s p n", p=P)
            with sp.Fori(0, TILES // 2) as it:
                for i in range(2):
                    sp.wait_ge(result_ready, 2 * it + i + 1)
                    sp.dma_start(rows[2 * it + i], result[i][:, :]).then_inc(stored[i], 16)
            for i in range(2):
                sp.wait_ge(stored[i], 16 * TILES // 2)

        @block.gpsimd
        def _(pool):
            pool.tensor_copy(ident_b[:, :], ident[:, :]).then_inc(id_ready, 1)

            def H(s, i):
                if not is_at(s, 0):
                    pool.wait_ge(turned, s)
                pool.wait_ge(clip_done, s + 1)
                alone(pool, lone["pool"])
                pool.tensor_scalar(xq[:, :], y[:, :], -MAGIC, None, ALU.add).then_inc(xq_ready, 1)

            def W(s, i, n):
                if not is_at(s, 0):
                    pool.wait_ge(turned2, s)
                pool.wait_ge(clip2_done, s + 1)
                alone(pool, lone["pool"])
                pool.tensor_scalar(q2[:, :], y2[:, :], -MAGIC, None, ALU.add).then_inc(q2_ready, 1)

            over_groups(pool, nothing, H, nothing, nothing, W, nothing, nothing)

        @block.scalar
        def _(act):
            def T(s, i):
                act.wait_ge(t_done, s + 1)
                act.activation(xt[0][:, :], t_ps[:, :], ACT.Copy).then_inc(t_hi, 1)

            def H(s, i):
                if not is_at(s, 0):
                    act.wait_ge(xq_ready, s)
                act.wait_ge(factor_done, s + 1)
                act.activation(y[:, :], h_ps[:, :], ACT.Identity, scale=factor[:, 0:1],
                               bias=F["magic"][:, 0:1]).then_inc(y_done, 1)

            def Q(s, i):
                act.wait_ge(turned, s + 1)
                act.activation(xqT[:, :, i * P:(i + 1) * P], r3(turned_view, P), ACT.Copy).then_inc(xq_copied, 1)

            def U(n):
                def leading(o):
                    act.wait_ge(square_done, KF * n + o + 1)
                    act.activation(u[0][:, o, :], r[o % 2][:, :], ACT.Copy).then_inc(u_hi, 1)

                for o in range(KF):
                    act.wait_ge(up_done, KF * n + o + 1)
                    if not (is_at(n, 0) and o < 2):
                        act.wait_ge(u_split, KF * n + o - 1)
                    act.activation(r[o % 2][:, :], up_ps[o % 2][:, :], ACT.Relu).then_inc(relu_done, 1)
                    if o:
                        leading(o - 1)
                leading(KF - 1)

            def W(s, i, n):
                if not is_at(s, 0):
                    act.wait_ge(q2_ready, s)
                act.wait_ge(factor2_done, s + 1)
                for j in range(2):
                    ins = act.activation(y2[:, j * 512:(j + 1) * 512], w_ps[j][:, :], ACT.Identity,
                                         scale=factor2[:, 0:1], bias=F["magic"][:, 0:1])
                ins.then_inc(y2_done, 1)

            def D1(s, i):
                act.wait_ge(turned2, s + 1)
                if not is_at(s, 0):
                    act.wait_ge(down_done, s)
                act.activation(q2T[:, :, :], r3(turn2_ps[:, :], P), ACT.Copy).then_inc(q2_copied, 1)

            over_groups(act, T, H, Q, U, W, D1, nothing)

        @block.vector
        def _(dve):
            def normalize(s):
                dve.tensor_scalar(xn[:, :], tile_of_X(s), F["mv"][:, bass.ds(s, 1), 0],
                                  F["rstd"][:, bass.ds(s, 1)], ALU.subtract, ALU.mult).then_inc(xn_ready, 1)

            def T(s, i):
                if i == 0:
                    normalize(s)
                dve.wait_ge(t_hi, s + 1)
                dve.tensor_tensor(xt[1][:, :], t_ps[:, :], xt[0][:, :].bitcast(F32),
                                  ALU.subtract).then_inc(t_split, 1)
                if i < CT - 1:
                    normalize(s + 1)

            def H(s, i):
                dve.wait_ge(h_done, s + 1)
                dve.tensor_reduce(amax[:, :], h_ps[:, :], AX.X, ALU.max,
                                  apply_absolute_value=True).then_inc(amax_done, 1)
                dve.wait_ge(amax_done, s + 1)
                dve.tensor_scalar(bound[:, bass.ds(s, 1)], amax[:, :], H_IN, 1e-5, ALU.mult,
                                  ALU.max).then_inc(bound_done, 1)
                dve.wait_ge(bound_done, s + 1)
                alone(dve, lone["dve"])
                dve.reciprocal(rec[:, :], bound[:, bass.ds(s, 1)]).then_inc(rec_done, 1)
                dve.wait_ge(rec_done, s + 1)
                dve.tensor_scalar(factor[:, :], rec[:, :], QMAX * H_IN, None, ALU.mult).then_inc(factor_done, 1)
                dve.wait_ge(y_done, s + 1)
                dve.tensor_scalar(y[:, :], y[:, :], MAGIC + QMAX, MAGIC - QMAX, ALU.min,
                                  ALU.max).then_inc(clip_done, 1)

            def U(n):
                def rest(o):
                    dve.wait_ge(u_hi, KF * n + o + 1)
                    dve.tensor_tensor(u[1][:, o, :], r[o % 2][:, :], u[0][:, o, :].bitcast(F32),
                                      ALU.subtract).then_inc(u_split, 1)

                for o in range(KF):
                    dve.wait_ge(relu_done, KF * n + o + 1)
                    dve.tensor_tensor(r[o % 2][:, :], r[o % 2][:, :], r[o % 2][:, :],
                                      ALU.mult).then_inc(square_done, 1)
                    if o:
                        rest(o - 1)
                rest(KF - 1)

            def W(s, i, n):
                dve.wait_ge(w_done, s + 1)
                for j in range(2):
                    ins = dve.tensor_reduce(amax2[:, j:j + 1], w_ps[j][:, :], AX.X, ALU.max,
                                            apply_absolute_value=True)
                dve.tensor_scalar(unit[:, :], bound[:, bass.ds(s, 1)], F["scale_w"][:, 0:1], 1.0 / QMAX,
                                  ALU.mult, ALU.mult).then_inc(small, 1)
                dve.wait_ge(small, 5 * s + 1)
                dve.tensor_scalar(gain[:, :], unit[:, :], unit[:, 0:1], H_MID, ALU.mult, ALU.mult).then_inc(small, 1)
                dve.wait_ge(small, 5 * s + 2)
                dve.tensor_scalar(top[:, :], amax2[:, 0:1], amax2[:, 1:2], gain[:, 0:1], ALU.max,
                                  ALU.mult).then_inc(small, 1)
                dve.wait_ge(small, 5 * s + 3)
                dve.tensor_scalar(bound2[:, :], top[:, :], 1e-5, None, ALU.max).then_inc(small, 1)
                dve.wait_ge(small, 5 * s + 4)
                dve.reciprocal(rec2[:, :], bound2[:, :]).then_inc(small, 1)
                dve.tensor_scalar(back[:, i % 2:i % 2 + 1], bound2[:, :], F["scale_w"][:, 1:2], 1.0 / QMAX,
                                  ALU.mult, ALU.mult)
                dve.wait_ge(small, 5 * s + 5)
                dve.tensor_scalar(factor2[:, :], rec2[:, :], gain[:, 0:1], QMAX, ALU.mult,
                                  ALU.mult).then_inc(factor2_done, 1)
                dve.wait_ge(y2_done, s + 1)
                dve.tensor_scalar(y2[:, :], y2[:, :], MAGIC + QMAX, MAGIC - QMAX, ALU.min,
                                  ALU.max).then_inc(clip2_done, 1)

            def D2(s, i, n):
                if not (is_at(s, 0) or is_at(s, 1)):
                    dve.wait_ge(stored[i % 2], 32 * n + 16 * (i // 2))
                dve.wait_ge(down_done, s + 1)
                dve.scalar_tensor_tensor(out=result[i % 2][:, :], in0=down_ps[:, :],
                                         scalar=back[:, i % 2:i % 2 + 1], in1=tile_of_X(s),
                                         op0=ALU.mult, op1=ALU.add).then_inc(result_ready, 1)

            over_groups(dve, T, H, nothing, U, W, nothing, D2)

        @block.tensor
        def _(pe):
            pe.wait_ge(id_ready, 1)

            def T(s, i):
                pe.wait_ge(xn_ready, s + 1)
                if not is_at(s, 0):
                    pe.wait_ge(t_split, s)
                for k in range(KD):
                    mm = pe.transpose(t_ps[:, k * P:(k + 1) * P], xn[:, k * P:(k + 1) * P], ident[:, :])
                mm.then_inc(t_done, 1)

            def H(s, i):
                pe.wait_ge(t_split, s + 1)
                if not is_at(s, 0):
                    pe.wait_ge(xq_copied, s)
                for k in range(KD):
                    for part in range(2):
                        mm = pe.matmul(h_ps[:, :], xt[part][:, k * P:(k + 1) * P], h3[:, k, 0:D],
                                       start=(k == 0 and part == 0), stop=(k == KD - 1 and part == 1))
                mm.then_inc(h_done, 1)

            def Q(s, i):
                pe.wait_ge(xq_ready, s + 1)
                for k in range(KD):
                    mm = pe.transpose(turned_view[:, k * P:(k + 1) * P], xq[:, k * P:(k + 1) * P], ident_b[:, :])
                mm.then_inc(turned, 1)

            def U(n):
                pe.wait_ge(xq_copied, 4 * n + 4)
                for o in range(KF):
                    if not (is_at(n, 0) and o < 2):
                        pe.wait_ge(relu_done, KF * n + o - 1)
                    for k in range(KD):
                        mm = pe.matmul(up_ps[o % 2][:, :], up3[:, k, o * P:(o + 1) * P], xqT[:, k, :],
                                       start=(k == 0), stop=(k == KD - 1))
                    mm.then_inc(up_done, 1)

            def W(s, i, n):
                pe.wait_ge(u_split, KF * n + KF)
                if not is_at(s, 0):
                    pe.wait_ge(y2_done, s)
                for k in range(KF):
                    for part in range(2):
                        for j in range(2):
                            mm = pe.matmul(w_ps[j][:, :], u[part][:, k, i * P:(i + 1) * P],
                                           h3[:, k, j * 512:(j + 1) * 512],
                                           start=(k == 0 and part == 0), stop=(k == KF - 1 and part == 1))
                mm.then_inc(w_done, 1)

            def D1(s, i):
                pe.wait_ge(q2_ready, s + 1)
                if not is_at(s, 0):
                    pe.wait_ge(q2_copied, s)
                for k in range(KF):
                    mm = pe.transpose(turn2_ps[:, k * P:(k + 1) * P], q2[:, k * P:(k + 1) * P], ident_b[:, :])
                mm.then_inc(turned2, 1)

            def D2(s, i, n):
                pe.wait_ge(q2_copied, s + 1)
                if not is_at(s, 0):
                    pe.wait_ge(result_ready, s)
                for k in range(KF):
                    mm = pe.matmul(down_ps[:, :], q2T[:, k, :], down3[:, k, :], start=(k == 0), stop=(k == KF - 1))
                mm.then_inc(down_done, 1)

            over_groups(pe, T, H, Q, U, W, D1, D2)


def decoder_layer(nc, d, out):
    attT = nc.dram_tensor("attT", (STEPS, P, 2, CHUNK), F32, kind="Internal").ap()
    x1 = nc.dram_tensor("x1", (TOKENS, D), F32, kind="Internal").ap()
    with ExitStack() as ctx:
        X = ctx.enter_context(nc.sbuf_tensor("X", [P, TILES, D], F32))
        ident = ctx.enter_context(nc.sbuf_tensor("ident", [P, P], F32))
        LOADS = 4
        x_loaded = [ctx.enter_context(nc.semaphore(f"x_loaded{i}")) for i in range(LOADS)]
        consts_loaded = ctx.enter_context(nc.semaphore("consts_loaded"))

        with nc.Block() as block:
            @block.sync
            def _(sp):
                for i in range(LOADS):
                    rows = slice(i * TOKENS // LOADS, (i + 1) * TOKENS // LOADS)
                    sp.dma_start(X[:, i * TILES // LOADS:(i + 1) * TILES // LOADS, :],
                                 d["x"][rows, :].rearrange("(t p) n -> p t n", p=P)).then_inc(x_loaded[i], 16)
                sp.dma_start(ident[:, :], d["ident"]).then_inc(consts_loaded, 16)
                sp.wait_ge(consts_loaded, 16)

        with ExitStack() as phase:
            xT = [phase.enter_context(nc.sbuf_tensor("xT_" + n, [P, KD, TOKENS], F32R)) for n in ("hi", "lo")]
            layernorm_transposed(nc, X, x_loaded, LOADS, ident, "l1_", *xT)
            segment_attention(nc, X, ident, xT, d, consts_loaded, attT)
        attention_output(nc, X, d, attT, x1)
        reuse_semaphores(nc)

        with ExitStack() as phase:
            def sb(name, shape, dt=F32):
                return phase.enter_context(nc.sbuf_tensor("t_" + name, shape, dt))

            def parts(name, shape):
                return sb(name + "_hi", shape, F32R), sb(name + "_lo", shape, F32R)

            T = {"ident": ident, "cos": sb("cos", [P, KEYS]), "sin": sb("sin", [P, KEYS]),
                 "mask": sb("mask", [P, TILES, KEYS], BF16), "kvT": parts("kvT", [P, TOKENS]),
                 "kv": parts("kv", [P, TILES, P]), "kr": parts("kr", [P, SEQS, 2, KEYS]),
                 "qc": parts("qc", [P, QC, TOKENS])}
            latents(nc, d, T)
            with ExitStack() as inner:
                xT = [inner.enter_context(nc.sbuf_tensor("x2T_" + n, [P, KD, TOKENS], F32R)) for n in ("hi", "lo")]
                layernorm_transposed(nc, X, None, None, ident, "l2_", *xT)
                query_latent(nc, d, T, xT)
            cross_attention(nc, X, d, T)

        with ExitStack() as phase:
            def sb(name, shape, dt=F32):
                return phase.enter_context(nc.sbuf_tensor("g_" + name, shape, dt))

            F = {"mv": sb("mv", [P, TILES, 2]), "rstd": sb("rstd", [P, TILES]), "magic": sb("magic", [P, 1]),
                 "scale_w": sb("scale_w", [P, 2]), "h": sb("h", [P, KF * FF], F32R),
                 "t": [sb("up_t", [P, D * FF // P], BF16), sb("down_t", [P, D * FF // P], BF16)]}
            ternary_weights(nc, X, d, F)
            feed_forward(nc, X, d, F, ident, out)


def lay_out(inputs):
    f = {k: np.asarray(v) for k, v in inputs.items()}
    a = {"x": f["x"].reshape(TOKENS, D)}
    a["ident"] = np.eye(P, dtype=np.float32)
    s = np.arange(P)
    a["causal"] = np.where(s[None, :] <= s[:, None], 0.0, NEG).astype(np.float32)
    a["betas"] = f["L0_attn_betas"].reshape(HEADS, P).T
    for n in "qkv":
        a["w" + n] = f["L0_attn_W" + n].reshape(KD, P, PAIRS, 256).transpose(2, 1, 0, 3).reshape(PAIRS, P, 1024)
    a["wo"] = f["L0_attn_Wo"].reshape(HEADS, P, D).transpose(1, 0, 2)
    def rows(w, n):
        return w.reshape(n, P, -1).transpose(1, 0, 2)

    def filled(w):
        return np.concatenate([w, np.zeros((QC * P - w.shape[0],) + w.shape[1:], w.dtype)])

    a["ctxT"] = f["ctx_2048"].reshape(CHUNKS, CHUNK, KD, P).transpose(0, 3, 2, 1)
    kr = f["L0_xattn_W_kr"].reshape(P, 2, 1, 32)
    a["wkv"] = np.concatenate([rows(f["L0_xattn_W_kvc"], KD), np.repeat(kr, 2, 2).reshape(P, 1, P)], 1)
    a["wdq"] = rows(np.ascontiguousarray(filled(f["L0_xattn_W_dq"].T).T), KD)
    a["ids"] = f["itok_BxS_0_1023"].reshape(TILES, P).T
    a["kio"] = np.broadcast_to(np.arange(KEYS, dtype=np.float32), (P, KEYS))
    freq = np.float32(1.0) / np.float32(10000.0) ** (np.arange(32, dtype=np.float32) / np.float32(32))
    ang = (np.arange(KEYS, dtype=np.float32)[:, None] * freq).T
    a["cos"] = np.tile(np.cos(ang), (4, 1))
    a["sin"] = np.concatenate([np.tile(-np.sin(ang), (2, 1)), np.tile(np.sin(ang), (2, 1))])
    head_of_row = np.arange(P) // 32 % 2
    a["rows_of"] = np.stack([head_of_row == 0, head_of_row == 1], 1).astype(np.float32)
    uq = filled(f["L0_xattn_W_uq"]).reshape(QC * P, PAIRS, 2, P).transpose(1, 3, 2, 0)
    uk = f["L0_xattn_W_uk"].reshape(P, PAIRS, 2, P).transpose(1, 3, 2, 0)
    uv = f["L0_xattn_W_uv"].reshape(P, PAIRS, 2, P).transpose(1, 3, 2, 0)
    wo = f["L0_xattn_W_o"].reshape(PAIRS, 2, P, D).transpose(0, 2, 1, 3)
    a["xw"] = np.concatenate([uq, uk, uv, wo], 3)
    qr = filled(f["L0_xattn_W_qr"]).reshape(QC, P, PAIRS, 2, 2, 32)
    a["xwr"] = qr.transpose(2, 1, 0, 4, 3, 5).reshape(PAIRS, P, QC, P)
    a["up"] = rows(f["L0_ffn_w_up"].T, KD).reshape(P, -1)
    a["down"] = rows(f["L0_ffn_w_down"].T, KF).reshape(P, -1)
    sylvester = np.ones((1, 1), np.float32)
    while len(sylvester) < FF:
        sylvester = np.block([[sylvester, sylvester], [sylvester, -sylvester]])
    a["hadamard"] = rows(sylvester, KF).reshape(P, -1)
    return {k: np.ascontiguousarray(v) for k, v in a.items()}


def kernel(**inputs):
    import concourse.bacc as _bacc
    from concourse.bass_utils import run_bass_kernel_spmd as _run

    nc = _bacc.Bacc("TRN2", target_bir_lowering=False, num_devices=1, dynamic_dma_scratch_size=1024)
    arrays = lay_out(inputs)
    d = {k: nc.dram_tensor("in_" + k, v.shape, mybir.dt.from_np(v.dtype), kind="ExternalInput").ap()
         for k, v in arrays.items()}
    out = nc.dram_tensor("out_x", (TOKENS, D), F32, kind="ExternalOutput").ap()
    decoder_layer(nc, d, out)
    r = _run(nc, [{"in_" + k: v for k, v in arrays.items()}], core_ids=[0])
    return r.results[0]["out_x"].reshape(8, 256, D)
```

```python
from contextlib import ExitStack

import numpy as np

import concourse.bass as bass
from concourse import mybir

F32 = mybir.dt.float32
F32R = mybir.dt.float32r
BF16 = mybir.dt.bfloat16
I32 = mybir.dt.int32
ACT = mybir.ActivationFunctionType
ALU = mybir.AluOpType
AX = mybir.AxisListType

P = 128
TOKENS = 2048
TILES = TOKENS // P
D = 512
KD = D // P
HEADS = 16
PAIRS = HEADS // 2
CHUNK = 512
CHUNKS = TOKENS // CHUNK
CT = CHUNK // P
STEPS = PAIRS * CHUNKS
EPS = 1e-5
NEG = -1e30
ATT_SCALE = float(np.float32(128.0) ** np.float32(-0.5))


def r3(ap, n):
    return ap.rearrange("p (a b) -> p a b", b=n)


def mm3(pe, out, lhs, rhs, first=True, last=True):
    (lh, ll), (rh, rl) = lhs, rhs
    pe.matmul(out, lh, rh, start=first, stop=False)
    pe.matmul(out, lh, rl, start=False, stop=False)
    return pe.matmul(out, ll, rh, start=False, stop=last)


def reuse_semaphores(nc):
    over = sorted(nc.released_uncleared_semaphores)
    with nc.Block() as block:
        @block.gpsimd
        def _(pool):
            pool.sem_clear(range(over[0], over[-1] + 1))


def alone(eng, sem):
    eng.sem_inc(sem, 1)


def statistics(nc, ctx, tag, mv, rstd):
    def sb(name, shape):
        return ctx.enter_context(nc.sbuf_tensor(tag + name, shape, F32))

    S = {n: ctx.enter_context(nc.semaphore(tag + n)) for n in
         ("stats_done", "aggr_done", "var_ready", "std_ready", "rstd_ready")}
    S.update(mv=mv, rstd=rstd, st=sb("st", [P, TILES, 6]), var_eps=sb("var_eps", [P, TILES]),
             std=sb("std", [P, TILES]))
    return S


def statistics_vector(dve, X, S, x_loaded, x_loads):
    for t in range(TILES):
        if x_loaded is not None:
            dve.wait_ge(x_loaded[t // (TILES // x_loads)], 16)
        dve.bn_stats(S["st"][:, t, :], X[:, t, :]).then_inc(S["stats_done"], 1)
    for t in range(TILES):
        dve.wait_ge(S["stats_done"], t + 1)
        dve.bn_aggr(S["mv"][:, t, :], S["st"][:, t, :]).then_inc(S["aggr_done"], 1)
    std, rstd, done = S["std"], S["rstd"], S["rstd_ready"]
    dve.wait_ge(S["aggr_done"], TILES)
    dve.tensor_scalar(S["var_eps"][:, :], S["mv"][:, :, 1], EPS, None, ALU.add).then_inc(S["var_ready"], 1)
    dve.wait_ge(S["std_ready"], 1)
    dve.reciprocal(rstd[:, :], std[:, :]).then_inc(done, 1)
    dve.wait_ge(done, 1)
    dve.tensor_tensor(std[:, :], rstd[:, :], rstd[:, :], ALU.mult).then_inc(done, 1)
    dve.wait_ge(done, 2)
    dve.tensor_tensor(std[:, :], std[:, :], S["var_eps"][:, :], ALU.mult).then_inc(done, 1)
    dve.wait_ge(done, 3)
    dve.tensor_scalar(std[:, :], std[:, :], -0.5, 1.5, ALU.mult, ALU.add).then_inc(done, 1)
    dve.wait_ge(done, 4)
    dve.tensor_tensor(rstd[:, :], rstd[:, :], std[:, :], ALU.mult).then_inc(done, 1)
    dve.wait_ge(done, 5)


def statistics_scalar(act, S):
    act.wait_ge(S["var_ready"], 1)
    act.activation(S["std"][:, :], S["var_eps"][:, :], ACT.Sqrt).then_inc(S["std_ready"], 1)


def layernorm_transposed(nc, X, x_loaded, x_loads, ident, tag, hi, lo):
    with ExitStack() as ctx:
        def sb(name, shape, dt=F32):
            return ctx.enter_context(nc.sbuf_tensor(tag + name, shape, dt))

        def sem(name):
            return ctx.enter_context(nc.semaphore(tag + name))

        mv = sb("mv", [P, TILES, 2])
        rstd = sb("rstd", [P, TILES])
        S = statistics(nc, ctx, tag, mv, rstd)
        xn = sb("xn", [P, 2, D])
        turned = [ctx.enter_context(nc.psum_tensor(f"{tag}turned{i}", [P, D], F32)) for i in range(2)]
        xn_ready = sem("xn_ready")
        lone = sem("lone")
        turned_ready = sem("turned_ready")
        hi_written = sem("hi_written")
        lo_written = sem("lo_written")
        block = ctx.enter_context(nc.Block())

        @block.vector
        def _(dve):
            statistics_vector(dve, X, S, x_loaded, x_loads)

            def normalize(t, i):
                dve.tensor_scalar(xn[:, i, :], X[:, bass.ds(t, 1), :].rearrange("p a n -> p (a n)"),
                                  mv[:, bass.ds(t, 1), 0], rstd[:, bass.ds(t, 1)],
                                  ALU.subtract, ALU.mult).then_inc(xn_ready, 1)

            normalize(0, 0)
            normalize(1, 1)
            with dve.Fori(0, TILES // 2) as it:
                for i in range(2):
                    t = 2 * it + i
                    dve.wait_ge(hi_written, t + 1)
                    dve.tensor_tensor(lo[:, :, bass.ds(t * P, P)], r3(turned[i][:, :], P),
                                      hi[:, :, bass.ds(t * P, P)].bitcast(F32),
                                      ALU.subtract).then_inc(lo_written, 1)
                    normalize((t + 2) % TILES, i)

        @block.scalar
        def _(act):
            statistics_scalar(act, S)
            with act.Fori(0, TILES // 2) as it:
                for i in range(2):
                    t = 2 * it + i
                    act.wait_ge(turned_ready, t + 1)
                    alone(act, lone)
                    act.activation(hi[:, :, bass.ds(t * P, P)], r3(turned[i][:, :], P),
                                   ACT.Copy).then_inc(hi_written, 1)

        @block.tensor
        def _(pe):
            def turn(t, i):
                pe.wait_ge(xn_ready, t + 1)
                for k in range(KD):
                    mm = pe.transpose(turned[i][:, k * P:(k + 1) * P], xn[:, i, k * P:(k + 1) * P],
                                      ident[:, :])
                mm.then_inc(turned_ready, 1)

            turn(0, 0)
            turn(1, 1)
            with pe.Fori(1, TILES // 2) as it:
                for i in range(2):
                    pe.wait_ge(lo_written, 2 * it + i - 1)
                    turn(2 * it + i, i)


def segment_attention(nc, X, ident, xT, d, consts_loaded, attT):
    with ExitStack() as ctx:
        def sb(name, shape, dt=F32):
            return ctx.enter_context(nc.sbuf_tensor("a_" + name, shape, dt))

        def parts(name, shape):
            return sb(name + "_hi", shape, F32R), sb(name + "_lo", shape, F32R)

        def sem(name):
            return ctx.enter_context(nc.semaphore("a_" + name))

        def psum(name):
            return ctx.enter_context(nc.psum_tensor("a_" + name, [P, 512], F32))

        def both(pair, *index):
            return pair[0][index], pair[1][index]

        ones = sb("ones", [P, P])
        ones_r = sb("ones_r", [P, P], F32R)
        z_start = sb("z_start", [P, P], F32R)
        mask = sb("mask", [P, P])
        betas = sb("betas", [P, HEADS])
        beta_e = sb("beta_e", [P, HEADS])
        gate = sb("gate", [P, HEADS, 2])
        gate_p = sb("gate_p", [P, 2, 2])
        w_raw = {n: sb("raw_" + n, [P, 1024]) for n in "qkv"}
        w = {n: parts("w" + n, [P, KD, 256]) for n in "qkv"}
        qT = parts("qT", [P, 2, CHUNK])
        kT = parts("kT", [P, 2, CHUNK])
        v = parts("v", [P, CT, 256])
        e = sb("e", [P, 2, 256])
        sq = sb("sq", [P, 2, 256])
        sk = sb("sk", [P, 2, 256])
        sqp = [parts(f"sq{i}", [P, 2, 256]) for i in range(2)]
        skp = parts("skt", [P, 4, P])
        prob = sb("prob", [P, 2, CT, P])
        probT = parts("probT", [P, 2, CT * P])
        mx = sb("mx", [P, 2, CT])
        nb = sb("nb", [P, 2, CT])
        rs = sb("rs", [P, 2, CT])
        rr = sb("rr", [P, 2, CT])
        mem = parts("mem", [P, 2, 512])
        att = sb("att", [P, 2, CHUNK])
        rec = sb("rec", [P, 256])
        amr = sb("amr", [P, 256])

        bank = [psum("bank0"), psum("bank1")]
        s_ps = [psum("s0"), psum("s1")]
        mem_ps = [psum("mem0"), psum("mem1")]
        ad_ps = [psum("ad0"), psum("ad1")]

        raw_loaded = {n: sem("raw_loaded_" + n) for n in "qkv"}
        w_split = {n: sem("w_split_" + n) for n in "qkv"}
        w_hi = sem("w_hi")
        ones_ready = sem("ones_ready")
        beta_step = sem("beta_step")
        gate_ready = sem("gate_ready")
        filled = sem("filled")
        hi_done = sem("hi_done")
        freed = sem("freed")
        sig_done = sem("sig_done")
        sq_hi = sem("sq_hi")
        sq_ready = sem("sq_ready")
        s_done = sem("s_done")
        max_done = sem("max_done")
        nb_done = sem("nb_done")
        exp_done = sem("exp_done")
        rr_done = sem("rr_done")
        p_ready = sem("p_ready")
        pt_done = sem("pt_done")
        pt_hi = sem("pt_hi")
        pt_ready = sem("pt_ready")
        skt_done = sem("skt_done")
        skt_hi = sem("skt_hi")
        sk_ready = sem("sk_ready")
        mem_done = sem("mem_done")
        mem_hi = sem("mem_hi")
        mem_ready = sem("mem_ready")
        ad_done = sem("ad_done")
        ad_read = sem("ad_read")
        am_done = sem("am_done")
        rec_done = sem("rec_done")
        amr_done = sem("amr_done")
        att_done = sem("att_done")
        att_stored = sem("att_stored")
        wo_loaded = sem("wo_loaded")
        lone = {n: sem("lone_" + n) for n in ("dve", "pool")}
        block = ctx.enter_context(nc.Block())

        Q, K, V = 0, 2, 4

        def fill(chunk, kind, j):
            return 6 * chunk + kind + j

        def over_steps(eng, step):
            step(0, 0, True)
            with eng.Fori(0, PAIRS - 1) as p:
                for c in range(1, CHUNKS + 1):
                    step(CHUNKS * p + c, c % CHUNKS, True)
            for g in range(STEPS - CHUNKS + 1, STEPS):
                step(g, g % CHUNKS, g < STEPS - 1)

        def seg(ap, s):
            return ap.rearrange("p (b s t) -> p b s t", b=2, s=2)[:, :, s, :]

        @block.sync
        def _(sp):
            sp.dma_start(mask[:, :], d["causal"]).then_inc(consts_loaded, 16)
            sp.dma_start(betas[:, :], d["betas"]).then_inc(consts_loaded, 16)
            for n in "qkv":
                sp.dma_start(w_raw[n][:, :], d["w" + n][0]).then_inc(raw_loaded[n], 16)

            sp.dma_start(X[:, :, :], d["wo"]).then_inc(wo_loaded, 16)

            def store(g):
                sp.wait_ge(att_done, 2 * g + 2)
                sp.dma_start(attT[g], att[:, :, :]).then_inc(att_stored, 16)

            def load(n, p):
                sp.wait_ge(w_split[n], p + 1)
                sp.dma_start(w_raw[n][:, :], d["w" + n][p + 1]).then_inc(raw_loaded[n], 16)

            with sp.Fori(0, PAIRS - 1) as p:
                for n in "qkv":
                    load(n, p)
                for c in range(CHUNKS):
                    store(CHUNKS * p + c)
            for g in range(STEPS - CHUNKS, STEPS):
                store(g)
            sp.wait_ge(att_stored, 16 * STEPS)
            sp.wait_ge(wo_loaded, 16)

        @block.gpsimd
        def _(pool):
            pool.memset(ones[:, :], 1.0).then_inc(ones_ready, 1)
            pool.wait_ge(ones_ready, 1)
            pool.tensor_copy(ones_r[:, :], ones[:, :]).then_inc(ones_ready, 1)
            pool.tensor_scalar(z_start[:, :], ones[:, :], 1.0 / (P * P), None,
                               ALU.mult).then_inc(ones_ready, 1)

            def split(n, raw, loads, dst, p, splits):
                flat = [x[:, :, :].rearrange("p a b -> p (a b)") for x in dst]
                pool.wait_ge(raw_loaded[raw], 16 * loads)
                alone(pool, lone["pool"])
                pool.tensor_copy(flat[0], w_raw[raw][:, :]).then_inc(w_hi, 1)
                pool.wait_ge(w_hi, splits)
                pool.tensor_tensor(flat[1], w_raw[raw][:, :], flat[0].bitcast(F32),
                                   ALU.subtract).then_inc(w_split[n], 1)

            def take_gate(p):
                pool.wait_ge(gate_ready, 1)
                pool.tensor_copy(gate_p[:, :, :], gate[:, bass.ds(2 * p, 2), :]).then_inc(gate_ready, 1)

            for i, n in enumerate("qkv"):
                split(n, n, 1, w[n], 0, i + 1)

            def step(g, c, nxt):
                if c == 0:
                    if not (isinstance(g, int) and g == 0):
                        pool.wait_ge(att_done, 2 * g)
                    take_gate(pair_of[0])
                for h in range(2):
                    pool.wait_ge(rr_done, 2 * g + h + 1)
                    pool.tensor_tensor(prob[:, h], prob[:, h],
                                       rr[:, h, :].unsqueeze(2).to_broadcast([P, CT, P]),
                                       ALU.mult).then_inc(p_ready, 1)
                if nxt:
                    split_sq(g + 1, (c + 1) % 2)
                p = pair_of[0]
                if c == 2 and not (isinstance(p, int) and p == PAIRS - 1):
                    for i, (n, kind) in enumerate((("q", Q), ("k", K), ("v", V))):
                        pool.wait_ge(filled, fill(g + 1, kind, 1) + 1)
                        split(n, n, p + 2, w[n], p + 1, 3 * p + 4 + i)

            def split_sq(g, par):
                pool.wait_ge(sig_done, 4 * g + 2)
                alone(pool, lone["pool"])
                hi, lo = sqp[par]
                pool.tensor_copy(hi[:, :, :], sq[:, :, :]).then_inc(sq_hi, 1)
                pool.wait_ge(sq_hi, g + 1)
                pool.tensor_tensor(lo[:, :, :], sq[:, :, :], hi[:, :, :].bitcast(F32),
                                   ALU.subtract).then_inc(sq_ready, 1)

            split_sq(0, 0)
            pair_of = [0]
            step(0, 0, True)
            with pool.Fori(0, PAIRS - 1) as p:
                for c in range(1, CHUNKS + 1):
                    pair_of[0] = p + c // CHUNKS
                    step(CHUNKS * p + c, c % CHUNKS, True)
            pair_of[0] = PAIRS - 1
            for g in range(STEPS - CHUNKS + 1, STEPS):
                step(g, g % CHUNKS, g < STEPS - 1)

        @block.scalar
        def _(act):
            act.wait_ge(consts_loaded, 48)
            act.activation(beta_e[:, :], betas[:, :], ACT.Exp, scale=-1.0).then_inc(beta_step, 1)

            def project(gc, kind):
                for j in range(2):
                    act.wait_ge(filled, fill(gc, kind, j) + 1)
                    src = bank[j]
                    if kind == V:
                        dst = v[0][:, 2 * j:2 * j + 2, :].rearrange("p a n -> p (a n)")
                    else:
                        dst = (qT if kind == Q else kT)[0][:, j]
                        if not (isinstance(gc, int) and gc == 0):
                            act.wait_ge(sq_ready if kind == Q else skt_done, gc)
                        if kind == K:
                            act.wait_ge(sig_done, 4 * gc + 1 + j)
                        elif not (isinstance(gc, int) and gc == 0):
                            act.wait_ge(sig_done, 4 * gc - 1 + j)
                        half = seg(src[:, :], 1 if kind == Q else 0)
                        act.activation(r3(e[:, j], P), half, ACT.Exp)
                        act.activation(r3((sq if kind == Q else sk)[:, j], P), half, ACT.Relu)
                    act.activation(dst, src[:, :], ACT.Copy).then_inc(hi_done, 1)

            for kind in (Q, K, V):
                project(0, kind)

            def step(g, c, nxt):
                for h in range(2):
                    act.wait_ge(nb_done, 2 * g + h + 1)
                    for t in range(CT):
                        ins = act.activation(prob[:, h, t, :], prob[:, h, t, :], ACT.Exp,
                                             bias=nb[:, h, t:t + 1], scale=ATT_SCALE,
                                             accum_out=rs[:, h, t:t + 1])
                    ins.then_inc(exp_done, 1)
                act.wait_ge(skt_done, g + 1)
                act.activation(skp[0][:, :, :], r3(ad_ps[0][:, :], P), ACT.Copy).then_inc(skt_hi, 1)
                if nxt:
                    project(g + 1, Q)
                    project(g + 1, K)
                for h in range(2):
                    act.wait_ge(pt_done, 2 * g + h + 1)
                    act.activation(probT[0][:, h], s_ps[h][:, :], ACT.Copy).then_inc(pt_hi, 1)
                for h in range(2):
                    act.wait_ge(mem_done, 2 * g + h + 1)
                    act.activation(mem[0][:, h], mem_ps[h][:, :], ACT.Copy).then_inc(mem_hi, 1)
                for h in range(2):
                    act.wait_ge(ad_done, 2 * g + h + 1)
                    if not (isinstance(g, int) and g == 0):
                        act.wait_ge(att_stored, 16 * g)
                    act.wait_ge(gate_ready, pair_of[0] + 2)
                    act.activation(att[:, h], ad_ps[h][:, :], ACT.Copy,
                                   scale=gate_p[:, h, 1:2]).then_inc(ad_read, 1)
                if nxt:
                    project(g + 1, V)

            pair_of = [0]
            step(0, 0, True)
            with act.Fori(0, PAIRS - 1) as p:
                for c in range(1, CHUNKS + 1):
                    pair_of[0] = p + c // CHUNKS
                    step(CHUNKS * p + c, c % CHUNKS, True)
            pair_of[0] = PAIRS - 1
            for g in range(STEPS - CHUNKS + 1, STEPS):
                step(g, g % CHUNKS, g < STEPS - 1)

        @block.vector
        def _(dve):
            dve.wait_ge(beta_step, 1)
            dve.tensor_scalar(beta_e[:, :], beta_e[:, :], 1.0, None, ALU.add).then_inc(beta_step, 1)
            dve.wait_ge(beta_step, 2)
            dve.reciprocal(gate[:, :, 0], beta_e[:, :]).then_inc(beta_step, 1)
            dve.wait_ge(beta_step, 3)
            dve.tensor_scalar(gate[:, :, 1], gate[:, :, 0], -1.0, 1.0, ALU.mult,
                              ALU.add).then_inc(gate_ready, 1)

            def project(gc, kind):
                for j in range(2):
                    dst = (qT, kT, v)[kind // 2]
                    dst = [x[:, j] if kind != V else x[:, 2 * j:2 * j + 2, :].rearrange("p a n -> p (a n)")
                           for x in dst]
                    dve.wait_ge(hi_done, fill(gc, kind, j) + 1)
                    dve.tensor_tensor(dst[1], bank[j][:, :], dst[0].bitcast(F32),
                                      ALU.subtract).then_inc(freed, 1)
                    if kind != V:
                        s = sq if kind == Q else sk
                        dve.scalar_tensor_tensor(out=s[:, j], in0=e[:, j], scalar=1.0, in1=s[:, j],
                                                 op0=ALU.min, op1=ALU.add).then_inc(sig_done, 1)

            for kind in (Q, K, V):
                project(0, kind)

            def step(g, c, nxt):
                for h in range(2):
                    dve.wait_ge(s_done, 2 * g + h + 1)
                    alone(dve, lone["dve"])
                    for t in range(CT):
                        ins = dve.tensor_tensor_reduce(prob[:, h, t, :], s_ps[h][:, t * P:(t + 1) * P],
                                                       mask[:, :], 1.0, -3e38, ALU.add, ALU.max,
                                                       mx[:, h, t:t + 1])
                    ins.then_inc(max_done, 1)
                    dve.wait_ge(max_done, 2 * g + h + 1)
                    dve.tensor_scalar(nb[:, h, :], mx[:, h, :], -ATT_SCALE, None,
                                      ALU.mult).then_inc(nb_done, 1)
                dve.wait_ge(skt_hi, g + 1)
                dve.tensor_tensor(skp[1][:, :, :], r3(ad_ps[0][:, :], P), skp[0][:, :, :].bitcast(F32),
                                  ALU.subtract).then_inc(sk_ready, 1)
                for h in range(2):
                    dve.wait_ge(exp_done, 2 * g + h + 1)
                    dve.reciprocal(rr[:, h, :], rs[:, h, :]).then_inc(rr_done, 1)
                if nxt:
                    project(g + 1, Q)
                    project(g + 1, K)
                for h in range(2):
                    dve.wait_ge(pt_hi, 2 * g + h + 1)
                    dve.tensor_tensor(probT[1][:, h], s_ps[h][:, :], probT[0][:, h].bitcast(F32),
                                      ALU.subtract).then_inc(pt_ready, 1)
                for h in range(2):
                    dve.wait_ge(mem_hi, 2 * g + h + 1)
                    dve.tensor_tensor(mem[1][:, h], mem_ps[h][:, :], mem[0][:, h].bitcast(F32),
                                      ALU.subtract).then_inc(mem_ready, 1)
                for h in range(2):
                    dve.wait_ge(am_done, 2 * g + h + 1)
                    dve.reciprocal(rec[:, :], mem_ps[h][:, 256:512]).then_inc(rec_done, 1)
                    dve.wait_ge(rec_done, 2 * g + h + 1)
                    dve.tensor_tensor(amr[:, :], mem_ps[h][:, 0:256], rec[:, :],
                                      ALU.mult).then_inc(amr_done, 1)
                    dve.wait_ge(amr_done, 2 * g + h + 1)
                    dve.wait_ge(ad_read, 2 * g + h + 1)
                    half = seg(att[:, h], 1)
                    dve.scalar_tensor_tensor(out=half, in0=r3(amr[:, :], P), scalar=gate_p[:, h, 0:1],
                                             in1=half, op0=ALU.mult, op1=ALU.add).then_inc(att_done, 1)
                if nxt:
                    project(g + 1, V)

            dve.wait_ge(consts_loaded, 48)
            over_steps(dve, step)

        @block.tensor
        def _(pe):
            pe.wait_ge(ones_ready, 3)

            def project(gc, kind, p):
                c = project_chunk[0]
                n = "qkv"[kind // 2]
                for j in range(2):
                    f = fill(gc, kind, j)
                    if not (isinstance(f, int) and f < 2):
                        pe.wait_ge(freed, f - 1)
                    if j == 0:
                        pe.wait_ge(w_split[n], p + 1)
                    if kind == V:
                        for i in range(2):
                            t = 2 * j + i
                            tok = slice(c * CHUNK + t * P, c * CHUNK + (t + 1) * P)
                            for k in range(KD):
                                mm = mm3(pe, bank[j][:, i * 256:(i + 1) * 256],
                                         both(xT, slice(None), k, tok), both(w[n], slice(None), k),
                                         k == 0, k == KD - 1)
                    else:
                        for k in range(KD):
                            mm = mm3(pe, bank[j][:, :],
                                     both(w[n], slice(None), k, slice(j * P, (j + 1) * P)),
                                     both(xT, slice(None), k, slice(c * CHUNK, (c + 1) * CHUNK)),
                                     k == 0, k == KD - 1)
                    mm.then_inc(filled, 1)

            project_chunk = [0]
            for kind in (Q, K, V):
                project(0, kind, 0)

            def step(g, c, nxt, p_next):
                start = isinstance(g, int) and g == 0
                pe.wait_ge(freed, fill(g, V, 0))
                if not start:
                    pe.wait_ge(pt_ready, 2 * g)
                for h in range(2):
                    for t in range(CT):
                        tok = slice(t * P, (t + 1) * P)
                        mm = mm3(pe, s_ps[h][:, tok], both(qT, slice(None), h, tok),
                                 both(kT, slice(None), h, tok))
                    mm.then_inc(s_done, 1)
                pe.wait_ge(sig_done, 4 * g + 4)
                if not start:
                    pe.wait_ge(ad_read, 2 * g - 1)
                for h in range(2):
                    for b in range(2):
                        i = 2 * h + b
                        mm = pe.transpose(ad_ps[0][:, i * P:(i + 1) * P], sk[:, h, b * P:(b + 1) * P], ident[:, :])
                mm.then_inc(skt_done, 1)
                project_chunk[0] = (c + 1) % CHUNKS
                if nxt:
                    project(g + 1, Q, p_next)
                    project(g + 1, K, p_next)
                for h in range(2):
                    pe.wait_ge(p_ready, 2 * g + h + 1)
                    for t in range(CT):
                        mm = pe.transpose(s_ps[h][:, t * P:(t + 1) * P], prob[:, h, t, :], ident[:, :])
                    mm.then_inc(pt_done, 1)
                pe.wait_ge(sk_ready, g + 1)
                for h in range(2):
                    if not start:
                        pe.wait_ge(att_done, 2 * g - 1 + h)
                    for b in range(2):
                        s = both(skp, slice(None), 2 * h + b)
                        out = mem_ps[h][:, b * 256:b * 256 + P]
                        mm3(pe, out, s, both(v, slice(None), 2 * b, slice(h * P, (h + 1) * P)))
                        out = mem_ps[h][:, b * 256 + P:(b + 1) * 256]
                        pe.matmul(out, s[0], ones_r[:, :], start=True, stop=False)
                        pe.matmul(out, s[1], ones_r[:, :], start=False, stop=False)
                        mm = pe.matmul(out, ones_r[:, :], z_start[:, :], start=False, stop=True)
                    mm.then_inc(mem_done, 1)
                for h in range(2):
                    pe.wait_ge(pt_ready, 2 * g + h + 1)
                    if not start:
                        pe.wait_ge(ad_read, 2 * g - 1 + h)
                    for t in range(CT):
                        tok = slice(t * P, (t + 1) * P)
                        mm = mm3(pe, ad_ps[h][:, tok], both(v, slice(None), t, slice(h * P, (h + 1) * P)),
                                 both(probT, slice(None), h, tok))
                    mm.then_inc(ad_done, 1)
                pe.wait_ge(sq_ready, g + 1)
                for h in range(2):
                    pe.wait_ge(mem_ready, 2 * g + h + 1)
                    for b in range(2):
                        q_b = both(sqp[c % 2], slice(None), h, slice(b * P, (b + 1) * P))
                        mm3(pe, mem_ps[h][:, b * P:(b + 1) * P],
                            both(mem, slice(None), h, slice(b * 256, b * 256 + P)), q_b)
                        mm = mm3(pe, mem_ps[h][:, 256 + b * P:256 + (b + 1) * P],
                                 both(mem, slice(None), h, slice(b * 256 + P, (b + 1) * 256)), q_b)
                    mm.then_inc(am_done, 1)
                if nxt:
                    project(g + 1, V, p_next)

            step(0, 0, True, 0)
            with pe.Fori(0, PAIRS - 1) as p:
                for c in range(1, CHUNKS + 1):
                    step(CHUNKS * p + c, c % CHUNKS, True, p + (c + 1) // CHUNKS)
            for g in range(STEPS - CHUNKS + 1, STEPS):
                step(g, g % CHUNKS, g < STEPS - 1, PAIRS - 1)


QC = 2


def attention_output(nc, X, d, ident, attT, x1, qc):
    J = HEADS
    ROWS = P // J
    with ExitStack() as ctx:
        def sb(name, shape, dt=F32):
            return ctx.enter_context(nc.sbuf_tensor("o_" + name, shape, dt))

        def sem(name):
            return ctx.enter_context(nc.semaphore("o_" + name))

        wo = [sb("wo_" + n, [P, J, D], F32R) for n in ("hi", "lo")]
        raw = [sb(f"raw{i}", [P, TOKENS]) for i in range(2)]
        head = [[sb(f"head{i}_{n}", [P, J, P], F32R) for n in ("hi", "lo")] for i in range(2)]
        xrow = [sb(f"xrow{i}", [P, D]) for i in range(2)]
        row = [sb(f"row{i}", [P, D]) for i in range(2)]
        wq_raw = sb("wq_raw", [P, KD, QC * P])
        wq = [sb("wq_" + n, [P, KD, QC * P], F32R) for n in ("hi", "lo")]
        st, mv = sb("st", [P, 6]), sb("mv", [P, 2])
        var_eps, std, rstd, newton = (sb(n, [P, 1]) for n in ("var_eps", "std", "rstd", "newton"))
        xn = [sb(f"xn{i}", [P, D]) for i in range(2)]
        xs = [sb("xs_" + n, [P, KD, J, 2, ROWS], F32R) for n in ("hi", "lo")]

        def psum(name):
            return ctx.enter_context(nc.psum_tensor("o_" + name, [P, D], F32))

        ps = [psum(f"ps{i}") for i in range(2)]
        t_ps = [psum(f"t_ps{i}") for i in range(2)]
        q_ps = psum("q_ps")
        wq_loaded, wq_hi, wq_split = sem("wq_loaded"), sem("wq_hi"), sem("wq_split")
        small, var_ready, std_ready = sem("small"), sem("var_ready"), sem("std_ready")
        newton_done = sem("newton_done")
        xn_ready, turned, xs_hi, xs_ready = sem("xn_ready"), sem("turned"), sem("xs_hi"), sem("xs_ready")
        q_done, q_hi, q_ready = sem("q_done"), sem("q_hi"), sem("q_ready")
        lone = {n: sem("lone_" + n) for n in ("act", "dve")}
        head_loaded = [sem(f"head_loaded{i}") for i in range(2)]
        x_loaded = [sem(f"x_loaded{i}") for i in range(2)]
        head_hi = sem("head_hi")
        head_split = sem("head_split")
        wo_hi = sem("wo_hi")
        wo_split = sem("wo_split")
        product = sem("product")
        row_ready = sem("row_ready")
        row_stored = [sem(f"row_stored{i}") for i in range(2)]
        block = ctx.enter_context(nc.Block())

        def columns(part, p):
            return (qc[part][:, :, :].rearrange("l k (t m) -> l k t m", m=P)
                    [:, :, :, bass.ds(2 * ROWS * p, 2 * ROWS)])

        def of_head(x, i):
            return x[:, :, :, i, :]

        heads = attT.rearrange("(p c) d h t -> p h d c t", c=CHUNKS)
        x_rows = d["x"].rearrange("(t h s) n -> h t s n", h=HEADS, s=ROWS)
        x1_rows = x1.rearrange("(t h s) n -> h t s n", h=HEADS, s=ROWS)

        @block.sync
        def _(sp):
            def load(p, i):
                sp.dma_start(r3(raw[i][:, :], CHUNK), heads[p, i]).then_inc(head_loaded[i], 16)

            def load_x(p, i):
                sp.dma_start(xrow[i][:, :], x_rows[2 * p + i]).then_inc(x_loaded[i], 16)

            def store(p, i):
                sp.wait_ge(row_ready, 2 * p + i + 1)
                sp.dma_start(x1_rows[2 * p + i], row[i][:, :]).then_inc(row_stored[i], 16)

            for i in range(2):
                load(0, i)
                load_x(0, i)
            sp.dma_start(wq_raw[:, :, :], d["wdq"]).then_inc(wq_loaded, 16)
            with sp.Fori(0, HEADS // 2 - 1) as p:
                for i in range(2):
                    sp.wait_ge(head_split, 2 * p + i + 1)
                    load(p + 1, i)
                    store(p, i)
                    load_x(p + 1, i)
            for i in range(2):
                store(HEADS // 2 - 1, i)
            for i in range(2):
                sp.wait_ge(row_stored[i], 16 * HEADS // 2)

        @block.scalar
        def _(act):
            def head_part(h, i, p):
                act.wait_ge(head_loaded[i], 16 * (p + 1))
                if not (isinstance(p, int) and p == 0):
                    act.wait_ge(product, h - 1)
                act.activation(head[i][0][:, :, :], raw[i][:, :].rearrange("d (m j) -> d j m", j=J),
                               ACT.Copy).then_inc(head_hi, 1)

            def root(h):
                act.wait_ge(var_ready, h + 1)
                act.activation(std[:, :], var_eps[:, :], ACT.Sqrt).then_inc(std_ready, 1)

            def turned_part(h, i):
                act.wait_ge(turned, h + 1)
                act.activation(of_head(xs[0], i), t_ps[i][:, :].rearrange("f (k t s) -> f k t s", k=KD, t=J),
                               ACT.Copy).then_inc(xs_hi, 1)

            def latent(p):
                act.wait_ge(q_done, p + 1)
                alone(act, lone["act"])
                act.activation(columns(0, p), q_ps[:, :].rearrange("l (k t m) -> l k t m", k=QC, t=J),
                               ACT.Copy).then_inc(q_hi, 1)

            head_part(0, 0, 0)
            for j in range(J):
                act.activation(wo[0][:, j, :], X[:, j, :], ACT.Copy).then_inc(wo_hi, 1)
            head_part(1, 1, 0)
            act.wait_ge(wq_loaded, 16)
            act.activation(wq[0][:, :, :], wq_raw[:, :, :], ACT.Copy).then_inc(wq_hi, 1)
            root(0)
            head_part(2, 0, 1)
            root(1)
            turned_part(0, 0)
            head_part(3, 1, 1)
            with act.Fori(1, PAIRS - 1) as p:
                root(2 * p)
                turned_part(2 * p - 1, 1)
                head_part(2 * p + 2, 0, p + 1)
                root(2 * p + 1)
                latent(p - 1)
                turned_part(2 * p, 0)
                head_part(2 * p + 3, 1, p + 1)
            root(HEADS - 2)
            turned_part(HEADS - 3, 1)
            root(HEADS - 1)
            latent(PAIRS - 2)
            turned_part(HEADS - 2, 0)
            turned_part(HEADS - 1, 1)
            latent(PAIRS - 1)

        @block.vector
        def _(dve):
            def head_part(h, i):
                dve.wait_ge(head_hi, h + 1)
                dve.tensor_tensor(head[i][1][:, :, :], raw[i][:, :].rearrange("d (m j) -> d j m", j=J),
                                  head[i][0][:, :, :].bitcast(F32), ALU.subtract).then_inc(head_split, 1)

            def finish(h, i, p):
                dve.wait_ge(product, h + 1)
                dve.wait_ge(x_loaded[i], 16 * (p + 1))
                if not (isinstance(p, int) and p == 0):
                    dve.wait_ge(row_stored[i], 16 * p)
                dve.tensor_tensor(row[i][:, :], ps[i][:, :], xrow[i][:, :], ALU.add).then_inc(row_ready, 1)
                dve.wait_ge(row_ready, h + 1)
                alone(dve, lone["dve"])
                dve.bn_stats(st[:, :], row[i][:, :]).then_inc(small, 1)
                dve.wait_ge(small, 5 * h + 1)
                alone(dve, lone["dve"])
                dve.bn_aggr(mv[:, :], st[:, :]).then_inc(small, 1)
                dve.wait_ge(small, 5 * h + 2)
                dve.tensor_scalar(var_eps[:, :], mv[:, 1:2], EPS, None, ALU.add).then_inc(var_ready, 1)

            def normalize(h, i):
                dve.wait_ge(std_ready, h + 1)
                dve.reciprocal(rstd[:, :], std[:, :]).then_inc(small, 1)
                dve.wait_ge(small, 5 * h + 3)
                dve.tensor_scalar(newton[:, :], rstd[:, :], rstd[:, 0:1], var_eps[:, 0:1], ALU.mult,
                                  ALU.mult).then_inc(small, 1)
                dve.wait_ge(small, 5 * h + 4)
                dve.tensor_scalar(std[:, :], newton[:, :], -0.5, 1.5, ALU.mult, ALU.add).then_inc(small, 1)
                dve.wait_ge(small, 5 * h + 5)
                dve.tensor_scalar(newton[:, :], rstd[:, :], std[:, 0:1], None, ALU.mult).then_inc(newton_done, 1)
                dve.wait_ge(newton_done, h + 1)
                dve.tensor_scalar(xn[i][:, :], row[i][:, :], mv[:, 0:1], newton[:, 0:1], ALU.subtract,
                                  ALU.mult).then_inc(xn_ready, 1)

            def turned_part(h, i):
                dve.wait_ge(xs_hi, h + 1)
                dve.tensor_tensor(of_head(xs[1], i), t_ps[i][:, :].rearrange("f (k t s) -> f k t s", k=KD, t=J),
                                  of_head(xs[0], i).bitcast(F32), ALU.subtract).then_inc(xs_ready, 1)

            def latent(p):
                dve.wait_ge(q_hi, p + 1)
                dve.tensor_tensor(columns(1, p), q_ps[:, :].rearrange("l (k t m) -> l k t m", k=QC, t=J),
                                  columns(0, p).bitcast(F32), ALU.subtract).then_inc(q_ready, 1)

            head_part(0, 0)
            for j in range(J):
                dve.wait_ge(wo_hi, j + 1)
                dve.tensor_tensor(wo[1][:, j, :], X[:, j, :], wo[0][:, j, :].bitcast(F32),
                                  ALU.subtract).then_inc(wo_split, 1)
            head_part(1, 1)
            dve.wait_ge(wq_hi, 1)
            dve.tensor_tensor(wq[1][:, :, :], wq_raw[:, :, :], wq[0][:, :, :].bitcast(F32),
                              ALU.subtract).then_inc(wq_split, 1)
            finish(0, 0, 0)
            normalize(0, 0)
            head_part(2, 0)
            finish(1, 1, 0)
            turned_part(0, 0)
            normalize(1, 1)
            head_part(3, 1)
            with dve.Fori(1, PAIRS - 1) as p:
                finish(2 * p, 0, p)
                turned_part(2 * p - 1, 1)
                normalize(2 * p, 0)
                head_part(2 * p + 2, 0)
                finish(2 * p + 1, 1, p)
                latent(p - 1)
                turned_part(2 * p, 0)
                normalize(2 * p + 1, 1)
                head_part(2 * p + 3, 1)
            finish(HEADS - 2, 0, PAIRS - 1)
            turned_part(HEADS - 3, 1)
            normalize(HEADS - 2, 0)
            finish(HEADS - 1, 1, PAIRS - 1)
            latent(PAIRS - 2)
            turned_part(HEADS - 2, 0)
            normalize(HEADS - 1, 1)
            turned_part(HEADS - 1, 1)
            latent(PAIRS - 1)

        @block.tensor
        def _(pe):
            def multiply(h, i):
                pe.wait_ge(head_split, h + 1)
                if not (isinstance(h, int) and h < 2):
                    pe.wait_ge(row_ready, h - 1)
                for j in range(J):
                    if isinstance(h, int) and h == 0:
                        pe.wait_ge(wo_split, j + 1)
                    mm = mm3(pe, ps[i][:, :], (head[i][0][:, j, :], head[i][1][:, j, :]),
                             (wo[0][:, j, :], wo[1][:, j, :]), j == 0, j == J - 1)
                mm.then_inc(product, 1)

            def turn(h, i):
                pe.wait_ge(xn_ready, h + 1)
                if not (isinstance(h, int) and h < 2):
                    pe.wait_ge(xs_ready, h - 1)
                for k in range(KD):
                    mm = pe.transpose(t_ps[i][:, k * P:(k + 1) * P], xn[i][:, k * P:(k + 1) * P], ident[:, :])
                mm.then_inc(turned, 1)

            def latent(p):
                pe.wait_ge(wq_split, 1)
                pe.wait_ge(xs_ready, 2 * p + 2)
                if not (isinstance(p, int) and p == 0):
                    pe.wait_ge(q_ready, p)
                for j in range(QC):
                    for k in range(KD):
                        mm = mm3(pe, q_ps[:, j * 256:(j + 1) * 256], [w[:, k, j * P:(j + 1) * P] for w in wq],
                                 [x[:, k, :, :, :].rearrange("f t h s -> f (t h s)") for x in xs],
                                 k == 0, k == KD - 1)
                mm.then_inc(q_done, 1)

            multiply(0, 0)
            multiply(1, 1)
            turn(0, 0)
            multiply(2, 0)
            turn(1, 1)
            multiply(3, 1)
            latent(0)
            turn(2, 0)
            with pe.Fori(2, PAIRS) as p:
                multiply(2 * p, 0)
                turn(2 * p - 1, 1)
                multiply(2 * p + 1, 1)
                latent(p - 1)
                turn(2 * p, 0)
            turn(HEADS - 1, 1)
            latent(PAIRS - 1)


KEYS = 256
SEQS = TOKENS // KEYS
LOOKBACK = 8
X_SCALE = float(np.float32(1.0) / np.sqrt(np.float32(192.0)))


def latents(nc, d, T, X, x1):
    with ExitStack() as ctx:
        def sb(name, shape, dt=F32):
            return ctx.enter_context(nc.sbuf_tensor("k_" + name, shape, dt))

        def sem(name):
            return ctx.enter_context(nc.semaphore("k_" + name))

        w_raw = sb("w_raw", [P, KD + 1, P])
        w = [sb("w_" + n, [P, KD + 1, P], F32R) for n in ("hi", "lo")]
        raw = [sb(f"raw{i}", [P, KD, CHUNK]) for i in range(2)]
        cT = [[sb(f"c{i}_{n}", [P, KD, CHUNK], F32R) for n in ("hi", "lo")] for i in range(2)]
        kvf = sb("kvf", [P, CHUNK])
        rot = sb("rot", [P, CHUNK])
        rot_swap = sb("rot_swap", [P, CHUNK])
        kr = sb("kr", [P, CHUNK])
        kio = sb("kio", [P, KEYS])
        ids_i = sb("ids_i", [P, TILES], I32)
        ids = sb("ids", [P, TILES])
        ids_low = sb("ids_low", [P, TILES])
        above = sb("above", [P, KEYS])
        below = sb("below", [P, KEYS])
        rows_of = sb("rows_of", [P, 2])
        kv_ps, tok_ps, kr_ps = ([ctx.enter_context(nc.psum_tensor(f"k_{n}{i}", [P, 512], F32)) for i in range(2)]
                                for n in ("kv", "tok", "kr"))
        w_loaded = sem("w_loaded")
        small_loaded = sem("small_loaded")
        raw_loaded = [sem(f"raw_loaded{i}") for i in range(2)]
        w_hi = sem("w_hi")
        w_split = sem("w_split")
        c_hi = sem("c_hi")
        c_split = sem("c_split")
        kv_done = sem("kv_done")
        kv_hi = sem("kv_hi")
        kv_split = sem("kv_split")
        tok_done = sem("tok_done")
        tok_hi = sem("tok_hi")
        tok_split = sem("tok_split")
        kr_done = sem("kr_done")
        rot_done = sem("rot_done")
        kr_ready = sem("kr_ready")
        kr_hi = sem("kr_hi")
        kr_split = sem("kr_split")
        ids_step = sem("ids_step")
        mask_part = sem("mask_part")
        mask_done = sem("mask_done")
        block = ctx.enter_context(nc.Block())

        def cols(c):
            return slice(c * CHUNK, (c + 1) * CHUNK)

        @block.sync
        def _(sp):
            sp.dma_start(w_raw[:, :, :], d["wkv"]).then_inc(w_loaded, 16)
            for c in range(CHUNKS):
                if c >= 2:
                    sp.wait_ge(c_split, c - 1)
                sp.dma_start(raw[c % 2][:, :, :], d["ctxT"][c]).then_inc(raw_loaded[c % 2], 16)
                if c == 1:
                    sp.dma_start(T["cos"][:, :], d["cos"]).then_inc(small_loaded, 16)
                    sp.dma_start(T["sin"][:, :], d["sin"]).then_inc(small_loaded, 16)
                    sp.dma_start(kio[:, :], d["kio"]).then_inc(small_loaded, 16)
                    sp.dma_start(ids_i[:, :], d["ids"]).then_inc(small_loaded, 16)
                    sp.dma_start(rows_of[:, :], d["rows_of"]).then_inc(small_loaded, 16)
            sp.dma_start(X[:, :, :], x1.rearrange("(t p) n -> p t n", p=P)).then_inc(T["x1_loaded"], 16)

        @block.scalar
        def _(act):
            act.wait_ge(w_loaded, 16)
            act.activation(w[0][:, :, :], w_raw[:, :, :], ACT.Copy).then_inc(w_hi, 1)

            def context(c):
                act.wait_ge(raw_loaded[c % 2], 16 * (c // 2 + 1))
                if c >= 2:
                    act.wait_ge(kv_done, c - 1)
                act.activation(cT[c % 2][0][:, :, :], raw[c % 2][:, :, :], ACT.Copy).then_inc(c_hi, 1)

            context(0)
            act.wait_ge(small_loaded, 80)
            for c in range(CHUNKS):
                if c + 1 < CHUNKS:
                    context(c + 1)
                act.wait_ge(kv_done, c + 1)
                if c >= 1:
                    act.wait_ge(tok_done, c)
                act.activation(kvf[:, :], kv_ps[c % 2][:, :], ACT.Copy)
                act.activation(T["kvT"][0][:, cols(c)], kv_ps[c % 2][:, :], ACT.Copy).then_inc(kv_hi, 1)
                act.wait_ge(tok_done, c + 1)
                act.activation(T["kv"][0][:, c * CT:(c + 1) * CT, :], r3(tok_ps[c % 2][:, :], P),
                               ACT.Copy).then_inc(tok_hi, 1)
                act.wait_ge(kr_ready, c + 1)
                for h in range(2):
                    act.activation(T["kr"][0][:, 2 * c:2 * c + 2, h, :], r3(kr[:, :], KEYS), ACT.Copy,
                                   scale=rows_of[:, h:h + 1]).then_inc(kr_hi, 1)

        @block.vector
        def _(dve):
            dve.wait_ge(w_hi, 1)
            dve.tensor_tensor(w[1][:, :, :], w_raw[:, :, :], w[0][:, :, :].bitcast(F32),
                              ALU.subtract).then_inc(w_split, 1)

            def context(c):
                dve.wait_ge(c_hi, c + 1)
                dve.tensor_tensor(cT[c % 2][1][:, :, :], raw[c % 2][:, :, :],
                                  cT[c % 2][0][:, :, :].bitcast(F32), ALU.subtract).then_inc(c_split, 1)

            context(0)
            dve.wait_ge(small_loaded, 80)
            dve.tensor_copy(ids[:, :], ids_i[:, :]).then_inc(ids_step, 1)
            dve.wait_ge(ids_step, 1)
            dve.tensor_scalar(ids_low[:, :], ids[:, :], -float(LOOKBACK), None, ALU.add).then_inc(ids_step, 1)
            dve.wait_ge(ids_step, 2)

            def mask(t):
                if t:
                    dve.wait_ge(mask_done, t)
                dve.tensor_scalar(above[:, :], kio[:, :], ids[:, t:t + 1], NEG, ALU.is_gt, ALU.mult)
                dve.tensor_scalar(below[:, :], kio[:, :], ids_low[:, t:t + 1], NEG, ALU.is_lt,
                                  ALU.mult).then_inc(mask_part, 1)
                dve.wait_ge(mask_part, t + 1)
                dve.tensor_tensor(T["mask"][:, t, :], above[:, :], below[:, :], ALU.add).then_inc(mask_done, 1)

            for c in range(CHUNKS):
                if c + 1 < CHUNKS:
                    context(c + 1)
                dve.wait_ge(kv_hi, c + 1)
                dve.tensor_tensor(T["kvT"][1][:, cols(c)], kv_ps[c % 2][:, :],
                                  T["kvT"][0][:, cols(c)].bitcast(F32), ALU.subtract).then_inc(kv_split, 1)
                for t in range(c * CT, (c + 1) * CT):
                    mask(t)
                dve.wait_ge(tok_hi, c + 1)
                dve.tensor_tensor(T["kv"][1][:, c * CT:(c + 1) * CT, :], r3(tok_ps[c % 2][:, :], P),
                                  T["kv"][0][:, c * CT:(c + 1) * CT, :].bitcast(F32),
                                  ALU.subtract).then_inc(tok_split, 1)
                dve.wait_ge(kr_done, c + 1)
                rotate(dve, T, kr_ps[c % 2], rot, rot_swap).then_inc(rot_done, 1)
                dve.wait_ge(rot_done, c + 1)
                dve.tensor_tensor(kr[:, :], rot[:, :], rot_swap[:, :], ALU.add).then_inc(kr_ready, 1)
                for h in range(2):
                    dve.wait_ge(kr_hi, 2 * c + h + 1)
                    dve.scalar_tensor_tensor(
                        out=T["kr"][1][:, 2 * c:2 * c + 2, h, :], in0=r3(kr[:, :], KEYS),
                        scalar=rows_of[:, h:h + 1], in1=T["kr"][0][:, 2 * c:2 * c + 2, h, :].bitcast(F32),
                        op0=ALU.mult, op1=ALU.subtract).then_inc(kr_split, 1)

        @block.tensor
        def _(pe):
            pe.wait_ge(w_split, 1)
            for c in range(CHUNKS):
                pe.wait_ge(c_split, c + 1)
                if c >= 2:
                    pe.wait_ge(kv_split, c - 1)
                for k in range(KD):
                    mm = mm3(pe, kv_ps[c % 2][:, :], (w[0][:, k, :], w[1][:, k, :]),
                             (cT[c % 2][0][:, k, :], cT[c % 2][1][:, k, :]), k == 0, k == KD - 1)
                mm.then_inc(kv_done, 1)
                pe.wait_ge(kv_hi, c + 1)
                if c >= 2:
                    pe.wait_ge(tok_split, c - 1)
                for t in range(CT):
                    mm = pe.transpose(tok_ps[c % 2][:, t * P:(t + 1) * P], kvf[:, t * P:(t + 1) * P],
                                      T["ident"][:, :])
                mm.then_inc(tok_done, 1)
                pe.wait_ge(kv_split, c + 1)
                if c >= 2:
                    pe.wait_ge(rot_done, c - 1)
                mm3(pe, kr_ps[c % 2][:, :], (w[0][:, KD, :], w[1][:, KD, :]),
                    (T["kvT"][0][:, cols(c)], T["kvT"][1][:, cols(c)])).then_inc(kr_done, 1)


def rotate(dve, T, ps, rot, rot_swap):
    def table(name, rows):
        return T[name][rows, :].unsqueeze(1).to_broadcast([rows.stop - rows.start, 2, KEYS])

    H = P // 2
    dve.tensor_tensor(r3(rot[:, :], KEYS), r3(ps[:, :], KEYS), table("cos", slice(0, P)), ALU.mult)
    dve.tensor_tensor(r3(rot_swap[0:H, :], KEYS), r3(ps[H:P, :], KEYS), table("sin", slice(0, H)), ALU.mult)
    return dve.tensor_tensor(r3(rot_swap[H:P, :], KEYS), r3(ps[0:H, :], KEYS), table("sin", slice(H, P)),
                             ALU.mult)


def cross_attention(nc, X, d, T):
    with ExitStack() as ctx:
        def sb(name, shape, dt=F32):
            return ctx.enter_context(nc.sbuf_tensor("x_" + name, shape, dt))

        def parts(name, shape):
            return sb(name + "_hi", shape, F32R), sb(name + "_lo", shape, F32R)

        def sem(name):
            return ctx.enter_context(nc.semaphore("x_" + name))

        def psum(name):
            return ctx.enter_context(nc.psum_tensor("x_" + name, [P, 512], F32))

        def both(pair, *index):
            return pair[0][index], pair[1][index]

        ALL = slice(None)
        UQ, UK, UV, WO = 0, 256, 384, 512
        raw = sb("raw", [P, 2, WO + D])
        raw_r = sb("raw_r", [P, QC, P])
        wa = parts("wa", [P, 2, QC, P])
        wb = parts("wb", [P, 2, D])
        wr = parts("wr", [P, QC, P])
        qa = parts("qa", [P, 2, CHUNK])
        qr = parts("qr", [P, CHUNK])
        rot = sb("rot", [P, CHUNK])
        rot_swap = sb("rot_swap", [P, CHUNK])
        prob = sb("prob", [P, CT, 2, KEYS])
        probT = parts("probT", [P, 4, 512])
        ao = parts("ao", [P, 2, 512])
        mx = sb("mx", [P, CT, 2])
        nb = sb("nb", [P, CT, 2])
        rs = sb("rs", [P, CT, 2])
        rr = sb("rr", [P, CT, 2])
        bank = [psum("bank0"), psum("bank1")]
        s_ps = [psum("s0"), psum("s1")]
        pt_ps = [psum("pt0"), psum("pt1")]
        av_ps = [psum("av0"), psum("av1")]

        raw_loaded = sem("raw_loaded")
        raw_r_loaded = sem("raw_r_loaded")
        wr_hi, wr_split = sem("wr_hi"), sem("wr_split")
        a_done, a_hi, a_split = sem("a_done"), sem("a_hi"), sem("a_split")
        b_done, b_hi, b_split = sem("b_done"), sem("b_hi"), sem("b_split")
        qa_done, qa_hi, qa_split = sem("qa_done"), sem("qa_hi"), sem("qa_split")
        qr_done, rot_done, rot_sum = sem("qr_done"), sem("rot_done"), sem("rot_sum")
        qr_hi, qr_ready = sem("qr_hi"), sem("qr_ready")
        s_done, max_done, nb_done = sem("s_done"), sem("max_done"), sem("nb_done")
        exp_done, rr_done, p_ready = sem("exp_done"), sem("rr_done"), sem("p_ready")
        pt_done, pt_hi, pt_ready = sem("pt_done"), sem("pt_hi"), sem("pt_ready")
        av_done, av_hi, av_ready = sem("av_done"), sem("av_hi"), sem("av_ready")
        out_done, out_added = sem("out_done"), sem("out_added")
        lone = {n: sem("lone_" + n) for n in ("act", "dve", "pool")}
        block = ctx.enter_context(nc.Block())

        def over_steps(eng, step):
            step(0, 0, 0, True)
            with eng.Fori(0, PAIRS - 1) as p:
                for c in range(1, CHUNKS + 1):
                    step(CHUNKS * p + c, p + c // CHUNKS, c % CHUNKS, True)
            for g in range(STEPS - CHUNKS + 1, STEPS):
                step(g, PAIRS - 1, g % CHUNKS, g < STEPS - 1)

        def is_at(g, value):
            return isinstance(g, int) and g == value

        def folds_a(p, c):
            return c == 2 and not is_at(p, PAIRS - 1)

        @block.sync
        def _(sp):
            sp.dma_start(raw[:, :, :], d["xw"][0]).then_inc(raw_loaded, 16)
            sp.dma_start(raw_r[:, :, :], d["xwr"][0]).then_inc(raw_r_loaded, 16)
            with sp.Fori(0, PAIRS - 1) as p:
                sp.wait_ge(wr_split, p + 1)
                sp.dma_start(raw_r[:, :, :], d["xwr"][p + 1]).then_inc(raw_r_loaded, 16)
                sp.wait_ge(b_done, 2 * p + 2)
                sp.dma_start(raw[:, :, :], d["xw"][p + 1]).then_inc(raw_loaded, 16)

        @block.gpsimd
        def _(pool):
            def split_wr(p):
                pool.wait_ge(raw_r_loaded, 16 * (p + 1))
                alone(pool, lone["pool"])
                pool.tensor_copy(wr[0][:, :, :], raw_r[:, :, :]).then_inc(wr_hi, 1)
                pool.wait_ge(wr_hi, p + 1)
                pool.tensor_tensor(wr[1][:, :, :], raw_r[:, :, :], wr[0][:, :, :].bitcast(F32),
                                   ALU.subtract).then_inc(wr_split, 1)

            def rotary(gc):
                pool.wait_ge(rot_done, gc + 1)
                pool.tensor_tensor(rot[:, :], rot[:, :], rot_swap[:, :], ALU.add).then_inc(rot_sum, 1)
                pool.wait_ge(qr_hi, gc + 1)
                pool.tensor_tensor(qr[1][:, :], rot[:, :], qr[0][:, :].bitcast(F32),
                                   ALU.subtract).then_inc(qr_ready, 1)

            def step(g, p, c, nxt):
                for t in range(CT):
                    pool.wait_ge(rr_done, 4 * g + t + 1)
                    pool.tensor_tensor(prob[:, t], prob[:, t],
                                       rr[:, t, :].unsqueeze(2).to_broadcast([P, 2, KEYS]),
                                       ALU.mult).then_inc(p_ready, 1)
                if nxt:
                    rotary(g + 1)
                if folds_a(p, c):
                    split_wr(p + 1)

            split_wr(0)
            rotary(0)
            over_steps(pool, step)

        @block.scalar
        def _(act):
            def fold_a(p):
                act.wait_ge(a_done, p + 1)
                act.activation(wa[0][:, :, :, :].rearrange("p h k n -> p (h k n)"), av_ps[1][:, :],
                               ACT.Copy).then_inc(a_hi, 1)

            def queries(gc):
                for h in range(2):
                    act.wait_ge(qa_done, 2 * gc + h + 1)
                    act.activation(qa[0][:, h], bank[h][:, :], ACT.Copy).then_inc(qa_hi, 1)

            def rotary(gc):
                act.wait_ge(rot_sum, gc + 1)
                act.activation(qr[0][:, :], rot[:, :], ACT.Copy).then_inc(qr_hi, 1)

            def step(g, p, c, nxt):
                for t in range(CT):
                    act.wait_ge(nb_done, 4 * g + t + 1)
                    for h in range(2):
                        ins = act.activation(prob[:, t, h, :], prob[:, t, h, :], ACT.Exp,
                                             bias=nb[:, t, h:h + 1], scale=X_SCALE,
                                             accum_out=rs[:, t, h:h + 1])
                    ins.then_inc(exp_done, 1)
                if nxt:
                    queries(g + 1)
                if folds_a(p, c):
                    fold_a(p + 1)
                for i in range(4):
                    act.wait_ge(pt_done, 4 * g + i + 1)
                    act.activation(probT[0][:, i], pt_ps[i % 2][:, :], ACT.Copy).then_inc(pt_hi, 1)
                    if i == 1 and nxt:
                        rotary(g + 1)
                for b in range(2):
                    act.wait_ge(av_done, 2 * g + b + 1)
                    act.activation(ao[0][:, b], av_ps[b][:, :], ACT.Copy).then_inc(av_hi, 1)
                if c == 0:
                    for h in range(2):
                        act.wait_ge(b_done, 2 * p + h + 1)
                        act.activation(wb[0][:, h], bank[h][:, :], ACT.Copy).then_inc(b_hi, 1)

            fold_a(0)
            queries(0)
            rotary(0)
            over_steps(act, step)

        @block.vector
        def _(dve):
            def fold_a(p):
                dve.wait_ge(a_hi, p + 1)
                dve.tensor_tensor(wa[1][:, :, :, :].rearrange("p h k n -> p (h k n)"), av_ps[1][:, :],
                                  wa[0][:, :, :, :].rearrange("p h k n -> p (h k n)").bitcast(F32),
                                  ALU.subtract).then_inc(a_split, 1)

            def queries(gc):
                for h in range(2):
                    dve.wait_ge(qa_hi, 2 * gc + h + 1)
                    dve.tensor_tensor(qa[1][:, h], bank[h][:, :], qa[0][:, h].bitcast(F32),
                                      ALU.subtract).then_inc(qa_split, 1)

            def rotary(gc):
                dve.wait_ge(qr_done, gc + 1)
                if not is_at(gc, 0):
                    dve.wait_ge(qr_ready, gc)
                rotate(dve, T, av_ps[0], rot, rot_swap).then_inc(rot_done, 1)

            def reciprocal(g, t):
                dve.wait_ge(exp_done, 4 * g + t + 1)
                dve.reciprocal(rr[:, t, :], rs[:, t, :]).then_inc(rr_done, 1)

            def output(m, c, tiles):
                for j in tiles:
                    dve.wait_ge(out_done, 4 * m + j + 1)
                    dve.tensor_tensor(X[:, c * CT + j, :], bank[j % 2][:, :], X[:, c * CT + j, :],
                                      ALU.add).then_inc(out_added, 1)

            def step(g, p, c, nxt):
                before = (c - 1) % CHUNKS
                for t in range(CT):
                    dve.wait_ge(s_done, 4 * g + t + 1)
                    alone(dve, lone["dve"])
                    for h in range(2):
                        ins = dve.tensor_tensor_reduce(prob[:, t, h, :], s_ps[t % 2][:, h * KEYS:(h + 1) * KEYS],
                                                       T["mask"][:, c * CT + t, :], 1.0, -3e38, ALU.add,
                                                       ALU.max, mx[:, t, h:h + 1])
                    ins.then_inc(max_done, 1)
                    dve.wait_ge(max_done, 4 * g + t + 1)
                    dve.tensor_scalar(nb[:, t, :], mx[:, t, :], -X_SCALE, None, ALU.mult).then_inc(nb_done, 1)
                    if t:
                        reciprocal(g, t - 1)
                reciprocal(g, CT - 1)
                if nxt:
                    queries(g + 1)
                if folds_a(p, c):
                    fold_a(p + 1)
                if nxt:
                    rotary(g + 1)
                for b in range(2):
                    if not is_at(g, 0):
                        output(g - 1, before, ((0, 1), (2,))[b])
                    for i in (2 * b, 2 * b + 1):
                        dve.wait_ge(pt_hi, 4 * g + i + 1)
                        dve.tensor_tensor(probT[1][:, i], pt_ps[i % 2][:, :], probT[0][:, i].bitcast(F32),
                                          ALU.subtract).then_inc(pt_ready, 1)
                if not is_at(g, 0):
                    output(g - 1, before, (3,))
                for b in range(2):
                    dve.wait_ge(av_hi, 2 * g + b + 1)
                    dve.tensor_tensor(ao[1][:, b], av_ps[b][:, :], ao[0][:, b].bitcast(F32),
                                      ALU.subtract).then_inc(av_ready, 1)
                if c == 0:
                    for h in range(2):
                        dve.wait_ge(b_hi, 2 * p + h + 1)
                        dve.tensor_tensor(wb[1][:, h], bank[h][:, :], wb[0][:, h].bitcast(F32),
                                          ALU.subtract).then_inc(b_split, 1)

            fold_a(0)
            queries(0)
            rotary(0)
            dve.wait_ge(T["x1_loaded"], 16)
            over_steps(dve, step)
            output(STEPS - 1, CHUNKS - 1, range(CT))

        @block.tensor
        def _(pe):
            def fold_a(p):
                pe.wait_ge(raw_loaded, 16 * (p + 1))
                for h in range(2):
                    for k in range(QC):
                        at = (2 * h + k) * P
                        mm = pe.matmul(av_ps[1][:, at:at + P], raw[:, h, UQ + k * P:UQ + (k + 1) * P],
                                       raw[:, h, UK:UK + P], start=True, stop=True)
                mm.then_inc(a_done, 1)

            def fold_b(g, p):
                for h in range(2):
                    if is_at(g, 0):
                        pe.wait_ge(qa_split, 2 + h + 1)
                    else:
                        pe.wait_ge(out_added, 4 * g + h - 1)
                    pe.matmul(bank[h][:, :], raw[:, h, UV:UV + P], raw[:, h, WO:WO + D],
                              start=True, stop=True).then_inc(b_done, 1)

            def queries(c, h):
                tok = slice(c * CHUNK, (c + 1) * CHUNK)
                for k in range(QC):
                    mm = mm3(pe, bank[h][:, :], both(wa, ALL, h, k), both(T["qc"], ALL, k, tok),
                             k == 0, k == QC - 1)
                mm.then_inc(qa_done, 1)

            def rotary(c):
                tok = slice(c * CHUNK, (c + 1) * CHUNK)
                for k in range(QC):
                    mm = mm3(pe, av_ps[0][:, :], both(wr, ALL, k), both(T["qc"], ALL, k, tok),
                             k == 0, k == QC - 1)
                mm.then_inc(qr_done, 1)

            def turn(g, b, start):
                for i in (2 * b, 2 * b + 1):
                    pe.wait_ge(p_ready, 4 * g + 2 * b + 2)
                    if not (start and i < 2):
                        pe.wait_ge(pt_ready, 4 * g + i - 1)
                    for h in range(2):
                        for t in range(2):
                            at = h * 256 + t * P
                            key = slice(i % 2 * P, (i % 2 + 1) * P)
                            mm = pe.transpose(pt_ps[i % 2][:, at:at + P], prob[:, 2 * b + t, h, key],
                                              T["ident"][:, :])
                    mm.then_inc(pt_done, 1)

            def output(m, p, free, tiles):
                pe.wait_ge(av_ready, 2 * m + 2)
                pe.wait_ge(b_split, 2 * p + 2)
                for j in tiles:
                    if j < 2:
                        free(j)
                    else:
                        pe.wait_ge(out_added, 4 * m + j - 1)
                    for h in range(2):
                        at = h * 256 + j % 2 * P
                        mm = mm3(pe, bank[j % 2][:, :], both(ao, ALL, j // 2, slice(at, at + P)),
                                 both(wb, ALL, h), h == 0, h == 1)
                    mm.then_inc(out_done, 1)

            def step(g, p, c, nxt):
                start = is_at(g, 0)
                pe.wait_ge(qa_split, 2 * g + 2)
                pe.wait_ge(qr_ready, g + 1)
                for t in range(CT):
                    if not (start and t < 2):
                        pe.wait_ge(max_done, 4 * g + t - 1)
                    seq = 2 * c + t // 2
                    tok = slice(t * P, (t + 1) * P)
                    mm3(pe, s_ps[t % 2][:, :], both(qr, ALL, tok),
                        [x[:, seq].rearrange("p h k -> p (h k)") for x in T["kr"]], True, False)
                    for h in range(2):
                        mm = mm3(pe, s_ps[t % 2][:, h * KEYS:(h + 1) * KEYS], both(qa, ALL, h, tok),
                                 both(T["kvT"], ALL, slice(seq * KEYS, (seq + 1) * KEYS)), False, h == 1)
                    mm.then_inc(s_done, 1)
                if nxt:
                    next_c = (c + 1) % CHUNKS
                    pe.wait_ge(a_split, (p + 2 if c == 3 else p + 1))
                    for h in range(2):
                        if start:
                            pe.wait_ge(qa_split, h + 1)
                        elif c == 1:
                            pe.wait_ge(b_split, 2 * p + h + 1)
                        else:
                            pe.wait_ge(out_added, 4 * g - 5 + h)
                        queries(next_c, h)
                    pe.wait_ge(wr_split, (p + 2 if c == 3 else p + 1))
                    if start:
                        pe.wait_ge(rot_done, 1)
                    else:
                        pe.wait_ge(av_ready, 2 * g - 1)
                    rotary(next_c)
                if folds_a(p, c):
                    pe.wait_ge(av_ready, 2 * g)
                    fold_a(p + 1)
                def free(j):
                    if nxt:
                        pe.wait_ge(qa_split, 2 * g + 2 + j + 1)
                    else:
                        pe.wait_ge(out_added, 4 * g - 5 + j)

                for b in range(2):
                    if not start:
                        output(g - 1, (p - 1 if c == 0 else p), free, ((0, 1), (2,))[b])
                    turn(g, b, start)
                if not start:
                    output(g - 1, (p - 1 if c == 0 else p), free, (3,))
                for b in range(2):
                    if not start:
                        pe.wait_ge(av_ready, 2 * g - 1 + b)
                    if b == 0 and nxt:
                        pe.wait_ge(rot_done, g + 2)
                    if b == 1 and folds_a(p, c):
                        pe.wait_ge(a_split, p + 2)
                    pe.wait_ge(pt_ready, 4 * g + 2 * b + 2)
                    for k in range(2):
                        mm = mm3(pe, av_ps[b][:, :], both(T["kv"], ALL, 4 * c + 2 * b + k),
                                 both(probT, ALL, 2 * b + k), k == 0, k == 1)
                    mm.then_inc(av_done, 1)
                if c == 0:
                    fold_b(g, p)

            fold_a(0)
            pe.wait_ge(a_split, 1)
            queries(0, 0)
            queries(0, 1)
            pe.wait_ge(wr_split, 1)
            rotary(0)
            over_steps(pe, step)
            output(STEPS - 1, PAIRS - 1, lambda j: pe.wait_ge(out_added, 4 * STEPS - 5 + j), range(CT))


FF = 1024
KF = FF // P
QMAX = 127.0
MAGIC = 1.5 * 2.0 ** 23
H_IN = float(np.float32(1.0) / np.sqrt(np.float32(D)))
H_MID = float(np.float32(1.0) / np.sqrt(np.float32(FF)))


def ternary_weights(nc, X, d, F):
    with ExitStack() as ctx:
        def sb(name, shape, dt=F32):
            return ctx.enter_context(nc.sbuf_tensor("w_" + name, shape, dt))

        def sem(name):
            return ctx.enter_context(nc.semaphore("w_" + name))

        N = D * FF // P
        S = statistics(nc, ctx, "l3_", F["mv"], F["rstd"])
        raw = [sb("up_raw", [P, N]), sb("down_raw", [P, N])]
        h_raw = sb("h_raw", [P, KF * FF])
        ones = sb("ones", [P, P])
        magic = F["magic"]
        sums = sb("sums", [P, 2])
        inverse = sb("inverse", [P, 2])
        total_ps = ctx.enter_context(nc.psum_tensor("w_total", [P, 2], F32))
        loaded = [sem("up_loaded"), sem("down_loaded")]
        h_loaded = sem("h_loaded")
        h_copied = sem("h_copied")
        const_ready = sem("const_ready")
        summed = sem("summed")
        total_done = sem("total_done")
        mean_done = sem("mean_done")
        inverse_done = sem("inverse_done")
        rounded = sem("rounded")
        clipped = sem("clipped")
        written = sem("written")
        block = ctx.enter_context(nc.Block())
        PIECE = N // 4
        pieces = [(i, slice(j * PIECE, (j + 1) * PIECE)) for i in range(2) for j in range(4)]

        def h_scratch(i):
            return F["h"][:, i * N:(i + 1) * N]

        @block.sync
        def _(sp):
            sp.dma_start(raw[0][:, :], d["up"]).then_inc(loaded[0], 16)
            sp.dma_start(raw[1][:, :], d["down"]).then_inc(loaded[1], 16)
            sp.dma_start(h_raw[:, :], d["hadamard"]).then_inc(h_loaded, 16)

        @block.gpsimd
        def _(pool):
            pool.memset(ones[:, :], 1.0).then_inc(const_ready, 1)
            pool.memset(magic[:, :], MAGIC).then_inc(const_ready, 1)
            for n, (i, part) in enumerate(pieces):
                pool.wait_ge(clipped, n + 1)
                pool.tensor_scalar(F["t"][i][:, part], raw[i][:, part], -MAGIC, None,
                                   ALU.add).then_inc(written, 1)

        @block.scalar
        def _(act):
            statistics_scalar(act, S)
            for i in range(2):
                act.wait_ge(loaded[i], 16)
                act.activation(h_scratch(i), raw[i][:, :], ACT.Abs, accum_out=sums[:, i:i + 1]).then_inc(summed, 1)
            for n, (i, part) in enumerate(pieces):
                act.wait_ge(inverse_done, 1)
                act.wait_ge(const_ready, 2)
                act.activation(raw[i][:, part], raw[i][:, part], ACT.Identity, scale=inverse[:, i:i + 1],
                               bias=magic[:, 0:1]).then_inc(rounded, 1)
            act.wait_ge(h_loaded, 16)
            half = KF * FF // 2
            act.activation(F["h"][:, half:], h_raw[:, half:], ACT.Copy).then_inc(h_copied, 1)

        @block.vector
        def _(dve):
            statistics_vector(dve, X, S, None, 0)
            dve.wait_ge(total_done, 1)
            dve.tensor_scalar(F["scale_w"][:, :], total_ps[:, :], 1.0 / (D * FF), 1e-5, ALU.mult,
                              ALU.max).then_inc(mean_done, 1)
            dve.wait_ge(mean_done, 1)
            dve.reciprocal(inverse[:, :], F["scale_w"][:, :]).then_inc(inverse_done, 1)
            for n, (i, part) in enumerate(pieces):
                dve.wait_ge(rounded, n + 1)
                dve.tensor_scalar(raw[i][:, part], raw[i][:, part], MAGIC + 1.0, MAGIC - 1.0, ALU.min,
                                  ALU.max).then_inc(clipped, 1)
            dve.wait_ge(h_loaded, 16)
            dve.wait_ge(summed, 2)
            half = KF * FF // 2
            dve.tensor_copy(F["h"][:, 0:half], h_raw[:, 0:half]).then_inc(h_copied, 1)

        @block.tensor
        def _(pe):
            pe.wait_ge(const_ready, 2)
            pe.wait_ge(summed, 2)
            pe.matmul(total_ps[:, :], ones[:, :], sums[:, :], start=True, stop=True).then_inc(total_done, 1)


def feed_forward(nc, X, d, F, ident, out):
    with ExitStack() as ctx:
        def sb(name, shape, dt=F32):
            return ctx.enter_context(nc.sbuf_tensor("f_" + name, shape, dt))

        def sem(name):
            return ctx.enter_context(nc.semaphore("f_" + name))

        def psum(name, shape=(P, 512), dt=F32):
            return ctx.enter_context(nc.psum_tensor("f_" + name, list(shape), dt))

        ident_b = sb("ident_b", [P, P], BF16)
        RS = 4
        xn = sb("xn", [P, D])
        xt = [sb("xt_" + n, [P, D], F32R) for n in ("hi", "lo")]
        y = sb("y", [P, D])
        xq = sb("xq", [P, D], BF16)
        xqT = sb("xqT", [P, KD, CHUNK], BF16)
        amax = sb("amax", [P, 1])
        bound = sb("bound", [P, TILES])
        rec = sb("rec", [P, 1])
        factor = sb("factor", [P, 1])
        r = [sb(f"r{i}", [P, CHUNK]) for i in range(RS)]
        u = [sb("u_" + n, [P, KF, CHUNK], F32R) for n in ("hi", "lo")]
        amax2 = sb("amax2", [P, 2])
        unit = sb("unit", [P, 1])
        gain = sb("gain", [P, 1])
        top = sb("top", [P, 1])
        bound2 = sb("bound2", [P, 1])
        rec2 = sb("rec2", [P, 1])
        factor2 = sb("factor2", [P, 1])
        back = sb("back", [P, 2])
        y2 = sb("y2", [P, FF])
        q2 = sb("q2", [P, FF], BF16)
        q2T = sb("q2T", [P, KF, P], BF16)
        result = [sb(f"result{i}", [P, D]) for i in range(2)]
        t_ps, h_ps, down_ps = psum("t_ps"), psum("h_ps"), psum("down_ps")
        turn2_ps = psum("turn2_ps", (P, FF), BF16)
        up_ps = [psum(f"up_ps{i}") for i in range(2)]
        w_ps = [psum(f"w_ps{i}") for i in range(2)]
        turned_view = h_ps[:, 0:D // 2].bitcast(BF16)

        id_ready = sem("id_ready")
        xn_ready, t_done, t_hi, t_split = sem("xn_ready"), sem("t_done"), sem("t_hi"), sem("t_split")
        h_done, amax_done, bound_done = sem("h_done"), sem("amax_done"), sem("bound_done")
        rec_done, factor_done, y_done = sem("rec_done"), sem("factor_done"), sem("y_done")
        clip_done, xq_ready, turned, xq_copied = sem("clip_done"), sem("xq_ready"), sem("turned"), sem("xq_copied")
        up_done, relu_done, square_done = sem("up_done"), sem("relu_done"), sem("square_done")
        u_hi, u_even, u_odd, w_done = sem("u_hi"), sem("u_even"), sem("u_odd"), sem("w_done")
        small = sem("small")
        factor2_done, y2_done, clip2_done = sem("factor2_done"), sem("y2_done"), sem("clip2_done")
        q2_ready, turned2, q2_copied = sem("q2_ready"), sem("turned2"), sem("q2_copied")
        down_done, result_ready = sem("down_done"), sem("result_ready")
        stored = [sem(f"stored{i}") for i in range(2)]
        lone = {n: sem("lone_" + n) for n in ("dve", "pool")}
        block = ctx.enter_context(nc.Block())
        GROUPS = TILES // CT
        h3 = F["h"][:, :].rearrange("p (k n) -> p k n", k=KF)
        up3 = F["t"][0][:, :].rearrange("p (k n) -> p k n", k=KD)
        down3 = F["t"][1][:, :].rearrange("p (k n) -> p k n", k=KF)

        def is_at(g, value):
            return isinstance(g, int) and g == value

        def tile_of_X(s):
            return X[:, bass.ds(s, 1), :].rearrange("p a n -> p (a n)")

        def over_groups(eng, T, H, Q, U, W, R, D1, D2):
            T(0, 0)
            for i in range(CT):
                H(i, i)
                if i < CT - 1:
                    T(i + 1, i + 1)
                Q(i, i)
            U(0, 0, KF)

            def group(n, has_next):
                for i in range(CT):
                    s, ahead = 4 * n + i, 4 * n + 4 + i
                    if not has_next:
                        if i >= 2:
                            D2(s - 2, i - 2, n)
                        W(s, i, n, 0, KF)
                    elif i == 0:
                        W(s, i, n, 0, 2)
                        T(ahead, i)
                        W(s, i, n, 2, 5)
                        H(ahead, i)
                        T(ahead + 1, i + 1)
                        W(s, i, n, 5, KF)
                        Q(ahead, i)
                    else:
                        H(ahead, i)
                        if i < CT - 1:
                            T(ahead + 1, i + 1)
                        if i >= 2:
                            D2(s - 2, i - 2, n)
                        W(s, i, n, 0, KF - 1)
                        Q(ahead, i)
                        W(s, i, n, KF - 1, KF)
                    if i >= 1:
                        D1(s - 1, i - 1)
                    R(s, i, n)
                D2(4 * n + 2, 2, n)
                if has_next:
                    U(n + 1, 0, 6)
                D1(4 * n + 3, 3)
                if has_next:
                    U(n + 1, 6, KF)
                D2(4 * n + 3, 3, n)

            group(0, True)
            with eng.Fori(1, GROUPS - 1) as n:
                group(n, True)
            group(GROUPS - 1, False)

        def nothing(*_):
            pass

        @block.sync
        def _(sp):
            rows = out.rearrange("(s p) n -> s p n", p=P)
            with sp.Fori(0, TILES // 2) as it:
                for i in range(2):
                    sp.wait_ge(result_ready, 2 * it + i + 1)
                    sp.dma_start(rows[2 * it + i], result[i][:, :]).then_inc(stored[i], 16)
            for i in range(2):
                sp.wait_ge(stored[i], 16 * TILES // 2)

        @block.gpsimd
        def _(pool):
            pool.tensor_copy(ident_b[:, :], ident[:, :]).then_inc(id_ready, 1)

            def H(s, i):
                if not is_at(s, 0):
                    pool.wait_ge(turned, s)
                pool.wait_ge(clip_done, s + 1)
                alone(pool, lone["pool"])
                pool.tensor_scalar(xq[:, :], y[:, :], -MAGIC, None, ALU.add).then_inc(xq_ready, 1)

            def U(n, first, end):
                for o in range(first, end, 2):
                    pool.wait_ge(u_hi, KF * n + o + 1)
                    alone(pool, lone["pool"])
                    pool.tensor_tensor(u[1][:, o, :], r[o % RS][:, :], u[0][:, o, :].bitcast(F32),
                                       ALU.subtract).then_inc(u_even, 1)

            def R(s, i, n):
                if not is_at(s, 0):
                    pool.wait_ge(turned2, s)
                pool.wait_ge(clip2_done, s + 1)
                alone(pool, lone["pool"])
                pool.tensor_scalar(q2[:, :], y2[:, :], -MAGIC, None, ALU.add).then_inc(q2_ready, 1)

            over_groups(pool, nothing, H, nothing, U, nothing, R, nothing, nothing)

        @block.scalar
        def _(act):
            def T(s, i):
                act.wait_ge(t_done, s + 1)
                act.activation(xt[0][:, :], t_ps[:, :], ACT.Copy).then_inc(t_hi, 1)

            def H(s, i):
                if not is_at(s, 0):
                    act.wait_ge(xq_ready, s)
                act.wait_ge(factor_done, s + 1)
                act.activation(y[:, :], h_ps[:, :], ACT.Identity, scale=factor[:, 0:1],
                               bias=F["magic"][:, 0:1]).then_inc(y_done, 1)

            def Q(s, i):
                act.wait_ge(turned, s + 1)
                act.activation(xqT[:, :, i * P:(i + 1) * P], r3(turned_view, P), ACT.Copy).then_inc(xq_copied, 1)

            def U(n, first, end):
                def leading(o):
                    act.wait_ge(square_done, KF * n + o + 1)
                    act.activation(u[0][:, o, :], r[o % RS][:, :], ACT.Copy).then_inc(u_hi, 1)

                for o in range(first, end):
                    act.wait_ge(up_done, KF * n + o + 1)
                    if not (is_at(n, 0) and o < RS):
                        act.wait_ge((u_even, u_odd)[o % 2], KF // 2 * n + (o - RS) // 2 + 1)
                    act.activation(r[o % RS][:, :], up_ps[o % 2][:, :], ACT.Relu).then_inc(relu_done, 1)
                    if o:
                        leading(o - 1)
                if end == KF:
                    leading(KF - 1)

            def R(s, i, n):
                if not is_at(s, 0):
                    act.wait_ge(q2_ready, s)
                act.wait_ge(factor2_done, s + 1)
                for j in range(2):
                    ins = act.activation(y2[:, j * 512:(j + 1) * 512], w_ps[j][:, :], ACT.Identity,
                                         scale=factor2[:, 0:1], bias=F["magic"][:, 0:1])
                ins.then_inc(y2_done, 1)

            def D1(s, i):
                act.wait_ge(turned2, s + 1)
                if not is_at(s, 0):
                    act.wait_ge(down_done, s)
                act.activation(q2T[:, :, :], r3(turn2_ps[:, :], P), ACT.Copy).then_inc(q2_copied, 1)

            over_groups(act, T, H, Q, U, nothing, R, D1, nothing)

        @block.vector
        def _(dve):
            def normalize(s):
                dve.tensor_scalar(xn[:, :], tile_of_X(s), F["mv"][:, bass.ds(s, 1), 0],
                                  F["rstd"][:, bass.ds(s, 1)], ALU.subtract, ALU.mult).then_inc(xn_ready, 1)

            def T(s, i):
                if i == 0:
                    normalize(s)
                dve.wait_ge(t_hi, s + 1)
                dve.tensor_tensor(xt[1][:, :], t_ps[:, :], xt[0][:, :].bitcast(F32),
                                  ALU.subtract).then_inc(t_split, 1)
                if i < CT - 1:
                    normalize(s + 1)

            def H(s, i):
                dve.wait_ge(h_done, s + 1)
                dve.tensor_reduce(amax[:, :], h_ps[:, :], AX.X, ALU.max,
                                  apply_absolute_value=True).then_inc(amax_done, 1)
                dve.wait_ge(amax_done, s + 1)
                dve.tensor_scalar(bound[:, bass.ds(s, 1)], amax[:, :], H_IN, 1e-5, ALU.mult,
                                  ALU.max).then_inc(bound_done, 1)
                dve.wait_ge(bound_done, s + 1)
                alone(dve, lone["dve"])
                dve.reciprocal(rec[:, :], bound[:, bass.ds(s, 1)]).then_inc(rec_done, 1)
                dve.wait_ge(rec_done, s + 1)
                dve.tensor_scalar(factor[:, :], rec[:, :], QMAX * H_IN, None, ALU.mult).then_inc(factor_done, 1)
                dve.wait_ge(y_done, s + 1)
                dve.tensor_scalar(y[:, :], y[:, :], MAGIC + QMAX, MAGIC - QMAX, ALU.min,
                                  ALU.max).then_inc(clip_done, 1)

            def U(n, first, end):
                def rest(o):
                    dve.wait_ge(u_hi, KF * n + o + 1)
                    dve.tensor_tensor(u[1][:, o, :], r[o % RS][:, :], u[0][:, o, :].bitcast(F32),
                                      ALU.subtract).then_inc(u_odd, 1)

                for o in range(first, end):
                    dve.wait_ge(relu_done, KF * n + o + 1)
                    dve.tensor_tensor(r[o % RS][:, :], r[o % RS][:, :], r[o % RS][:, :],
                                      ALU.mult).then_inc(square_done, 1)
                    if o >= 2 and o % 2 == 0:
                        rest(o - 1)
                if end == KF:
                    rest(KF - 1)

            def R(s, i, n):
                dve.wait_ge(w_done, s + 1)
                for j in range(2):
                    ins = dve.tensor_reduce(amax2[:, j:j + 1], w_ps[j][:, :], AX.X, ALU.max,
                                            apply_absolute_value=True)
                dve.tensor_scalar(unit[:, :], bound[:, bass.ds(s, 1)], F["scale_w"][:, 0:1], 1.0 / QMAX,
                                  ALU.mult, ALU.mult).then_inc(small, 1)
                dve.wait_ge(small, 5 * s + 1)
                dve.tensor_scalar(gain[:, :], unit[:, :], unit[:, 0:1], H_MID, ALU.mult, ALU.mult).then_inc(small, 1)
                dve.wait_ge(small, 5 * s + 2)
                dve.tensor_scalar(top[:, :], amax2[:, 0:1], amax2[:, 1:2], gain[:, 0:1], ALU.max,
                                  ALU.mult).then_inc(small, 1)
                dve.wait_ge(small, 5 * s + 3)
                dve.tensor_scalar(bound2[:, :], top[:, :], 1e-5, None, ALU.max).then_inc(small, 1)
                dve.wait_ge(small, 5 * s + 4)
                dve.reciprocal(rec2[:, :], bound2[:, :]).then_inc(small, 1)
                dve.tensor_scalar(back[:, i % 2:i % 2 + 1], bound2[:, :], F["scale_w"][:, 1:2], 1.0 / QMAX,
                                  ALU.mult, ALU.mult)
                dve.wait_ge(small, 5 * s + 5)
                dve.tensor_scalar(factor2[:, :], rec2[:, :], gain[:, 0:1], QMAX, ALU.mult,
                                  ALU.mult).then_inc(factor2_done, 1)
                dve.wait_ge(y2_done, s + 1)
                dve.tensor_scalar(y2[:, :], y2[:, :], MAGIC + QMAX, MAGIC - QMAX, ALU.min,
                                  ALU.max).then_inc(clip2_done, 1)

            def D2(s, i, n):
                if not (is_at(s, 0) or is_at(s, 1)):
                    dve.wait_ge(stored[i % 2], 32 * n + 16 * (i // 2))
                dve.wait_ge(down_done, s + 1)
                dve.scalar_tensor_tensor(out=result[i % 2][:, :], in0=down_ps[:, :],
                                         scalar=back[:, i % 2:i % 2 + 1], in1=tile_of_X(s),
                                         op0=ALU.mult, op1=ALU.add).then_inc(result_ready, 1)

            over_groups(dve, T, H, nothing, U, nothing, R, nothing, D2)

        @block.tensor
        def _(pe):
            pe.wait_ge(id_ready, 1)

            def T(s, i):
                pe.wait_ge(xn_ready, s + 1)
                if not is_at(s, 0):
                    pe.wait_ge(t_split, s)
                for k in range(KD):
                    mm = pe.transpose(t_ps[:, k * P:(k + 1) * P], xn[:, k * P:(k + 1) * P], ident[:, :])
                mm.then_inc(t_done, 1)

            def H(s, i):
                pe.wait_ge(t_split, s + 1)
                if not is_at(s, 0):
                    pe.wait_ge(xq_copied, s)
                for k in range(KD):
                    for part in range(2):
                        mm = pe.matmul(h_ps[:, :], xt[part][:, k * P:(k + 1) * P], h3[:, k, 0:D],
                                       start=(k == 0 and part == 0), stop=(k == KD - 1 and part == 1))
                mm.then_inc(h_done, 1)

            def Q(s, i):
                pe.wait_ge(xq_ready, s + 1)
                for k in range(KD):
                    mm = pe.transpose(turned_view[:, k * P:(k + 1) * P], xq[:, k * P:(k + 1) * P], ident_b[:, :])
                mm.then_inc(turned, 1)

            def U(n, first, end):
                if first == 0:
                    pe.wait_ge(xq_copied, 4 * n + 4)
                for o in range(first, end):
                    if not (is_at(n, 0) and o < 2):
                        pe.wait_ge(relu_done, KF * n + o - 1)
                    for k in range(KD):
                        mm = pe.matmul(up_ps[o % 2][:, :], up3[:, k, o * P:(o + 1) * P], xqT[:, k, :],
                                       start=(k == 0), stop=(k == KD - 1))
                    mm.then_inc(up_done, 1)

            def W(s, i, n, first, end):
                if first == 0:
                    pe.wait_ge(u_even, KF // 2 * n + KF // 2)
                    pe.wait_ge(u_odd, KF // 2 * n + KF // 2)
                    if not is_at(s, 0):
                        pe.wait_ge(y2_done, s)
                for k in range(first, end):
                    for part in range(2):
                        for j in range(2):
                            mm = pe.matmul(w_ps[j][:, :], u[part][:, k, i * P:(i + 1) * P],
                                           h3[:, k, j * 512:(j + 1) * 512],
                                           start=(k == 0 and part == 0), stop=(k == KF - 1 and part == 1))
                if end == KF:
                    mm.then_inc(w_done, 1)

            def D1(s, i):
                pe.wait_ge(q2_ready, s + 1)
                if not is_at(s, 0):
                    pe.wait_ge(q2_copied, s)
                for k in range(KF):
                    mm = pe.transpose(turn2_ps[:, k * P:(k + 1) * P], q2[:, k * P:(k + 1) * P], ident_b[:, :])
                mm.then_inc(turned2, 1)

            def D2(s, i, n):
                pe.wait_ge(q2_copied, s + 1)
                if not is_at(s, 0):
                    pe.wait_ge(result_ready, s)
                for k in range(KF):
                    mm = pe.matmul(down_ps[:, :], q2T[:, k, :], down3[:, k, :], start=(k == 0), stop=(k == KF - 1))
                mm.then_inc(down_done, 1)

            over_groups(pe, T, H, Q, U, W, nothing, D1, D2)


def decoder_layer(nc, d, out):
    attT = nc.dram_tensor("attT", (STEPS, P, 2, CHUNK), F32, kind="Internal").ap()
    x1 = nc.dram_tensor("x1", (TOKENS, D), F32, kind="Internal").ap()
    with ExitStack() as ctx:
        X = ctx.enter_context(nc.sbuf_tensor("X", [P, TILES, D], F32))
        ident = ctx.enter_context(nc.sbuf_tensor("ident", [P, P], F32))
        LOADS = 4
        x_loaded = [ctx.enter_context(nc.semaphore(f"x_loaded{i}")) for i in range(LOADS)]
        consts_loaded = ctx.enter_context(nc.semaphore("consts_loaded"))

        with nc.Block() as block:
            @block.sync
            def _(sp):
                for i in range(LOADS):
                    rows = slice(i * TOKENS // LOADS, (i + 1) * TOKENS // LOADS)
                    sp.dma_start(X[:, i * TILES // LOADS:(i + 1) * TILES // LOADS, :],
                                 d["x"][rows, :].rearrange("(t p) n -> p t n", p=P)).then_inc(x_loaded[i], 16)
                sp.dma_start(ident[:, :], d["ident"]).then_inc(consts_loaded, 16)
                sp.wait_ge(consts_loaded, 16)

        with ExitStack() as phase:
            xT = [phase.enter_context(nc.sbuf_tensor("xT_" + n, [P, KD, TOKENS], F32R)) for n in ("hi", "lo")]
            layernorm_transposed(nc, X, x_loaded, LOADS, ident, "l1_", *xT)
            segment_attention(nc, X, ident, xT, d, consts_loaded, attT)
        with ExitStack() as phase:
            def sb(name, shape, dt=F32):
                return phase.enter_context(nc.sbuf_tensor("t_" + name, shape, dt))

            def parts(name, shape):
                return sb(name + "_hi", shape, F32R), sb(name + "_lo", shape, F32R)

            qc = parts("qc", [P, QC, TOKENS])
            attention_output(nc, X, d, ident, attT, x1, qc)
            reuse_semaphores(nc)
            T = {"ident": ident, "qc": qc, "x1_loaded": ctx.enter_context(nc.semaphore("x1_loaded")), "cos": sb("cos", [P, KEYS]), "sin": sb("sin", [P, KEYS]),
                 "mask": sb("mask", [P, TILES, KEYS], BF16), "kvT": parts("kvT", [P, TOKENS]),
                 "kv": parts("kv", [P, TILES, P]), "kr": parts("kr", [P, SEQS, 2, KEYS])}
            latents(nc, d, T, X, x1)
            cross_attention(nc, X, d, T)

        with ExitStack() as phase:
            def sb(name, shape, dt=F32):
                return phase.enter_context(nc.sbuf_tensor("g_" + name, shape, dt))

            F = {"mv": sb("mv", [P, TILES, 2]), "rstd": sb("rstd", [P, TILES]), "magic": sb("magic", [P, 1]),
                 "scale_w": sb("scale_w", [P, 2]), "h": sb("h", [P, KF * FF], F32R),
                 "t": [sb("up_t", [P, D * FF // P], BF16), sb("down_t", [P, D * FF // P], BF16)]}
            ternary_weights(nc, X, d, F)
            feed_forward(nc, X, d, F, ident, out)


def lay_out(inputs):
    f = {k: np.asarray(v) for k, v in inputs.items()}
    a = {"x": f["x"].reshape(TOKENS, D)}
    a["ident"] = np.eye(P, dtype=np.float32)
    s = np.arange(P)
    a["causal"] = np.where(s[None, :] <= s[:, None], 0.0, NEG).astype(np.float32)
    a["betas"] = f["L0_attn_betas"].reshape(HEADS, P).T
    for n in "qkv":
        a["w" + n] = f["L0_attn_W" + n].reshape(KD, P, PAIRS, 256).transpose(2, 1, 0, 3).reshape(PAIRS, P, 1024)
    a["wo"] = f["L0_attn_Wo"].reshape(HEADS, P, D).transpose(1, 0, 2)
    def rows(w, n):
        return w.reshape(n, P, -1).transpose(1, 0, 2)

    def filled(w):
        return np.concatenate([w, np.zeros((QC * P - w.shape[0],) + w.shape[1:], w.dtype)])

    a["ctxT"] = f["ctx_2048"].reshape(CHUNKS, CHUNK, KD, P).transpose(0, 3, 2, 1)
    kr = f["L0_xattn_W_kr"].reshape(P, 2, 1, 32)
    a["wkv"] = np.concatenate([rows(f["L0_xattn_W_kvc"], KD), np.repeat(kr, 2, 2).reshape(P, 1, P)], 1)
    a["wdq"] = rows(np.ascontiguousarray(filled(f["L0_xattn_W_dq"].T).T), KD)
    a["ids"] = f["itok_BxS_0_1023"].reshape(TILES, P).T
    a["kio"] = np.broadcast_to(np.arange(KEYS, dtype=np.float32), (P, KEYS))
    freq = np.float32(1.0) / np.float32(10000.0) ** (np.arange(32, dtype=np.float32) / np.float32(32))
    ang = (np.arange(KEYS, dtype=np.float32)[:, None] * freq).T
    a["cos"] = np.tile(np.cos(ang), (4, 1))
    a["sin"] = np.concatenate([np.tile(-np.sin(ang), (2, 1)), np.tile(np.sin(ang), (2, 1))])
    head_of_row = np.arange(P) // 32 % 2
    a["rows_of"] = np.stack([head_of_row == 0, head_of_row == 1], 1).astype(np.float32)
    uq = filled(f["L0_xattn_W_uq"]).reshape(QC * P, PAIRS, 2, P).transpose(1, 3, 2, 0)
    uk = f["L0_xattn_W_uk"].reshape(P, PAIRS, 2, P).transpose(1, 3, 2, 0)
    uv = f["L0_xattn_W_uv"].reshape(P, PAIRS, 2, P).transpose(1, 3, 2, 0)
    wo = f["L0_xattn_W_o"].reshape(PAIRS, 2, P, D).transpose(0, 2, 1, 3)
    a["xw"] = np.concatenate([uq, uk, uv, wo], 3)
    qr = filled(f["L0_xattn_W_qr"]).reshape(QC, P, PAIRS, 2, 2, 32)
    a["xwr"] = qr.transpose(2, 1, 0, 4, 3, 5).reshape(PAIRS, P, QC, P)
    a["up"] = rows(f["L0_ffn_w_up"].T, KD).reshape(P, -1)
    a["down"] = rows(f["L0_ffn_w_down"].T, KF).reshape(P, -1)
    sylvester = np.ones((1, 1), np.float32)
    while len(sylvester) < FF:
        sylvester = np.block([[sylvester, sylvester], [sylvester, -sylvester]])
    a["hadamard"] = rows(sylvester, KF).reshape(P, -1)
    return {k: np.ascontiguousarray(v) for k, v in a.items()}


def kernel(**inputs):
    import concourse.bacc as _bacc
    from concourse.bass_utils import run_bass_kernel_spmd as _run

    nc = _bacc.Bacc("TRN2", target_bir_lowering=False, num_devices=1, dynamic_dma_scratch_size=1024)
    arrays = lay_out(inputs)
    d = {k: nc.dram_tensor("in_" + k, v.shape, mybir.dt.from_np(v.dtype), kind="ExternalInput").ap()
         for k, v in arrays.items()}
    out = nc.dram_tensor("out_x", (TOKENS, D), F32, kind="ExternalOutput").ap()
    decoder_layer(nc, d, out)
    r = _run(nc, [{"in_" + k: v for k, v in arrays.items()}], core_ids=[0])
    return r.results[0]["out_x"].reshape(8, 256, D)
```

```python
from contextlib import ExitStack

import numpy as np

import concourse.bass as bass
from concourse import mybir

F32 = mybir.dt.float32
F32R = mybir.dt.float32r
BF16 = mybir.dt.bfloat16
I32 = mybir.dt.int32
ACT = mybir.ActivationFunctionType
ALU = mybir.AluOpType
AX = mybir.AxisListType

P = 128
TOKENS = 2048
TILES = TOKENS // P
D = 512
KD = D // P
HEADS = 16
PAIRS = HEADS // 2
CHUNK = 512
CHUNKS = TOKENS // CHUNK
CT = CHUNK // P
STEPS = PAIRS * CHUNKS
EPS = 1e-5
NEG = -1e30
ATT_SCALE = float(np.float32(128.0) ** np.float32(-0.5))


def r3(ap, n):
    return ap.rearrange("p (a b) -> p a b", b=n)


def mm3(pe, out, lhs, rhs, first=True, last=True):
    (lh, ll), (rh, rl) = lhs, rhs
    pe.matmul(out, lh, rh, start=first, stop=False)
    pe.matmul(out, lh, rl, start=False, stop=False)
    return pe.matmul(out, ll, rh, start=False, stop=last)


def reuse_semaphores(nc):
    over = sorted(nc.released_uncleared_semaphores)
    assert over == list(range(over[0], over[-1] + 1))
    with nc.Block() as block:
        @block.gpsimd
        def _(pool):
            pool.sem_clear(range(over[0], over[-1] + 1))


def alone(eng, sem):
    eng.sem_inc(sem, 1)


def statistics(nc, ctx, tag, mv, rstd):
    def sb(name, shape):
        return ctx.enter_context(nc.sbuf_tensor(tag + name, shape, F32))

    S = {n: ctx.enter_context(nc.semaphore(tag + n)) for n in
         ("stats_done", "aggr_done", "var_ready", "std_ready", "rstd_ready")}
    S.update(mv=mv, rstd=rstd, st=sb("st", [P, TILES, 6]), var_eps=sb("var_eps", [P, TILES]),
             std=sb("std", [P, TILES]))
    return S


def moments(dve, X, S, x_loaded, n, parts):
    tiles = range(n * TILES // parts, (n + 1) * TILES // parts)
    if x_loaded is not None:
        dve.wait_ge(x_loaded[n], 16)
    for t in tiles:
        dve.bn_stats(S["st"][:, t, :], X[:, t, :]).then_inc(S["stats_done"], 1)
    for t in tiles:
        dve.wait_ge(S["stats_done"], t + 1)
        dve.bn_aggr(S["mv"][:, t, :], S["st"][:, t, :]).then_inc(S["aggr_done"], 1)
    at = slice(tiles[0], tiles[-1] + 1)
    dve.wait_ge(S["aggr_done"], at.stop)
    dve.tensor_scalar(S["var_eps"][:, at], S["mv"][:, at, 1], EPS, None, ALU.add).then_inc(S["var_ready"], 1)


def inverse_root(dve, S, n, parts):
    at = slice(n * TILES // parts, (n + 1) * TILES // parts)
    std, rstd, done = S["std"][:, at], S["rstd"][:, at], S["rstd_ready"]
    dve.wait_ge(S["std_ready"], n + 1)
    dve.reciprocal(rstd, std).then_inc(done, 1)
    dve.wait_ge(done, 5 * n + 1)
    dve.tensor_tensor(std, rstd, rstd, ALU.mult).then_inc(done, 1)
    dve.wait_ge(done, 5 * n + 2)
    dve.tensor_tensor(std, std, S["var_eps"][:, at], ALU.mult).then_inc(done, 1)
    dve.wait_ge(done, 5 * n + 3)
    dve.tensor_scalar(std, std, -0.5, 1.5, ALU.mult, ALU.add).then_inc(done, 1)
    dve.wait_ge(done, 5 * n + 4)
    dve.tensor_tensor(rstd, rstd, std, ALU.mult).then_inc(done, 1)
    dve.wait_ge(done, 5 * n + 5)


def root(act, S, n, parts):
    at = slice(n * TILES // parts, (n + 1) * TILES // parts)
    act.wait_ge(S["var_ready"], n + 1)
    act.activation(S["std"][:, at], S["var_eps"][:, at], ACT.Sqrt).then_inc(S["std_ready"], 1)


def layernorm_transposed(nc, X, x_loaded, x_loads, ident, tag, hi, lo):
    with ExitStack() as ctx:
        def sb(name, shape, dt=F32):
            return ctx.enter_context(nc.sbuf_tensor(tag + name, shape, dt))

        def sem(name):
            return ctx.enter_context(nc.semaphore(tag + name))

        mv = sb("mv", [P, TILES, 2])
        rstd = sb("rstd", [P, TILES])
        S = statistics(nc, ctx, tag, mv, rstd)
        xn = sb("xn", [P, 2, D])
        turned = [ctx.enter_context(nc.psum_tensor(f"{tag}turned{i}", [P, D], F32)) for i in range(2)]
        xn_ready = sem("xn_ready")
        turned_ready = sem("turned_ready")
        hi_written = sem("hi_written")
        lo_written = sem("lo_written")
        block = ctx.enter_context(nc.Block())

        part = TILES // x_loads

        @block.vector
        def _(dve):
            def normalize(t, i):
                dve.tensor_scalar(xn[:, i, :], X[:, t, :], mv[:, t:t + 1, 0], rstd[:, t:t + 1],
                                  ALU.subtract, ALU.mult).then_inc(xn_ready, 1)

            moments(dve, X, S, x_loaded, 0, x_loads)
            inverse_root(dve, S, 0, x_loads)
            normalize(0, 0)
            normalize(1, 1)
            for t in range(TILES):
                i, n = t % 2, t // part + 1
                if t % part == 0 and n < x_loads:
                    moments(dve, X, S, x_loaded, n, x_loads)
                if t % part == part - 2 and n < x_loads:
                    inverse_root(dve, S, n, x_loads)
                dve.wait_ge(hi_written, t + 1)
                dve.tensor_tensor(lo[:, :, t * P:(t + 1) * P], r3(turned[i][:, :], P),
                                  hi[:, :, t * P:(t + 1) * P].bitcast(F32),
                                  ALU.subtract).then_inc(lo_written, 1)
                if t + 2 < TILES:
                    normalize(t + 2, i)

        @block.scalar
        def _(act):
            root(act, S, 0, x_loads)
            for t in range(TILES):
                if t % part == 1 and t // part + 1 < x_loads:
                    root(act, S, t // part + 1, x_loads)
                act.wait_ge(turned_ready, t + 1)
                act.activation(hi[:, :, t * P:(t + 1) * P], r3(turned[t % 2][:, :], P),
                               ACT.Copy).then_inc(hi_written, 1)

        @block.tensor
        def _(pe):
            for t in range(TILES):
                pe.wait_ge(xn_ready, t + 1)
                if t >= 2:
                    pe.wait_ge(lo_written, t - 1)
                for k in range(KD):
                    mm = pe.transpose(turned[t % 2][:, k * P:(k + 1) * P], xn[:, t % 2, k * P:(k + 1) * P],
                                      ident[:, :])
                mm.then_inc(turned_ready, 1)


def heads_of(attT):
    return attT.rearrange("(p c) d h t -> p h d c t", c=CHUNKS)


def segment_attention(nc, X, ident, xT, w_raw, raw_loaded, d, consts_loaded, attT, head_raw, head_loaded):
    with ExitStack() as ctx:
        def sb(name, shape, dt=F32):
            return ctx.enter_context(nc.sbuf_tensor("a_" + name, shape, dt))

        def parts(name, shape):
            return sb(name + "_hi", shape, F32R), sb(name + "_lo", shape, F32R)

        def sem(name):
            return ctx.enter_context(nc.semaphore("a_" + name))

        def psum(name):
            return ctx.enter_context(nc.psum_tensor("a_" + name, [P, 512], F32))

        def both(pair, *index):
            return pair[0][index], pair[1][index]

        ones = sb("ones", [P, P])
        ones_r = sb("ones_r", [P, P], F32R)
        mask = sb("mask", [P, P])
        betas = sb("betas", [P, HEADS])
        beta_e = sb("beta_e", [P, HEADS])
        gate = sb("gate", [P, HEADS, 2])
        gate_p = sb("gate_p", [P, 2, 2])
        w = {n: parts("w" + n, [P, KD, 256]) for n in "qkv"}
        qT = parts("qT", [P, 2, CHUNK])
        kT = parts("kT", [P, 2, CHUNK])
        v = parts("v", [P, CT, 256])
        e = sb("e", [P, 2, 256])
        sq = sb("sq", [P, 2, 256])
        sk = sb("sk", [P, 2, 256])
        sqp = [parts(f"sq{i}", [P, 2, 256]) for i in range(2)]
        skp = parts("skt", [P, 4, P])
        zsum = sb("zsum", [P, 2, 2])
        z = sb("z", [P, 2, 2])
        zq = parts("zq", [P, 2, 256])
        prob = sb("prob", [P, 2, CT, P])
        probT = parts("probT", [P, 2, CT * P])
        mx = sb("mx", [P, 2, CT])
        nb = sb("nb", [P, 2, CT])
        rs = sb("rs", [P, 2, CT])
        rr = sb("rr", [P, 2, CT])
        mem = parts("mem", [P, 2, 256])
        att = sb("att", [P, 2, CHUNK])
        rec = sb("rec", [P, 256])
        amr = sb("amr", [P, 256])

        bank = [psum("bank0"), psum("bank1")]
        s_ps = [psum("s0"), psum("s1")]
        mem_ps = [psum("mem0"), psum("mem1")]
        ad_ps = [psum("ad0"), psum("ad1")]

        w_split = {n: sem("w_split_" + n) for n in "qkv"}
        w_hi = sem("w_hi")
        next_hi = sem("next_hi")
        ones_ready = sem("ones_ready")
        beta_step = sem("beta_step")
        gate_ready = sem("gate_ready")
        filled = sem("filled")
        hi_done = sem("hi_done")
        freed = sem("freed")
        sig_done = sem("sig_done")
        sq_hi = sem("sq_hi")
        sq_ready = sem("sq_ready")
        zsum_done, z_ready = sem("zsum_done"), sem("z_ready")
        zq_done, zq_hi, zq_ready = sem("zq_done"), sem("zq_hi"), sem("zq_ready")
        s_done = sem("s_done")
        max_done = sem("max_done")
        nb_done = sem("nb_done")
        exp_done = sem("exp_done")
        rr_done = sem("rr_done")
        p_ready = sem("p_ready")
        pt_done = sem("pt_done")
        pt_hi = sem("pt_hi")
        pt_ready = sem("pt_ready")
        den_done = sem("den_done")
        skt_done = sem("skt_done")
        skt_hi = sem("skt_hi")
        sk_ready = sem("sk_ready")
        mem_done = sem("mem_done")
        mem_hi = sem("mem_hi")
        mem_ready = sem("mem_ready")
        ad_done = sem("ad_done")
        ad_read = sem("ad_read")
        am_done = sem("am_done")
        rec_done = sem("rec_done")
        amr_done = sem("amr_done")
        att_done = sem("att_done")
        att_stored = sem("att_stored")
        wo_loaded = sem("wo_loaded")
        lone = {n: sem("lone_" + n) for n in ("dve", "pool")}
        block = ctx.enter_context(nc.Block())

        Q, K, V = 0, 2, 4

        def fill(chunk, kind, j):
            return 6 * chunk + kind + j

        def over_steps(eng, step):
            step(0, 0, True)
            with eng.Fori(0, PAIRS - 1) as p:
                for c in range(1, CHUNKS + 1):
                    step(CHUNKS * p + c, c % CHUNKS, True)
            for g in range(STEPS - CHUNKS + 1, STEPS):
                step(g, g % CHUNKS, g < STEPS - 1)

        def changes_weights(c, p):
            return c == CHUNKS - 2 and not (isinstance(p, int) and p == PAIRS - 1)

        def seg(ap, s):
            return ap.rearrange("p (b s t) -> p b s t", b=2, s=2)[:, :, s, :]

        @block.sync
        def _(sp):
            sp.dma_start(mask[:, :], d["causal"]).then_inc(consts_loaded, 16)
            sp.dma_start(betas[:, :], d["betas"]).then_inc(consts_loaded, 16)
            sp.dma_start(X[:, :, :], d["wo"]).then_inc(wo_loaded, 16)

            def store(g):
                sp.wait_ge(att_done, 2 * g + 2)
                sp.dma_start(attT[g], att[:, :, :]).then_inc(att_stored, 16)

            def load(n, p):
                sp.wait_ge(w_split[n], p + 1)
                sp.dma_start(w_raw[n][:, :], d["w" + n][p + 1]).then_inc(raw_loaded[n], 16)

            with sp.Fori(0, PAIRS - 1) as p:
                for n in "qkv":
                    load(n, p)
                for c in range(CHUNKS):
                    store(CHUNKS * p + c)
            sp.wait_ge(att_stored, 16 * (STEPS - CHUNKS))
            for i in range(2):
                sp.dma_start(r3(head_raw[i][:, :], CHUNK), heads_of(attT)[0, i]).then_inc(head_loaded[i], 16)
            for g in range(STEPS - CHUNKS, STEPS):
                store(g)
            sp.wait_ge(att_stored, 16 * STEPS)
            sp.wait_ge(wo_loaded, 16)

        @block.gpsimd
        def _(pool):
            pool.memset(ones[:, :], 1.0).then_inc(ones_ready, 1)
            pool.wait_ge(ones_ready, 1)
            pool.tensor_copy(ones_r[:, :], ones[:, :]).then_inc(ones_ready, 1)

            def take_gate(p):
                pool.wait_ge(gate_ready, 1)
                pool.tensor_copy(gate_p[:, :, :], gate[:, bass.ds(2 * p, 2), :]).then_inc(gate_ready, 1)

            def step(g, c, nxt):
                if c == 0:
                    if not (isinstance(g, int) and g == 0):
                        pool.wait_ge(att_done, 2 * g)
                    take_gate(pair_of[0])
                for h in range(2):
                    pool.wait_ge(rr_done, 2 * g + h + 1)
                    pool.tensor_tensor(prob[:, h], prob[:, h],
                                       rr[:, h, :].unsqueeze(2).to_broadcast([P, CT, P]),
                                       ALU.mult).then_inc(p_ready, 1)
                p = pair_of[0]
                ahead = changes_weights(c, p)
                if nxt:
                    split_sq(g + 1, (c + 1) % 2)
                    if ahead:
                        rest_of_weight(0, p)
                    make_zq(g + 1)
                if ahead:
                    rest_of_weight(1, p)
                    rest_of_weight(2, p)

            def rest_of_weight(i, p):
                n = "qkv"[i]
                hi, lo = (x[:, :, :].rearrange("p a b -> p (a b)") for x in w[n])
                pool.wait_ge(next_hi, 3 * p + i + 1)
                alone(pool, lone["pool"])
                pool.tensor_tensor(lo, w_raw[n][:, :], hi.bitcast(F32), ALU.subtract).then_inc(w_split[n], 1)

            def split_sq(g, par):
                pool.wait_ge(sig_done, 4 * g + 2)
                alone(pool, lone["pool"])
                hi, lo = sqp[par]
                pool.tensor_copy(hi[:, :, :], sq[:, :, :]).then_inc(sq_hi, 1)
                pool.wait_ge(sq_hi, g + 1)
                pool.tensor_tensor(lo[:, :, :], sq[:, :, :], hi[:, :, :].bitcast(F32),
                                   ALU.subtract).then_inc(sq_ready, 1)

            def make_zq(g):
                pool.wait_ge(z_ready, g + 1)
                if not (isinstance(g, int) and g == 0):
                    pool.wait_ge(den_done, g)
                alone(pool, lone["pool"])
                by_seq = sq[:, :, :].rearrange("p h (b t) -> p (h b) t", b=2)
                pool.tensor_tensor(by_seq, by_seq,
                                   z[:, :, :].rearrange("p h b -> p (h b)").unsqueeze(2).to_broadcast([P, 4, P]),
                                   ALU.mult).then_inc(zq_done, 1)
                pool.wait_ge(zq_done, g + 1)
                alone(pool, lone["pool"])
                pool.tensor_copy(zq[0][:, :, :], sq[:, :, :]).then_inc(zq_hi, 1)
                pool.wait_ge(zq_hi, g + 1)
                pool.tensor_tensor(zq[1][:, :, :], sq[:, :, :], zq[0][:, :, :].bitcast(F32),
                                   ALU.subtract).then_inc(zq_ready, 1)

            split_sq(0, 0)
            make_zq(0)
            pair_of = [0]
            step(0, 0, True)
            with pool.Fori(0, PAIRS - 1) as p:
                for c in range(1, CHUNKS + 1):
                    pair_of[0] = p + c // CHUNKS
                    step(CHUNKS * p + c, c % CHUNKS, True)
            pair_of[0] = PAIRS - 1
            for g in range(STEPS - CHUNKS + 1, STEPS):
                step(g, g % CHUNKS, g < STEPS - 1)

        @block.scalar
        def _(act):
            for n in "qkv":
                act.wait_ge(raw_loaded[n], 16)
                act.activation(w[n][0][:, :, :].rearrange("p a b -> p (a b)"), w_raw[n][:, :],
                               ACT.Copy).then_inc(w_hi, 1)
            act.wait_ge(consts_loaded, 48)
            act.activation(beta_e[:, :], betas[:, :], ACT.Exp, scale=-1.0).then_inc(beta_step, 1)

            def project(gc, kind, halves=(0, 1)):
                for j in halves:
                    act.wait_ge(filled, fill(gc, kind, j) + 1)
                    src = bank[j]
                    if kind == V:
                        dst = v[0][:, 2 * j:2 * j + 2, :].rearrange("p a n -> p (a n)")
                    else:
                        dst = (qT if kind == Q else kT)[0][:, j]
                        if not (isinstance(gc, int) and gc == 0):
                            act.wait_ge(zq_ready if kind == Q else skt_done, gc)
                        if kind == K:
                            act.wait_ge(sig_done, 4 * gc + 1 + j)
                        elif not (isinstance(gc, int) and gc == 0):
                            act.wait_ge(sig_done, 4 * gc - 1 + j)
                        half = seg(src[:, :], 1 if kind == Q else 0)
                        act.activation(r3(e[:, j], P), half, ACT.Exp)
                        act.activation(r3((sq if kind == Q else sk)[:, j], P), half, ACT.Relu)
                    act.activation(dst, src[:, :], ACT.Copy).then_inc(hi_done, 1)

            for kind in (Q, K, V):
                project(0, kind)

            def leading_of_weight(i, p):
                n = "qkv"[i]
                act.wait_ge(raw_loaded[n], 16 * (p + 2))
                act.activation(w[n][0][:, :, :].rearrange("p a b -> p (a b)"), w_raw[n][:, :],
                               ACT.Copy).then_inc(next_hi, 1)

            def step(g, c, nxt):
                ahead = changes_weights(c, pair_of[0])
                for h in range(2):
                    act.wait_ge(nb_done, 2 * g + h + 1)
                    for t in range(CT):
                        ins = act.activation(prob[:, h, t, :], prob[:, h, t, :], ACT.Exp,
                                             bias=nb[:, h, t:t + 1], scale=ATT_SCALE,
                                             accum_out=rs[:, h, t:t + 1])
                    ins.then_inc(exp_done, 1)
                act.wait_ge(skt_done, g + 1)
                act.activation(skp[0][:, :, :], r3(ad_ps[0][:, :], P), ACT.Copy).then_inc(skt_hi, 1)
                if nxt:
                    project(g + 1, Q)
                    project(g + 1, K, (0,))
                if ahead:
                    leading_of_weight(0, pair_of[0])
                for h in range(2):
                    act.wait_ge(pt_done, 2 * g + h + 1)
                    act.activation(probT[0][:, h], s_ps[h][:, :], ACT.Copy).then_inc(pt_hi, 1)
                for h in range(2):
                    act.wait_ge(mem_done, 2 * g + h + 1)
                    act.activation(mem[0][:, h], mem_ps[h][:, 0:256], ACT.Copy).then_inc(mem_hi, 1)
                if nxt:
                    project(g + 1, K, (1,))
                for h in range(2):
                    act.wait_ge(ad_done, 2 * g + h + 1)
                    if not (isinstance(g, int) and g == 0):
                        act.wait_ge(att_stored, 16 * g)
                    act.wait_ge(gate_ready, pair_of[0] + 2)
                    act.activation(att[:, h], ad_ps[h][:, :], ACT.Copy,
                                   scale=gate_p[:, h, 1:2]).then_inc(ad_read, 1)
                if ahead:
                    leading_of_weight(1, pair_of[0])
                if nxt:
                    project(g + 1, V)
                if ahead:
                    leading_of_weight(2, pair_of[0])

            pair_of = [0]
            step(0, 0, True)
            with act.Fori(0, PAIRS - 1) as p:
                for c in range(1, CHUNKS + 1):
                    pair_of[0] = p + c // CHUNKS
                    step(CHUNKS * p + c, c % CHUNKS, True)
            pair_of[0] = PAIRS - 1
            for g in range(STEPS - CHUNKS + 1, STEPS):
                step(g, g % CHUNKS, g < STEPS - 1)

        @block.vector
        def _(dve):
            for i, n in enumerate("qkv"):
                hi, lo = (x[:, :, :].rearrange("p a b -> p (a b)") for x in w[n])
                dve.wait_ge(w_hi, i + 1)
                dve.tensor_tensor(lo, w_raw[n][:, :], hi.bitcast(F32), ALU.subtract).then_inc(w_split[n], 1)
            dve.wait_ge(beta_step, 1)
            dve.tensor_scalar(beta_e[:, :], beta_e[:, :], 1.0, None, ALU.add).then_inc(beta_step, 1)
            dve.wait_ge(beta_step, 2)
            dve.reciprocal(gate[:, :, 0], beta_e[:, :]).then_inc(beta_step, 1)
            dve.wait_ge(beta_step, 3)
            dve.tensor_scalar(gate[:, :, 1], gate[:, :, 0], -1.0, 1.0, ALU.mult,
                              ALU.add).then_inc(gate_ready, 1)

            def project(gc, kind, halves=(0, 1)):
                for j in halves:
                    dst = (qT, kT, v)[kind // 2]
                    dst = [x[:, j] if kind != V else x[:, 2 * j:2 * j + 2, :].rearrange("p a n -> p (a n)")
                           for x in dst]
                    dve.wait_ge(hi_done, fill(gc, kind, j) + 1)
                    dve.tensor_tensor(dst[1], bank[j][:, :], dst[0].bitcast(F32),
                                      ALU.subtract).then_inc(freed, 1)
                    if kind != V:
                        s = sq if kind == Q else sk
                        dve.scalar_tensor_tensor(out=s[:, j], in0=e[:, j], scalar=1.0, in1=s[:, j],
                                                 op0=ALU.min, op1=ALU.add).then_inc(sig_done, 1)
                if kind == K and halves[-1] == 1:
                    dve.wait_ge(sig_done, 4 * gc + 4)
                    for j in range(2):
                        ins = dve.tensor_reduce(zsum[:, j, :], r3(sk[:, j], P), AX.X, ALU.add)
                    ins.then_inc(zsum_done, 1)
                    dve.wait_ge(zsum_done, gc + 1)
                    if not (isinstance(gc, int) and gc == 0):
                        dve.wait_ge(zq_done, gc)
                    dve.tensor_scalar(z[:, :, :], zsum[:, :, :], 1.0 / P, None, ALU.add).then_inc(z_ready, 1)

            for kind in (Q, K, V):
                project(0, kind)

            def step(g, c, nxt):
                for h in range(2):
                    dve.wait_ge(s_done, 2 * g + h + 1)
                    alone(dve, lone["dve"])
                    for t in range(CT):
                        ins = dve.tensor_tensor_reduce(prob[:, h, t, :], s_ps[h][:, t * P:(t + 1) * P],
                                                       mask[:, :], 1.0, -3e38, ALU.add, ALU.max,
                                                       mx[:, h, t:t + 1])
                    ins.then_inc(max_done, 1)
                    dve.wait_ge(max_done, 2 * g + h + 1)
                    dve.tensor_scalar(nb[:, h, :], mx[:, h, :], -ATT_SCALE, None,
                                      ALU.mult).then_inc(nb_done, 1)
                dve.wait_ge(skt_hi, g + 1)
                dve.tensor_tensor(skp[1][:, :, :], r3(ad_ps[0][:, :], P), skp[0][:, :, :].bitcast(F32),
                                  ALU.subtract).then_inc(sk_ready, 1)
                for h in range(2):
                    dve.wait_ge(exp_done, 2 * g + h + 1)
                    dve.reciprocal(rr[:, h, :], rs[:, h, :]).then_inc(rr_done, 1)
                if nxt:
                    project(g + 1, Q)
                    project(g + 1, K, (0,))
                for h in range(2):
                    dve.wait_ge(pt_hi, 2 * g + h + 1)
                    dve.tensor_tensor(probT[1][:, h], s_ps[h][:, :], probT[0][:, h].bitcast(F32),
                                      ALU.subtract).then_inc(pt_ready, 1)
                for h in range(2):
                    dve.wait_ge(mem_hi, 2 * g + h + 1)
                    dve.tensor_tensor(mem[1][:, h], mem_ps[h][:, 0:256], mem[0][:, h].bitcast(F32),
                                      ALU.subtract).then_inc(mem_ready, 1)
                if nxt:
                    project(g + 1, K, (1,))
                for h in range(2):
                    dve.wait_ge(am_done, 2 * g + h + 1)
                    dve.reciprocal(rec[:, :], mem_ps[h][:, 256:512]).then_inc(rec_done, 1)
                    dve.wait_ge(rec_done, 2 * g + h + 1)
                    dve.tensor_tensor(amr[:, :], mem_ps[h][:, 0:256], rec[:, :],
                                      ALU.mult).then_inc(amr_done, 1)
                    dve.wait_ge(amr_done, 2 * g + h + 1)
                    dve.wait_ge(ad_read, 2 * g + h + 1)
                    half = seg(att[:, h], 1)
                    dve.scalar_tensor_tensor(out=half, in0=r3(amr[:, :], P), scalar=gate_p[:, h, 0:1],
                                             in1=half, op0=ALU.mult, op1=ALU.add).then_inc(att_done, 1)
                if nxt:
                    project(g + 1, V)

            dve.wait_ge(consts_loaded, 48)
            over_steps(dve, step)

        @block.tensor
        def _(pe):
            pe.wait_ge(ones_ready, 2)

            def project(gc, kind, p, halves=(0, 1)):
                c = project_chunk[0]
                n = "qkv"[kind // 2]
                for j in halves:
                    f = fill(gc, kind, j)
                    if not (isinstance(f, int) and f < 2):
                        pe.wait_ge(freed, f - 1)
                    if j == 0:
                        pe.wait_ge(w_split[n], p + 1)
                    if kind == V:
                        for i in range(2):
                            t = 2 * j + i
                            tok = slice(c * CHUNK + t * P, c * CHUNK + (t + 1) * P)
                            for k in range(KD):
                                mm = mm3(pe, bank[j][:, i * 256:(i + 1) * 256],
                                         both(xT, slice(None), k, tok), both(w[n], slice(None), k),
                                         k == 0, k == KD - 1)
                    else:
                        for k in range(KD):
                            mm = mm3(pe, bank[j][:, :],
                                     both(w[n], slice(None), k, slice(j * P, (j + 1) * P)),
                                     both(xT, slice(None), k, slice(c * CHUNK, (c + 1) * CHUNK)),
                                     k == 0, k == KD - 1)
                    mm.then_inc(filled, 1)

            project_chunk = [0]
            for kind in (Q, K, V):
                project(0, kind, 0)

            def step(g, c, nxt, p_next):
                start = isinstance(g, int) and g == 0
                pe.wait_ge(freed, fill(g, V, 0))
                if not start:
                    pe.wait_ge(pt_ready, 2 * g)
                for h in range(2):
                    for t in range(CT):
                        tok = slice(t * P, (t + 1) * P)
                        mm = mm3(pe, s_ps[h][:, tok], both(qT, slice(None), h, tok),
                                 both(kT, slice(None), h, tok))
                    mm.then_inc(s_done, 1)
                pe.wait_ge(sig_done, 4 * g + 4)
                if not start:
                    pe.wait_ge(ad_read, 2 * g - 1)
                for h in range(2):
                    for b in range(2):
                        i = 2 * h + b
                        mm = pe.transpose(ad_ps[0][:, i * P:(i + 1) * P], sk[:, h, b * P:(b + 1) * P], ident[:, :])
                mm.then_inc(skt_done, 1)
                pe.wait_ge(zq_ready, g + 1)
                for h in range(2):
                    if not start:
                        pe.wait_ge(att_done, 2 * g - 1 + h)
                    for part in range(2):
                        mm = pe.matmul(mem_ps[h][:, 256:512], ones_r[:, :], zq[part][:, h],
                                       start=(part == 0), stop=(part == 1))
                mm.then_inc(den_done, 1)
                project_chunk[0] = (c + 1) % CHUNKS
                if nxt:
                    project(g + 1, Q, p_next)
                    project(g + 1, K, p_next, (0,))
                for h in range(2):
                    pe.wait_ge(p_ready, 2 * g + h + 1)
                    for t in range(CT):
                        mm = pe.transpose(s_ps[h][:, t * P:(t + 1) * P], prob[:, h, t, :], ident[:, :])
                    mm.then_inc(pt_done, 1)
                pe.wait_ge(sk_ready, g + 1)
                for h in range(2):
                    for b in range(2):
                        mm = mm3(pe, mem_ps[h][:, b * P:(b + 1) * P], both(skp, slice(None), 2 * h + b),
                                 both(v, slice(None), 2 * b, slice(h * P, (h + 1) * P)))
                    mm.then_inc(mem_done, 1)
                if nxt:
                    project(g + 1, K, p_next, (1,))
                for h in range(2):
                    pe.wait_ge(pt_ready, 2 * g + h + 1)
                    if not start:
                        pe.wait_ge(ad_read, 2 * g - 1 + h)
                    for t in range(CT):
                        tok = slice(t * P, (t + 1) * P)
                        mm = mm3(pe, ad_ps[h][:, tok], both(v, slice(None), t, slice(h * P, (h + 1) * P)),
                                 both(probT, slice(None), h, tok))
                    mm.then_inc(ad_done, 1)
                pe.wait_ge(sq_ready, g + 1)
                for h in range(2):
                    pe.wait_ge(mem_ready, 2 * g + h + 1)
                    for b in range(2):
                        mm = mm3(pe, mem_ps[h][:, b * P:(b + 1) * P],
                                 both(mem, slice(None), h, slice(b * P, (b + 1) * P)),
                                 both(sqp[c % 2], slice(None), h, slice(b * P, (b + 1) * P)))
                    mm.then_inc(am_done, 1)
                if nxt:
                    project(g + 1, V, p_next)

            step(0, 0, True, 0)
            with pe.Fori(0, PAIRS - 1) as p:
                for c in range(1, CHUNKS + 1):
                    step(CHUNKS * p + c, c % CHUNKS, True, p + (c + 1) // CHUNKS)
            for g in range(STEPS - CHUNKS + 1, STEPS):
                step(g, g % CHUNKS, g < STEPS - 1, PAIRS - 1)


QC = 2
HALF = P // 2


def attention_output(nc, X, d, ident, attT, x1, qc, raw, head_loaded, context_loaded):
    J = HEADS
    ROWS = P // J
    with ExitStack() as ctx:
        def sb(name, shape, dt=F32):
            return ctx.enter_context(nc.sbuf_tensor("o_" + name, shape, dt))

        def sem(name):
            return ctx.enter_context(nc.semaphore("o_" + name))

        wo = [sb("wo_" + n, [P, J, D], F32R) for n in ("hi", "lo")]
        head = [[sb(f"head{i}_{n}", [P, J, P], F32R) for n in ("hi", "lo")] for i in range(2)]
        xrow = [sb(f"xrow{i}", [P, D]) for i in range(2)]
        row = [sb(f"row{i}", [P, D]) for i in range(2)]
        wq_raw = sb("wq_raw", [P, KD, QC * P])
        wq = [sb("wq_" + n, [P, KD, QC * P], F32R) for n in ("hi", "lo")]
        st, mv = sb("st", [P, 6]), sb("mv", [P, 2])
        var_eps, std, rstd, newton = (sb(n, [P, 1]) for n in ("var_eps", "std", "rstd", "newton"))
        xn = [sb(f"xn{i}", [P, D]) for i in range(2)]
        xs = [sb("xs_" + n, [P, KD, J, 2, ROWS], F32R) for n in ("hi", "lo")]

        def psum(name):
            return ctx.enter_context(nc.psum_tensor("o_" + name, [P, D], F32))

        ps = [psum(f"ps{i}") for i in range(2)]
        t_ps = [psum(f"t_ps{i}") for i in range(2)]
        q_ps = psum("q_ps")
        wq_loaded, wq_hi, wq_split = sem("wq_loaded"), sem("wq_hi"), sem("wq_split")
        small, var_ready, std_ready = sem("small"), sem("var_ready"), sem("std_ready")
        newton_done = sem("newton_done")
        xn_ready, turned, xs_hi, xs_ready = sem("xn_ready"), sem("turned"), sem("xs_hi"), sem("xs_ready")
        q_done, q_hi, q_ready = sem("q_done"), sem("q_hi"), sem("q_ready")
        lone = {n: sem("lone_" + n) for n in ("act", "dve")}
        x_loaded = [sem(f"x_loaded{i}") for i in range(2)]
        head_hi = sem("head_hi")
        head_split = sem("head_split")
        wo_hi = sem("wo_hi")
        wo_split = sem("wo_split")
        product = sem("product")
        row_ready = sem("row_ready")
        row_stored = [sem(f"row_stored{i}") for i in range(2)]
        block = ctx.enter_context(nc.Block())

        def columns(part, p):
            return (qc[part][:, :, :].rearrange("l k (t m) -> l k t m", m=P)
                    [:, :, :, bass.ds(2 * ROWS * p, 2 * ROWS)])

        def of_head(x, i):
            return x[:, :, :, i, :]

        heads = heads_of(attT)
        x_rows = d["x"].rearrange("(t h s) n -> h t s n", h=HEADS, s=ROWS)
        x1_rows = x1.rearrange("(t h s) n -> h t s n", h=HEADS, s=ROWS)

        @block.sync
        def _(sp):
            def load(p, i):
                sp.dma_start(r3(raw[i][:, :], CHUNK), heads[p, i]).then_inc(head_loaded[i], 16)

            def load_x(p, i):
                sp.dma_start(xrow[i][:, :], x_rows[2 * p + i]).then_inc(x_loaded[i], 16)

            def store(p, i):
                sp.wait_ge(row_ready, 2 * p + i + 1)
                sp.dma_start(x1_rows[2 * p + i], row[i][:, :]).then_inc(row_stored[i], 16)

            for i in range(2):
                load_x(0, i)
            sp.dma_start(wq_raw[:, :, :], d["wdq"]).then_inc(wq_loaded, 16)
            def turn_over(p):
                for i in range(2):
                    sp.wait_ge(head_split, 2 * p + i + 1)
                    load(p + 1, i)
                    store(p, i)
                    load_x(p + 1, i)

            for c in range(CHUNKS):
                turn_over(c)
                if c == 0:
                    sp.wait_ge(wo_split, J)
                sp.dma_start(X[:, c * CT:(c + 1) * CT, :], d["ctxT"][c]).then_inc(context_loaded[c], 16)
            with sp.Fori(CHUNKS, PAIRS - 1) as p:
                turn_over(p)
            for i in range(2):
                store(HEADS // 2 - 1, i)
            for i in range(2):
                sp.wait_ge(row_stored[i], 16 * HEADS // 2)

        @block.scalar
        def _(act):
            def head_part(h, i, p):
                act.wait_ge(head_loaded[i], 16 * (p + 1))
                if not (isinstance(p, int) and p == 0):
                    act.wait_ge(product, h - 1)
                act.activation(head[i][0][:, :, :], raw[i][:, :].rearrange("d (m j) -> d j m", j=J),
                               ACT.Copy).then_inc(head_hi, 1)

            def root(h):
                act.wait_ge(var_ready, h + 1)
                act.activation(std[:, :], var_eps[:, :], ACT.Sqrt).then_inc(std_ready, 1)

            def turned_part(h, i):
                act.wait_ge(turned, h + 1)
                act.activation(of_head(xs[0], i), t_ps[i][:, :].rearrange("f (k t s) -> f k t s", k=KD, t=J),
                               ACT.Copy).then_inc(xs_hi, 1)

            def latent(p):
                act.wait_ge(q_done, p + 1)
                alone(act, lone["act"])
                act.activation(columns(0, p), q_ps[:, :].rearrange("l (k t m) -> l k t m", k=QC, t=J),
                               ACT.Copy).then_inc(q_hi, 1)

            head_part(0, 0, 0)
            for j in range(J):
                act.activation(wo[0][:, j, :], X[:, j, :], ACT.Copy).then_inc(wo_hi, 1)
            head_part(1, 1, 0)
            act.wait_ge(wq_loaded, 16)
            act.activation(wq[0][:, :, :], wq_raw[:, :, :], ACT.Copy).then_inc(wq_hi, 1)
            root(0)
            head_part(2, 0, 1)
            root(1)
            turned_part(0, 0)
            head_part(3, 1, 1)
            with act.Fori(1, PAIRS - 1) as p:
                root(2 * p)
                turned_part(2 * p - 1, 1)
                head_part(2 * p + 2, 0, p + 1)
                root(2 * p + 1)
                latent(p - 1)
                turned_part(2 * p, 0)
                head_part(2 * p + 3, 1, p + 1)
            root(HEADS - 2)
            turned_part(HEADS - 3, 1)
            root(HEADS - 1)
            latent(PAIRS - 2)
            turned_part(HEADS - 2, 0)
            turned_part(HEADS - 1, 1)
            latent(PAIRS - 1)

        @block.vector
        def _(dve):
            def head_part(h, i):
                dve.wait_ge(head_hi, h + 1)
                dve.tensor_tensor(head[i][1][:, :, :], raw[i][:, :].rearrange("d (m j) -> d j m", j=J),
                                  head[i][0][:, :, :].bitcast(F32), ALU.subtract).then_inc(head_split, 1)

            def finish(h, i, p):
                dve.wait_ge(product, h + 1)
                dve.wait_ge(x_loaded[i], 16 * (p + 1))
                if not (isinstance(p, int) and p == 0):
                    dve.wait_ge(row_stored[i], 16 * p)
                dve.tensor_tensor(row[i][:, :], ps[i][:, :], xrow[i][:, :], ALU.add).then_inc(row_ready, 1)
                dve.wait_ge(row_ready, h + 1)
                alone(dve, lone["dve"])
                dve.bn_stats(st[:, :], row[i][:, :]).then_inc(small, 1)
                dve.wait_ge(small, 5 * h + 1)
                alone(dve, lone["dve"])
                dve.bn_aggr(mv[:, :], st[:, :]).then_inc(small, 1)
                dve.wait_ge(small, 5 * h + 2)
                dve.tensor_scalar(var_eps[:, :], mv[:, 1:2], EPS, None, ALU.add).then_inc(var_ready, 1)

            def normalize(h, i):
                dve.wait_ge(std_ready, h + 1)
                dve.reciprocal(rstd[:, :], std[:, :]).then_inc(small, 1)
                dve.wait_ge(small, 5 * h + 3)
                dve.tensor_scalar(newton[:, :], rstd[:, :], rstd[:, 0:1], var_eps[:, 0:1], ALU.mult,
                                  ALU.mult).then_inc(small, 1)
                dve.wait_ge(small, 5 * h + 4)
                dve.tensor_scalar(std[:, :], newton[:, :], -0.5, 1.5, ALU.mult, ALU.add).then_inc(small, 1)
                dve.wait_ge(small, 5 * h + 5)
                dve.tensor_scalar(newton[:, :], rstd[:, :], std[:, 0:1], None, ALU.mult).then_inc(newton_done, 1)
                dve.wait_ge(newton_done, h + 1)
                dve.tensor_scalar(xn[i][:, :], row[i][:, :], mv[:, 0:1], newton[:, 0:1], ALU.subtract,
                                  ALU.mult).then_inc(xn_ready, 1)

            def turned_part(h, i):
                dve.wait_ge(xs_hi, h + 1)
                dve.tensor_tensor(of_head(xs[1], i), t_ps[i][:, :].rearrange("f (k t s) -> f k t s", k=KD, t=J),
                                  of_head(xs[0], i).bitcast(F32), ALU.subtract).then_inc(xs_ready, 1)

            def latent(p):
                dve.wait_ge(q_hi, p + 1)
                dve.tensor_tensor(columns(1, p), q_ps[:, :].rearrange("l (k t m) -> l k t m", k=QC, t=J),
                                  columns(0, p).bitcast(F32), ALU.subtract).then_inc(q_ready, 1)

            head_part(0, 0)
            for j in range(J):
                dve.wait_ge(wo_hi, j + 1)
                dve.tensor_tensor(wo[1][:, j, :], X[:, j, :], wo[0][:, j, :].bitcast(F32),
                                  ALU.subtract).then_inc(wo_split, 1)
            head_part(1, 1)
            dve.wait_ge(wq_hi, 1)
            dve.tensor_tensor(wq[1][:, :, :], wq_raw[:, :, :], wq[0][:, :, :].bitcast(F32),
                              ALU.subtract).then_inc(wq_split, 1)
            finish(0, 0, 0)
            normalize(0, 0)
            head_part(2, 0)
            finish(1, 1, 0)
            turned_part(0, 0)
            normalize(1, 1)
            head_part(3, 1)
            with dve.Fori(1, PAIRS - 1) as p:
                finish(2 * p, 0, p)
                turned_part(2 * p - 1, 1)
                normalize(2 * p, 0)
                head_part(2 * p + 2, 0)
                finish(2 * p + 1, 1, p)
                latent(p - 1)
                turned_part(2 * p, 0)
                normalize(2 * p + 1, 1)
                head_part(2 * p + 3, 1)
            finish(HEADS - 2, 0, PAIRS - 1)
            turned_part(HEADS - 3, 1)
            normalize(HEADS - 2, 0)
            finish(HEADS - 1, 1, PAIRS - 1)
            latent(PAIRS - 2)
            turned_part(HEADS - 2, 0)
            normalize(HEADS - 1, 1)
            turned_part(HEADS - 1, 1)
            latent(PAIRS - 1)

        @block.tensor
        def _(pe):
            def multiply(h, i):
                pe.wait_ge(head_split, h + 1)
                if not (isinstance(h, int) and h < 2):
                    pe.wait_ge(row_ready, h - 1)
                for j in range(J):
                    if isinstance(h, int) and h == 0:
                        pe.wait_ge(wo_split, j + 1)
                    mm = mm3(pe, ps[i][:, :], (head[i][0][:, j, :], head[i][1][:, j, :]),
                             (wo[0][:, j, :], wo[1][:, j, :]), j == 0, j == J - 1)
                mm.then_inc(product, 1)

            def turn(h, i):
                pe.wait_ge(xn_ready, h + 1)
                if not (isinstance(h, int) and h < 2):
                    pe.wait_ge(xs_ready, h - 1)
                for k in range(KD):
                    mm = pe.transpose(t_ps[i][:, k * P:(k + 1) * P], xn[i][:, k * P:(k + 1) * P], ident[:, :])
                mm.then_inc(turned, 1)

            def latent(p):
                pe.wait_ge(wq_split, 1)
                pe.wait_ge(xs_ready, 2 * p + 2)
                if not (isinstance(p, int) and p == 0):
                    pe.wait_ge(q_ready, p)
                for j in range(QC):
                    for k in range(KD):
                        mm = mm3(pe, q_ps[:, j * 256:(j + 1) * 256], [w[:, k, j * P:(j + 1) * P] for w in wq],
                                 [x[:, k, :, :, :].rearrange("f t h s -> f (t h s)") for x in xs],
                                 k == 0, k == KD - 1)
                mm.then_inc(q_done, 1)

            multiply(0, 0)
            multiply(1, 1)
            turn(0, 0)
            multiply(2, 0)
            turn(1, 1)
            multiply(3, 1)
            latent(0)
            turn(2, 0)
            with pe.Fori(2, PAIRS) as p:
                multiply(2 * p, 0)
                turn(2 * p - 1, 1)
                multiply(2 * p + 1, 1)
                latent(p - 1)
                turn(2 * p, 0)
            turn(HEADS - 1, 1)
            latent(PAIRS - 1)


KEYS = 256
SEQS = TOKENS // KEYS
LOOKBACK = 8
X_SCALE = float(np.float32(1.0) / np.sqrt(np.float32(192.0)))


def latents(nc, d, T, X, x1):
    with ExitStack() as ctx:
        def sb(name, shape, dt=F32):
            return ctx.enter_context(nc.sbuf_tensor("k_" + name, shape, dt))

        def sem(name):
            return ctx.enter_context(nc.semaphore("k_" + name))

        w_raw = sb("w_raw", [P, KD + 1, P])
        w = [sb("w_" + n, [P, KD + 1, P], F32R) for n in ("hi", "lo")]
        cT = [[sb(f"c{i}_{n}", [P, KD, CHUNK], F32R) for n in ("hi", "lo")] for i in range(2)]
        kvf = sb("kvf", [P, CHUNK])
        rot = sb("rot", [P, CHUNK])
        rot_swap = sb("rot_swap", [P, CHUNK])
        kr = sb("kr", [P, CHUNK])
        kio = sb("kio", [P, KEYS])
        ids_i = sb("ids_i", [P, TILES], I32)
        ids = sb("ids", [P, TILES])
        middle = sb("middle", [P, TILES])
        away = sb("away", [P, TILES, KEYS])
        rows_of = sb("rows_of", [P, 2])
        kv_ps, tok_ps, kr_ps = ([ctx.enter_context(nc.psum_tensor(f"k_{n}{i}", [P, 512], F32)) for i in range(2)]
                                for n in ("kv", "tok", "kr"))
        w_loaded = sem("w_loaded")
        small_loaded = sem("small_loaded")
        w_hi = sem("w_hi")
        w_split = sem("w_split")
        c_hi = sem("c_hi")
        c_split = sem("c_split")
        kv_done = sem("kv_done")
        kv_hi = sem("kv_hi")
        kv_split = sem("kv_split")
        tok_done = sem("tok_done")
        tok_hi = sem("tok_hi")
        tok_split = sem("tok_split")
        kr_done = sem("kr_done")
        rot_done = sem("rot_done")
        kr_ready = sem("kr_ready")
        kr_hi = sem("kr_hi")
        kr_split = sem("kr_split")
        ids_step = sem("ids_step")
        away_done = sem("away_done")
        mask_done = sem("mask_done")
        block = ctx.enter_context(nc.Block())

        def cols(c):
            return slice(c * CHUNK, (c + 1) * CHUNK)

        @block.sync
        def _(sp):
            sp.dma_start(w_raw[:, :, :], d["wkv"]).then_inc(w_loaded, 16)
            for n in ("cos", "sin"):
                sp.dma_start(T[n][:, :], d[n]).then_inc(small_loaded, 16)
            sp.dma_start(kio[:, :], d["kio"]).then_inc(small_loaded, 16)
            sp.dma_start(ids_i[:, :], d["ids"]).then_inc(small_loaded, 16)
            sp.dma_start(rows_of[:, :], d["rows_of"]).then_inc(small_loaded, 16)
            sp.dma_start(T["raw"][:, :, :], d["xw"][0]).then_inc(T["raw_loaded"], 16)
            sp.dma_start(T["raw_r"][:, :, :], d["xwr"][0]).then_inc(T["raw_r_loaded"], 16)
            sp.wait_ge(c_split, CHUNKS)
            sp.dma_start(X[:, :, :], x1.rearrange("(t p) n -> p t n", p=P)).then_inc(T["x1_loaded"], 16)

        @block.scalar
        def _(act):
            act.wait_ge(w_loaded, 16)
            act.activation(w[0][:, :, :], w_raw[:, :, :], ACT.Copy).then_inc(w_hi, 1)

            def context(c):
                act.wait_ge(T["context_loaded"][c], 16)
                if c >= 2:
                    act.wait_ge(kv_done, c - 1)
                act.activation(cT[c % 2][0][:, :, :], X[:, c * CT:(c + 1) * CT, :], ACT.Copy).then_inc(c_hi, 1)

            context(0)
            act.wait_ge(small_loaded, 80)
            for c in range(CHUNKS):
                if c + 1 < CHUNKS:
                    context(c + 1)
                act.wait_ge(kv_done, c + 1)
                if c >= 1:
                    act.wait_ge(tok_done, c)
                act.activation(kvf[:, :], kv_ps[c % 2][:, :], ACT.Copy)
                act.activation(T["kvT"][0][:, cols(c)], kv_ps[c % 2][:, :], ACT.Copy).then_inc(kv_hi, 1)
                act.wait_ge(ids_step, 2)
                for t in range(c * CT, (c + 1) * CT):
                    act.activation(away[:, t, :], kio[:, :], ACT.Square,
                                   bias=middle[:, t:t + 1]).then_inc(away_done, 1)
                act.wait_ge(tok_done, c + 1)
                act.activation(T["kv"][0][:, c * CT:(c + 1) * CT, :], r3(tok_ps[c % 2][:, :], P),
                               ACT.Copy).then_inc(tok_hi, 1)
                act.wait_ge(kr_ready, c + 1)
                for h in range(2):
                    act.activation(T["kr"][0][:, 2 * c:2 * c + 2, h, :], r3(kr[:, :], KEYS), ACT.Copy,
                                   scale=rows_of[:, h:h + 1]).then_inc(kr_hi, 1)

        @block.vector
        def _(dve):
            dve.wait_ge(w_hi, 1)
            dve.tensor_tensor(w[1][:, :, :], w_raw[:, :, :], w[0][:, :, :].bitcast(F32),
                              ALU.subtract).then_inc(w_split, 1)

            def context(c):
                dve.wait_ge(c_hi, c + 1)
                dve.tensor_tensor(cT[c % 2][1][:, :, :], X[:, c * CT:(c + 1) * CT, :],
                                  cT[c % 2][0][:, :, :].bitcast(F32), ALU.subtract).then_inc(c_split, 1)

            context(0)
            dve.wait_ge(small_loaded, 80)
            dve.tensor_copy(ids[:, :], ids_i[:, :]).then_inc(ids_step, 1)
            dve.wait_ge(ids_step, 1)
            dve.tensor_scalar(middle[:, :], ids[:, :], -1.0, LOOKBACK / 2.0, ALU.mult,
                              ALU.add).then_inc(ids_step, 1)

            def mask(c):
                dve.wait_ge(away_done, (c + 1) * CT)
                dve.tensor_scalar(T["mask"][:, c * CT:(c + 1) * CT, :], away[:, c * CT:(c + 1) * CT, :],
                                  (LOOKBACK / 2.0) ** 2, NEG, ALU.is_gt, ALU.mult).then_inc(mask_done, 1)

            for c in range(CHUNKS):
                if c + 1 < CHUNKS:
                    context(c + 1)
                dve.wait_ge(kv_hi, c + 1)
                dve.tensor_tensor(T["kvT"][1][:, cols(c)], kv_ps[c % 2][:, :],
                                  T["kvT"][0][:, cols(c)].bitcast(F32), ALU.subtract).then_inc(kv_split, 1)
                mask(c)
                dve.wait_ge(tok_hi, c + 1)
                dve.tensor_tensor(T["kv"][1][:, c * CT:(c + 1) * CT, :], r3(tok_ps[c % 2][:, :], P),
                                  T["kv"][0][:, c * CT:(c + 1) * CT, :].bitcast(F32),
                                  ALU.subtract).then_inc(tok_split, 1)
                dve.wait_ge(kr_done, c + 1)
                rotate(dve, T, kr_ps[c % 2], rot, rot_swap).then_inc(rot_done, 1)
                dve.wait_ge(rot_done, c + 1)
                dve.tensor_tensor(kr[:, :], rot[:, :], rot_swap[:, :], ALU.add).then_inc(kr_ready, 1)
                for h in range(2):
                    dve.wait_ge(kr_hi, 2 * c + h + 1)
                    dve.scalar_tensor_tensor(
                        out=T["kr"][1][:, 2 * c:2 * c + 2, h, :], in0=r3(kr[:, :], KEYS),
                        scalar=rows_of[:, h:h + 1], in1=T["kr"][0][:, 2 * c:2 * c + 2, h, :].bitcast(F32),
                        op0=ALU.mult, op1=ALU.subtract).then_inc(kr_split, 1)

        @block.tensor
        def _(pe):
            pe.wait_ge(w_split, 1)
            for c in range(CHUNKS):
                pe.wait_ge(c_split, c + 1)
                if c >= 2:
                    pe.wait_ge(kv_split, c - 1)
                for k in range(KD):
                    mm = mm3(pe, kv_ps[c % 2][:, :], (w[0][:, k, :], w[1][:, k, :]),
                             (cT[c % 2][0][:, k, :], cT[c % 2][1][:, k, :]), k == 0, k == KD - 1)
                mm.then_inc(kv_done, 1)
                pe.wait_ge(kv_hi, c + 1)
                if c >= 2:
                    pe.wait_ge(tok_split, c - 1)
                for t in range(CT):
                    mm = pe.transpose(tok_ps[c % 2][:, t * P:(t + 1) * P], kvf[:, t * P:(t + 1) * P],
                                      T["ident"][:, :])
                mm.then_inc(tok_done, 1)
                pe.wait_ge(kv_split, c + 1)
                if c >= 2:
                    pe.wait_ge(rot_done, c - 1)
                mm3(pe, kr_ps[c % 2][:, :], (w[0][:, KD, :], w[1][:, KD, :]),
                    (T["kvT"][0][:, cols(c)], T["kvT"][1][:, cols(c)])).then_inc(kr_done, 1)


def rotate(dve, T, ps, rot, rot_swap):
    def table(name, rows):
        return T[name][rows, :].unsqueeze(1).to_broadcast([rows.stop - rows.start, 2, KEYS])

    H = P // 2
    dve.tensor_tensor(r3(rot[:, :], KEYS), r3(ps[:, :], KEYS), table("cos", slice(0, P)), ALU.mult)
    dve.tensor_tensor(r3(rot_swap[0:H, :], KEYS), r3(ps[H:P, :], KEYS), table("sin", slice(0, H)), ALU.mult)
    return dve.tensor_tensor(r3(rot_swap[H:P, :], KEYS), r3(ps[0:H, :], KEYS), table("sin", slice(H, P)),
                             ALU.mult)


def cross_attention(nc, X, d, T):
    with ExitStack() as ctx:
        def sb(name, shape, dt=F32):
            return ctx.enter_context(nc.sbuf_tensor("x_" + name, shape, dt))

        def parts(name, shape):
            return sb(name + "_hi", shape, F32R), sb(name + "_lo", shape, F32R)

        def sem(name):
            return ctx.enter_context(nc.semaphore("x_" + name))

        def psum(name):
            return ctx.enter_context(nc.psum_tensor("x_" + name, [P, 512], F32))

        def both(pair, *index):
            return pair[0][index], pair[1][index]

        ALL = slice(None)
        UQ, UK, UV, WO = 0, 256, 384, 512
        raw, raw_r = T["raw"], T["raw_r"]
        wa = parts("wa", [P, 2, QC, P])
        wb = parts("wb", [P, 2, D])
        wr = parts("wr", [P, QC, P])
        qa = parts("qa", [P, 2, CHUNK])
        qr = parts("qr", [P, CHUNK])
        rot = sb("rot", [P, CHUNK])
        rot_swap = sb("rot_swap", [P, CHUNK])
        prob = T["prob"]
        probT = parts("probT", [P, 4, 512])
        ao = parts("ao", [P, 2, 512])
        mx = sb("mx", [P, CT, 2])
        nb = sb("nb", [P, CT, 2])
        rs = sb("rs", [P, CT, 2])
        rr = sb("rr", [P, CT, 2])
        bank = [psum("bank0"), psum("bank1")]
        s_ps = [psum("s0"), psum("s1")]
        pt_ps = [psum("pt0"), psum("pt1")]
        av_ps = [psum("av0"), psum("av1")]

        raw_loaded, raw_r_loaded = T["raw_loaded"], T["raw_r_loaded"]
        wr_hi, wr_lo, wr_split = sem("wr_hi"), sem("wr_lo"), sem("wr_split")
        a_done, a_hi, a_split = sem("a_done"), sem("a_hi"), sem("a_split")
        b_done, b_hi, b_split = sem("b_done"), sem("b_hi"), sem("b_split")
        qa_done, qa_hi, qa_split = sem("qa_done"), sem("qa_hi"), sem("qa_split")
        qr_done, rot_done, rot_sum = sem("qr_done"), sem("rot_done"), sem("rot_sum")
        qr_hi, qr_ready = sem("qr_hi"), sem("qr_ready")
        s_done, max_done, nb_done = sem("s_done"), sem("max_done"), sem("nb_done")
        exp_done, rr_done, p_ready = sem("exp_done"), sem("rr_done"), sem("p_ready")
        pt_done, pt_hi, pt_ready = sem("pt_done"), sem("pt_hi"), sem("pt_ready")
        av_done, av_hi, av_ready = sem("av_done"), sem("av_hi"), sem("av_ready")
        out_done, out_added = sem("out_done"), sem("out_added")
        lone = {n: sem("lone_" + n) for n in ("act", "dve", "pool")}
        block = ctx.enter_context(nc.Block())

        def over_steps(eng, step):
            step(0, 0, 0, True)
            with eng.Fori(0, PAIRS - 1) as p:
                for c in range(1, CHUNKS + 1):
                    step(CHUNKS * p + c, p + c // CHUNKS, c % CHUNKS, True)
            for g in range(STEPS - CHUNKS + 1, STEPS):
                step(g, PAIRS - 1, g % CHUNKS, g < STEPS - 1)

        def is_at(g, value):
            return isinstance(g, int) and g == value

        def folds_a(p, c):
            return c == 2 and not is_at(p, PAIRS - 1)

        @block.sync
        def _(sp):
            with sp.Fori(0, PAIRS - 1) as p:
                sp.wait_ge(wr_split, p + 1)
                sp.dma_start(raw_r[:, :, :], d["xwr"][p + 1]).then_inc(raw_r_loaded, 16)
                sp.wait_ge(b_done, 2 * p + 2)
                sp.dma_start(raw[:, :, :], d["xw"][p + 1]).then_inc(raw_loaded, 16)

        @block.gpsimd
        def _(pool):
            def split_wr(p):
                pool.wait_ge(raw_r_loaded, 16 * (p + 1))
                alone(pool, lone["pool"])
                pool.tensor_copy(wr[0][:, :, :], raw_r[:, :, :]).then_inc(wr_hi, 1)
                pool.wait_ge(wr_hi, p + 1)
                pool.tensor_tensor(wr[1][:, 0, :], raw_r[:, 0, :], wr[0][:, 0, :].bitcast(F32),
                                   ALU.subtract).then_inc(wr_lo, 1)
                low = wr[0][HALF:, 1, :]
                pool.wait_ge(wr_lo, p + 1)
                pool.tensor_tensor(low, raw_r[HALF:, 1, :], low.bitcast(F32), ALU.subtract).then_inc(wr_split, 1)
                pool.wait_ge(wr_split, p + 1)
                alone(pool, lone["pool"])

            def rotary(gc):
                pool.wait_ge(rot_done, gc + 1)
                pool.tensor_tensor(rot[:, :], rot[:, :], rot_swap[:, :], ALU.add).then_inc(rot_sum, 1)
                pool.wait_ge(qr_hi, gc + 1)
                pool.tensor_tensor(qr[1][:, :], rot[:, :], qr[0][:, :].bitcast(F32),
                                   ALU.subtract).then_inc(qr_ready, 1)

            def step(g, p, c, nxt):
                for t in range(CT):
                    pool.wait_ge(rr_done, 4 * g + t + 1)
                    pool.tensor_tensor(prob[:, t], prob[:, t],
                                       rr[:, t, :].unsqueeze(2).to_broadcast([P, 2, KEYS]),
                                       ALU.mult).then_inc(p_ready, 1)
                if nxt:
                    rotary(g + 1)
                if folds_a(p, c):
                    split_wr(p + 1)

            split_wr(0)
            rotary(0)
            over_steps(pool, step)

        @block.scalar
        def _(act):
            def fold_a(p):
                act.wait_ge(a_done, p + 1)
                act.activation(wa[0][:, :, :, :].rearrange("p h k n -> p (h k n)"), av_ps[1][:, :],
                               ACT.Copy).then_inc(a_hi, 1)

            def queries(gc):
                for h in range(2):
                    act.wait_ge(qa_done, 2 * gc + h + 1)
                    act.activation(qa[0][:, h], bank[h][:, :], ACT.Copy).then_inc(qa_hi, 1)

            def rotary(gc):
                act.wait_ge(rot_sum, gc + 1)
                act.activation(qr[0][:, :], rot[:, :], ACT.Copy).then_inc(qr_hi, 1)

            def step(g, p, c, nxt):
                for t in range(CT):
                    act.wait_ge(nb_done, 4 * g + t + 1)
                    for h in range(2):
                        ins = act.activation(prob[:, t, h, :], prob[:, t, h, :], ACT.Exp,
                                             bias=nb[:, t, h:h + 1], scale=X_SCALE,
                                             accum_out=rs[:, t, h:h + 1])
                    ins.then_inc(exp_done, 1)
                if nxt:
                    queries(g + 1)
                if folds_a(p, c):
                    fold_a(p + 1)
                for i in range(4):
                    act.wait_ge(pt_done, 4 * g + i + 1)
                    act.activation(probT[0][:, i], pt_ps[i % 2][:, :], ACT.Copy).then_inc(pt_hi, 1)
                    if i == 1 and nxt:
                        rotary(g + 1)
                for b in range(2):
                    act.wait_ge(av_done, 2 * g + b + 1)
                    act.activation(ao[0][:, b], av_ps[b][:, :], ACT.Copy).then_inc(av_hi, 1)
                if c == 0:
                    for h in range(2):
                        act.wait_ge(b_done, 2 * p + h + 1)
                        act.activation(wb[0][:, h], bank[h][:, :], ACT.Copy).then_inc(b_hi, 1)

            fold_a(0)
            queries(0)
            rotary(0)
            over_steps(act, step)

        @block.vector
        def _(dve):
            def fold_a(p):
                dve.wait_ge(a_hi, p + 1)
                folded = av_ps[1][:, :].rearrange("p (h k n) -> p h k n", h=2, k=QC)
                dve.tensor_tensor(wa[1][:, :, 0, :], folded[:, :, 0, :], wa[0][:, :, 0, :].bitcast(F32),
                                  ALU.subtract)
                low = wa[0][HALF:, :, 1, :]
                dve.tensor_tensor(low, folded[HALF:, :, 1, :], low.bitcast(F32), ALU.subtract).then_inc(a_split, 1)

            def queries(gc):
                for h in range(2):
                    dve.wait_ge(qa_hi, 2 * gc + h + 1)
                    dve.tensor_tensor(qa[1][:, h], bank[h][:, :], qa[0][:, h].bitcast(F32),
                                      ALU.subtract).then_inc(qa_split, 1)

            def rotary(gc):
                dve.wait_ge(qr_done, gc + 1)
                if not is_at(gc, 0):
                    dve.wait_ge(qr_ready, gc)
                rotate(dve, T, av_ps[0], rot, rot_swap).then_inc(rot_done, 1)

            def reciprocal(g, t):
                dve.wait_ge(exp_done, 4 * g + t + 1)
                dve.reciprocal(rr[:, t, :], rs[:, t, :]).then_inc(rr_done, 1)

            def output(m, c, tiles):
                for j in tiles:
                    dve.wait_ge(out_done, 4 * m + j + 1)
                    dve.tensor_tensor(X[:, c * CT + j, :], bank[j % 2][:, :], X[:, c * CT + j, :],
                                      ALU.add).then_inc(out_added, 1)

            def step(g, p, c, nxt):
                before = (c - 1) % CHUNKS
                for t in range(CT):
                    dve.wait_ge(s_done, 4 * g + t + 1)
                    alone(dve, lone["dve"])
                    for h in range(2):
                        ins = dve.tensor_tensor_reduce(prob[:, t, h, :], s_ps[t % 2][:, h * KEYS:(h + 1) * KEYS],
                                                       T["mask"][:, c * CT + t, :], 1.0, -3e38, ALU.add,
                                                       ALU.max, mx[:, t, h:h + 1])
                    ins.then_inc(max_done, 1)
                    dve.wait_ge(max_done, 4 * g + t + 1)
                    dve.tensor_scalar(nb[:, t, :], mx[:, t, :], -X_SCALE, None, ALU.mult).then_inc(nb_done, 1)
                    if t:
                        reciprocal(g, t - 1)
                reciprocal(g, CT - 1)
                if nxt:
                    queries(g + 1)
                if folds_a(p, c):
                    fold_a(p + 1)
                if nxt:
                    rotary(g + 1)
                for b in range(2):
                    for i in (2 * b, 2 * b + 1):
                        dve.wait_ge(pt_hi, 4 * g + i + 1)
                        dve.tensor_tensor(probT[1][:, i], pt_ps[i % 2][:, :], probT[0][:, i].bitcast(F32),
                                          ALU.subtract).then_inc(pt_ready, 1)
                    if not is_at(g, 0):
                        output(g - 1, before, (2 * b, 2 * b + 1))
                for b in range(2):
                    dve.wait_ge(av_hi, 2 * g + b + 1)
                    dve.tensor_tensor(ao[1][:, b], av_ps[b][:, :], ao[0][:, b].bitcast(F32),
                                      ALU.subtract).then_inc(av_ready, 1)
                if c == 0:
                    for h in range(2):
                        dve.wait_ge(b_hi, 2 * p + h + 1)
                        dve.tensor_tensor(wb[1][:, h], bank[h][:, :], wb[0][:, h].bitcast(F32),
                                          ALU.subtract).then_inc(b_split, 1)

            fold_a(0)
            queries(0)
            rotary(0)
            dve.wait_ge(T["x1_loaded"], 16)
            over_steps(dve, step)
            output(STEPS - 1, CHUNKS - 1, range(CT))

        @block.tensor
        def _(pe):
            def fold_a(p):
                pe.wait_ge(raw_loaded, 16 * (p + 1))
                for h in range(2):
                    for k in range(QC):
                        at = (2 * h + k) * P
                        mm = pe.matmul(av_ps[1][:, at:at + P], raw[:, h, UQ + k * P:UQ + (k + 1) * P],
                                       raw[:, h, UK:UK + P], start=True, stop=True)
                mm.then_inc(a_done, 1)

            def fold_b(g, p):
                for h in range(2):
                    if is_at(g, 0):
                        pe.wait_ge(qa_split, 2 + h + 1)
                    else:
                        pe.wait_ge(out_added, 4 * g + h - 1)
                    pe.matmul(bank[h][:, :], raw[:, h, UV:UV + P], raw[:, h, WO:WO + D],
                              start=True, stop=True).then_inc(b_done, 1)

            def short_chunk(out, weight, tok):
                pe.matmul(out[:, :], weight, T["qc"][0][:, 1, tok], start=False, stop=False)
                return pe.matmul(out[:, :], weight[:HALF], T["qc"][1][:HALF, 1, tok], start=False, stop=True)

            def queries(c, h):
                tok = slice(c * CHUNK, (c + 1) * CHUNK)
                mm3(pe, bank[h][:, :], both(wa, ALL, h, 0), both(T["qc"], ALL, 0, tok), True, False)
                short_chunk(bank[h], wa[0][:, h, 1, :], tok).then_inc(qa_done, 1)

            def rotary(c):
                tok = slice(c * CHUNK, (c + 1) * CHUNK)
                mm3(pe, av_ps[0][:, :], both(wr, ALL, 0), both(T["qc"], ALL, 0, tok), True, False)
                short_chunk(av_ps[0], wr[0][:, 1, :], tok).then_inc(qr_done, 1)

            def turn(g, b, start):
                for i in (2 * b, 2 * b + 1):
                    pe.wait_ge(p_ready, 4 * g + 2 * b + 2)
                    if not (start and i < 2):
                        pe.wait_ge(pt_ready, 4 * g + i - 1)
                    for h in range(2):
                        for t in range(2):
                            at = h * 256 + t * P
                            key = slice(i % 2 * P, (i % 2 + 1) * P)
                            mm = pe.transpose(pt_ps[i % 2][:, at:at + P], prob[:, 2 * b + t, h, key],
                                              T["ident"][:, :])
                    mm.then_inc(pt_done, 1)

            def output(m, p, free, tiles):
                pe.wait_ge(av_ready, 2 * m + 2)
                pe.wait_ge(b_split, 2 * p + 2)
                for j in tiles:
                    if j < 2:
                        free(j)
                    else:
                        pe.wait_ge(out_added, 4 * m + j - 1)
                    for h in range(2):
                        at = h * 256 + j % 2 * P
                        mm = mm3(pe, bank[j % 2][:, :], both(ao, ALL, j // 2, slice(at, at + P)),
                                 both(wb, ALL, h), h == 0, h == 1)
                    mm.then_inc(out_done, 1)

            def step(g, p, c, nxt):
                start = is_at(g, 0)
                pe.wait_ge(qa_split, 2 * g + 2)
                pe.wait_ge(qr_ready, g + 1)
                for t in range(CT):
                    if not (start and t < 2):
                        pe.wait_ge(max_done, 4 * g + t - 1)
                    seq = 2 * c + t // 2
                    tok = slice(t * P, (t + 1) * P)
                    mm3(pe, s_ps[t % 2][:, :], both(qr, ALL, tok),
                        [x[:, seq].rearrange("p h k -> p (h k)") for x in T["kr"]], True, False)
                    for h in range(2):
                        mm = mm3(pe, s_ps[t % 2][:, h * KEYS:(h + 1) * KEYS], both(qa, ALL, h, tok),
                                 both(T["kvT"], ALL, slice(seq * KEYS, (seq + 1) * KEYS)), False, h == 1)
                    mm.then_inc(s_done, 1)
                if nxt:
                    next_c = (c + 1) % CHUNKS
                    pe.wait_ge(a_split, (p + 2 if c == 3 else p + 1))
                    for h in range(2):
                        if start:
                            pe.wait_ge(qa_split, h + 1)
                        elif c == 1:
                            pe.wait_ge(b_split, 2 * p + h + 1)
                        else:
                            pe.wait_ge(out_added, 4 * g - 5 + h)
                        queries(next_c, h)
                    pe.wait_ge(wr_split, (p + 2 if c == 3 else p + 1))
                    if start:
                        pe.wait_ge(rot_done, 1)
                    else:
                        pe.wait_ge(av_ready, 2 * g - 1)
                    rotary(next_c)
                if folds_a(p, c):
                    pe.wait_ge(av_ready, 2 * g)
                    fold_a(p + 1)
                def free(j):
                    if nxt:
                        pe.wait_ge(qa_split, 2 * g + 2 + j + 1)
                    else:
                        pe.wait_ge(out_added, 4 * g - 5 + j)

                for b in range(2):
                    turn(g, b, start)
                    if not start:
                        output(g - 1, (p - 1 if c == 0 else p), free, (2 * b, 2 * b + 1))
                for b in range(2):
                    if not start:
                        pe.wait_ge(av_ready, 2 * g - 1 + b)
                    if b == 0 and nxt:
                        pe.wait_ge(rot_done, g + 2)
                    if b == 1 and folds_a(p, c):
                        pe.wait_ge(a_split, p + 2)
                    pe.wait_ge(pt_ready, 4 * g + 2 * b + 2)
                    for k in range(2):
                        mm = mm3(pe, av_ps[b][:, :], both(T["kv"], ALL, 4 * c + 2 * b + k),
                                 both(probT, ALL, 2 * b + k), k == 0, k == 1)
                    mm.then_inc(av_done, 1)
                if c == 0:
                    fold_b(g, p)

            fold_a(0)
            pe.wait_ge(a_split, 1)
            queries(0, 0)
            queries(0, 1)
            pe.wait_ge(wr_split, 1)
            rotary(0)
            over_steps(pe, step)
            output(STEPS - 1, PAIRS - 1, lambda j: pe.wait_ge(out_added, 4 * STEPS - 5 + j), range(CT))


FF = 1024
KF = FF // P
QMAX = 127.0
MAGIC = 1.5 * 2.0 ** 23
H_IN = float(np.float32(1.0) / np.sqrt(np.float32(D)))
H_MID = float(np.float32(1.0) / np.sqrt(np.float32(FF)))


def ternary_weights(nc, X, d, F):
    with ExitStack() as ctx:
        def sb(name, shape, dt=F32):
            return ctx.enter_context(nc.sbuf_tensor("w_" + name, shape, dt))

        def sem(name):
            return ctx.enter_context(nc.semaphore("w_" + name))

        N = D * FF // P
        S = statistics(nc, ctx, "l3_", F["mv"], F["rstd"])
        raw = [sb("up_raw", [P, N]), sb("down_raw", [P, N])]
        h_raw = sb("h_raw", [P, KD * D])
        scratch = sb("scratch", [P, 2, N])
        ones = sb("ones", [P, P])
        magic = F["magic"]
        PARTS = 4
        sums = sb("sums", [P, 2, PARTS])
        inverse = sb("inverse", [P, 2])
        total_ps = ctx.enter_context(nc.psum_tensor("w_total", [P, 2, PARTS], F32))
        total = sb("total_sum", [P, 2])
        loaded = [[sem(f"{n}_loaded{j}") for j in range(PARTS)] for n in ("up", "down")]
        h_loaded = sem("h_loaded")
        h_copied = sem("h_copied")
        const_ready = sem("const_ready")
        summed = sem("summed")
        total_done = sem("total_done")
        added = sem("added")
        shift_done = sem("shift_done")
        mean_done = sem("mean_done")
        inverse_done = sem("inverse_done")
        rounded = sem("rounded")
        clipped = sem("clipped")
        written = sem("written")
        block = ctx.enter_context(nc.Block())
        PIECE = N // PARTS
        pieces = [(i, j, slice(j * PIECE, (j + 1) * PIECE)) for i in range(2) for j in range(PARTS)]

        @block.sync
        def _(sp):
            sp.dma_start(h_raw[:, :], d["hadamard"]).then_inc(h_loaded, 16)
            for i, j, part in pieces:
                sp.dma_start(raw[i][:, part], (d["up"], d["down"])[i][:, part]).then_inc(loaded[i][j], 16)

        @block.gpsimd
        def _(pool):
            pool.memset(ones[:, :], 1.0).then_inc(const_ready, 1)
            pool.memset(magic[:, :], MAGIC).then_inc(const_ready, 1)

        @block.scalar
        def _(act):
            act.wait_ge(h_loaded, 16)
            act.activation(F["h"][:, :], h_raw[:, :], ACT.Copy).then_inc(h_copied, 1)
            root(act, S, 0, 1)
            for i, j, part in pieces:
                act.wait_ge(loaded[i][j], 16)
                act.activation(scratch[:, i, part], raw[i][:, part], ACT.Abs,
                               accum_out=sums[:, i, j:j + 1]).then_inc(summed, 1)
            for i, j, part in pieces:
                act.wait_ge(inverse_done, 1)
                act.wait_ge(const_ready, 2)
                act.activation(raw[i][:, part], raw[i][:, part], ACT.Identity, scale=inverse[:, i:i + 1],
                               bias=magic[:, 0:1]).then_inc(rounded, 1)

        @block.vector
        def _(dve):
            moments(dve, X, S, None, 0, 1)
            inverse_root(dve, S, 0, 1)
            dve.scalar_tensor_tensor(out=F["shift"][:, :], in0=F["mv"][:, :, 0], scalar=-1.0, in1=F["rstd"][:, :],
                                     op0=ALU.mult, op1=ALU.mult).then_inc(shift_done, 1)
            dve.wait_ge(total_done, 1)
            dve.tensor_reduce(total[:, :], total_ps[:, :, :], AX.X, ALU.add).then_inc(added, 1)
            dve.wait_ge(added, 1)
            dve.tensor_scalar(F["scale_w"][:, :], total[:, :], 1.0 / (D * FF), 1e-5, ALU.mult,
                              ALU.max).then_inc(mean_done, 1)
            dve.wait_ge(mean_done, 1)
            dve.reciprocal(inverse[:, :], F["scale_w"][:, :]).then_inc(inverse_done, 1)
            for n, (i, j, part) in enumerate(pieces):
                dve.wait_ge(rounded, n + 1)
                dve.tensor_scalar(F["t"][i][:, part], raw[i][:, part], -MAGIC, 1.0, ALU.add,
                                  ALU.min).then_inc(clipped, 1)
                dve.wait_ge(clipped, n + 1)
                dve.tensor_scalar(F["t"][i][:, part], F["t"][i][:, part], -1.0, None,
                                  ALU.max).then_inc(written, 1)

        @block.tensor
        def _(pe):
            pe.wait_ge(const_ready, 2)
            pe.wait_ge(summed, 2 * PARTS)
            pe.matmul(total_ps[:, :, :], ones[:, :], sums[:, :, :], start=True, stop=True).then_inc(total_done, 1)


def feed_forward(nc, X, d, F, ident, out):
    with ExitStack() as ctx:
        def sb(name, shape, dt=F32):
            return ctx.enter_context(nc.sbuf_tensor("f_" + name, shape, dt))

        def sem(name):
            return ctx.enter_context(nc.semaphore("f_" + name))

        def psum(name, shape=(P, 512), dt=F32):
            return ctx.enter_context(nc.psum_tensor("f_" + name, list(shape), dt))

        ident_b = sb("ident_b", [P, P], BF16)
        xn = sb("xn", [P, D])
        xt = [sb("xt_" + n, [P, D], F32R) for n in ("hi", "lo")]
        y = sb("y", [P, D])
        xq = sb("xq", [P, D], BF16)
        GT = 2
        GROUPS = TILES // GT
        M = 4
        xqT = sb("xqT", [P, KD, GT * P], BF16)
        amax = sb("amax", [P, 1])
        bound = sb("bound", [P, TILES])
        rec = sb("rec", [P, 1])
        factor = sb("factor", [P, 1])
        sq, sums, v = (sb(n, [P, M, 512]) for n in ("sq", "sums", "v"))
        u = [sb("u_" + n, [P, M, 512], F32R) for n in ("hi", "lo")]
        amax2 = sb("amax2", [P, 2])
        unit = sb("unit", [P, 1])
        gain = sb("gain", [P, 1])
        top = sb("top", [P, 1])
        bound2 = sb("bound2", [P, 1])
        rec2 = sb("rec2", [P, 1])
        factor2 = sb("factor2", [P, 1])
        back = sb("back", [P, 2])
        y2 = sb("y2", [P, FF])
        q2 = sb("q2", [P, FF], BF16)
        q2T = sb("q2T", [P, KF, P], BF16)
        result = [sb(f"result{i}", [P, D]) for i in range(2)]
        t_ps, h_ps, down_ps = psum("t_ps"), psum("h_ps"), psum("down_ps")
        turn2_ps = psum("turn2_ps", (P, FF), BF16)
        up_ps = [psum(f"up_ps{i}") for i in range(2)]
        w_ps = [psum(f"w_ps{i}") for i in range(2)]
        turned_view = h_ps[:, 0:D // 2].bitcast(BF16)

        id_ready = sem("id_ready")
        xn_ready, t_done, t_hi, t_split = sem("xn_ready"), sem("t_done"), sem("t_hi"), sem("t_split")
        h_done, amax_done, bound_done = sem("h_done"), sem("amax_done"), sem("bound_done")
        rec_done, factor_done, y_done = sem("rec_done"), sem("factor_done"), sem("y_done")
        clip_done, xq_ready, turned, xq_copied = sem("clip_done"), sem("xq_ready"), sem("turned"), sem("xq_copied")
        up_done, relu_done, square_done = sem("up_done"), sem("relu_done"), sem("square_done")
        sums_done = [sem(f"sums_done{i}") for i in range(2)]
        v_done = [sem(f"v_done{i}") for i in range(2)]
        u_ready = [sem(f"u_ready{i}") for i in range(2)]
        u_hi, w_done = sem("u_hi"), sem("w_done")
        small = sem("small")
        factor2_done, y2_done, clip2_done = sem("factor2_done"), sem("y2_done"), sem("clip2_done")
        q2_ready, turned2, q2_copied = sem("q2_ready"), sem("turned2"), sem("q2_copied")
        down_done, result_ready = sem("down_done"), sem("result_ready")
        stored = [sem(f"stored{i}") for i in range(2)]
        lone = {n: sem("lone_" + n) for n in ("dve", "pool")}
        block = ctx.enter_context(nc.Block())
        h3 = F["h"][:, :].rearrange("p (k n) -> p k n", k=KD)
        up3 = F["t"][0][:, :].rearrange("p (k n) -> p k n", k=KD)
        down3 = F["t"][1][:, :].rearrange("p (k n) -> p k n", k=KF)

        def is_at(g, value):
            return isinstance(g, int) and g == value

        def tile_of_X(s):
            return X[:, bass.ds(s, 1), :].rearrange("p a n -> p (a n)")

        def over_windows(eng, T, H1, H2, Q, U, V, S, W, R1, R2, D1, D2):

            def window(n, down, second, up, first, after):
                a, s, b = GT * n + 2 * GT, GT * n, GT * n - GT
                if up:
                    U(n + 1, 0)
                if first:
                    H1(a, 0)
                if down:
                    D1(b, 0)
                if first:
                    T(a + 1)
                    H2(a, 0)
                if up:
                    U(n + 1, 1)
                if down:
                    D2(b, 0, n - 1)
                if up:
                    V(n + 1)
                if first:
                    Q(a, 0)
                if down:
                    D1(b + 1, 1)
                if second:
                    W(s, 0, n)
                    R1(s, 0)
                if first:
                    H1(a + 1, 1)
                if second:
                    R2(s, 0)
                if first:
                    H2(a + 1, 1)
                if down:
                    D2(b + 1, 1, n - 1)
                if after:
                    T(a + 2)
                if second:
                    W(s + 1, 1, n)
                    R1(s + 1, 1)
                if first:
                    Q(a + 1, 1)
                if up:
                    S(n + 1)
                if second:
                    R2(s + 1, 1)

            def edge(n):
                window(n, n >= 1, 0 <= n < GROUPS, n + 1 < GROUPS, n + 2 < GROUPS, n + 3 < GROUPS)

            T(0)
            for i in range(GT):
                H1(i, i)
                H2(i, i)
                T(i + 1)
                Q(i, i)
            for n in (-1, 0, 1):
                edge(n)
            with eng.Fori(2, GROUPS - 3) as n:
                window(n, True, True, True, True, True)
            for n in range(GROUPS - 3, GROUPS + 1):
                edge(n)

        def nothing(*_):
            pass

        @block.sync
        def _(sp):
            rows = out.rearrange("(s p) n -> s p n", p=P)
            with sp.Fori(0, TILES // 2) as it:
                for i in range(2):
                    sp.wait_ge(result_ready, 2 * it + i + 1)
                    sp.dma_start(rows[2 * it + i], result[i][:, :]).then_inc(stored[i], 16)
            for i in range(2):
                sp.wait_ge(stored[i], 16 * TILES // 2)

        @block.gpsimd
        def _(pool):
            pool.tensor_copy(ident_b[:, :], ident[:, :]).then_inc(id_ready, 1)

            def U(n, half):
                if half == 0:
                    if not is_at(n, 0):
                        pool.wait_ge(v_done[0], n)
                    pool.wait_ge(square_done, M * n + 2)
                    alone(pool, lone["pool"])
                    pool.tensor_tensor(sums[:, 0], sq[:, 0], sq[:, 1], ALU.add)
                    pool.tensor_tensor(sums[:, 1], sq[:, 0], sq[:, 1], ALU.subtract).then_inc(sums_done[0], 1)

            def V(n):
                pool.wait_ge(sums_done[0], n + 1)
                pool.wait_ge(sums_done[1], n + 1)
                alone(pool, lone["pool"])
                pool.tensor_tensor(v[:, 2:4], sums[:, 0:2], sums[:, 2:4], ALU.subtract).then_inc(v_done[1], 1)

            def S(n):
                pool.wait_ge(u_hi, 2 * n + 2)
                alone(pool, lone["pool"])
                pool.tensor_tensor(u[1][:, 2:4], v[:, 2:4], u[0][:, 2:4].bitcast(F32),
                                   ALU.subtract).then_inc(u_ready[1], 1)

            over_windows(pool, nothing, nothing, nothing, nothing, U, V, S, nothing, nothing, nothing,
                         nothing, nothing)

        @block.scalar
        def _(act):
            def normalize(s):
                act.activation(xn[:, :], tile_of_X(s), ACT.Identity, scale=F["rstd"][:, bass.ds(s, 1)],
                               bias=F["shift"][:, bass.ds(s, 1)]).then_inc(xn_ready, 1)

            def T(s):
                if is_at(s, 0):
                    normalize(s)
                act.wait_ge(t_done, s + 1)
                act.activation(xt[0][:, :], t_ps[:, :], ACT.Copy).then_inc(t_hi, 1)
                if not is_at(s, TILES - 1):
                    normalize(s + 1)

            def H2(s, i):
                if not is_at(s, 0):
                    act.wait_ge(xq_ready, s)
                act.wait_ge(factor_done, s + 1)
                act.activation(y[:, :], h_ps[:, :], ACT.Identity, scale=factor[:, 0:1],
                               bias=F["magic"][:, 0:1]).then_inc(y_done, 1)

            def Q(s, i):
                act.wait_ge(turned, s + 1)
                act.activation(xqT[:, :, i * P:(i + 1) * P], r3(turned_view, P), ACT.Copy).then_inc(xq_copied, 1)

            def U(n, half):
                blocks = (2 * half, 2 * half + 1)
                for m in blocks:
                    act.wait_ge(up_done, M * n + m + 1)
                    if not is_at(n, 0):
                        act.wait_ge(sums_done[half], n)
                    act.activation(sq[:, m], up_ps[m % 2][:, :], ACT.Relu).then_inc(relu_done, 1)
                for m in blocks:
                    act.wait_ge(relu_done, M * n + m + 1)
                    act.activation(sq[:, m], sq[:, m], ACT.Square).then_inc(square_done, 1)

            def S(n):
                if not is_at(n, 0):
                    act.wait_ge(w_done, 2 * GT * n)
                for half in range(2):
                    act.wait_ge(v_done[half], n + 1)
                    act.activation(u[0][:, 2 * half:2 * half + 2], v[:, 2 * half:2 * half + 2],
                                   ACT.Copy).then_inc(u_hi, 1)

            def R2(s, i):
                if not is_at(s, 0):
                    act.wait_ge(q2_ready, s)
                act.wait_ge(factor2_done, s + 1)
                for j in range(2):
                    ins = act.activation(y2[:, j * 512:(j + 1) * 512], w_ps[j][:, :], ACT.Identity,
                                         scale=factor2[:, 0:1], bias=F["magic"][:, 0:1])
                ins.then_inc(y2_done, 1)

            def D1(s, i):
                act.wait_ge(turned2, s + 1)
                if not is_at(s, 0):
                    act.wait_ge(down_done, s)
                act.activation(q2T[:, :, :], r3(turn2_ps[:, :], P), ACT.Copy).then_inc(q2_copied, 1)

            over_windows(act, T, nothing, H2, Q, U, nothing, S, nothing, nothing, R2, D1, nothing)

        @block.vector
        def _(dve):
            def T(s):
                dve.wait_ge(t_hi, s + 1)
                dve.tensor_tensor(xt[1][:, :], t_ps[:, :], xt[0][:, :].bitcast(F32),
                                  ALU.subtract).then_inc(t_split, 1)

            def H1(s, i):
                dve.wait_ge(h_done, s + 1)
                dve.tensor_reduce(amax[:, :], h_ps[:, :], AX.X, ALU.max,
                                  apply_absolute_value=True).then_inc(amax_done, 1)
                dve.wait_ge(amax_done, s + 1)
                dve.tensor_scalar(bound[:, bass.ds(s, 1)], amax[:, :], H_IN, 1e-5, ALU.mult,
                                  ALU.max).then_inc(bound_done, 1)
                dve.wait_ge(bound_done, s + 1)
                alone(dve, lone["dve"])
                dve.reciprocal(rec[:, :], bound[:, bass.ds(s, 1)]).then_inc(rec_done, 1)
                dve.wait_ge(rec_done, s + 1)
                dve.tensor_scalar(factor[:, :], rec[:, :], QMAX * H_IN, None, ALU.mult).then_inc(factor_done, 1)

            def H2(s, i):
                if not is_at(s, 0):
                    dve.wait_ge(turned, s)
                dve.wait_ge(y_done, s + 1)
                dve.tensor_scalar(xq[:, :], y[:, :], -MAGIC, QMAX, ALU.add, ALU.min).then_inc(clip_done, 1)
                dve.wait_ge(clip_done, s + 1)
                dve.tensor_scalar(xq[:, :], xq[:, :], -QMAX, None, ALU.max).then_inc(xq_ready, 1)

            def V(n):
                dve.wait_ge(square_done, M * n + M)
                if not is_at(n, 0):
                    dve.wait_ge(v_done[1], n)
                dve.tensor_tensor(sums[:, 2], sq[:, 2], sq[:, 3], ALU.add)
                dve.tensor_tensor(sums[:, 3], sq[:, 2], sq[:, 3], ALU.subtract).then_inc(sums_done[1], 1)
                dve.wait_ge(sums_done[0], n + 1)
                dve.wait_ge(sums_done[1], n + 1)
                dve.tensor_tensor(v[:, 0:2], sums[:, 0:2], sums[:, 2:4], ALU.add).then_inc(v_done[0], 1)

            def S(n):
                dve.wait_ge(u_hi, 2 * n + 1)
                dve.tensor_tensor(u[1][:, 0:2], v[:, 0:2], u[0][:, 0:2].bitcast(F32),
                                  ALU.subtract).then_inc(u_ready[0], 1)

            def R1(s, i):
                dve.tensor_scalar(unit[:, :], bound[:, bass.ds(s, 1)], F["scale_w"][:, 0:1], 1.0 / QMAX,
                                  ALU.mult, ALU.mult).then_inc(small, 1)
                dve.wait_ge(small, 6 * s + 1)
                dve.tensor_scalar(gain[:, :], unit[:, :], unit[:, 0:1], H_MID, ALU.mult, ALU.mult).then_inc(small, 1)
                for j in range(2):
                    dve.wait_ge(w_done, 2 * s + j + 1)
                    ins = dve.tensor_reduce(amax2[:, j:j + 1], w_ps[j][:, :], AX.X, ALU.max,
                                            apply_absolute_value=True)
                ins.then_inc(small, 1)
                dve.wait_ge(small, 6 * s + 3)
                dve.tensor_scalar(top[:, :], amax2[:, 0:1], amax2[:, 1:2], gain[:, 0:1], ALU.max,
                                  ALU.mult).then_inc(small, 1)
                dve.wait_ge(small, 6 * s + 4)
                dve.tensor_scalar(bound2[:, :], top[:, :], 1e-5, None, ALU.max).then_inc(small, 1)
                dve.wait_ge(small, 6 * s + 5)
                dve.reciprocal(rec2[:, :], bound2[:, :]).then_inc(small, 1)
                dve.tensor_scalar(back[:, i % 2:i % 2 + 1], bound2[:, :], F["scale_w"][:, 1:2], 1.0 / QMAX,
                                  ALU.mult, ALU.mult)
                dve.wait_ge(small, 6 * s + 6)
                dve.tensor_scalar(factor2[:, :], rec2[:, :], gain[:, 0:1], QMAX, ALU.mult,
                                  ALU.mult).then_inc(factor2_done, 1)

            def R2(s, i):
                if not is_at(s, 0):
                    dve.wait_ge(turned2, s)
                dve.wait_ge(y2_done, s + 1)
                dve.tensor_scalar(q2[:, :], y2[:, :], -MAGIC, QMAX, ALU.add, ALU.min).then_inc(clip2_done, 1)
                dve.wait_ge(clip2_done, s + 1)
                dve.tensor_scalar(q2[:, :], q2[:, :], -QMAX, None, ALU.max).then_inc(q2_ready, 1)

            def D2(s, i, n):
                if not is_at(n, 0):
                    dve.wait_ge(stored[i], 16 * n)
                dve.wait_ge(down_done, s + 1)
                dve.scalar_tensor_tensor(out=result[i % 2][:, :], in0=down_ps[:, :],
                                         scalar=back[:, i % 2:i % 2 + 1], in1=tile_of_X(s),
                                         op0=ALU.mult, op1=ALU.add).then_inc(result_ready, 1)

            over_windows(dve, T, H1, H2, nothing, nothing, V, S, nothing, R1, R2, nothing, D2)

        @block.tensor
        def _(pe):
            pe.wait_ge(id_ready, 1)

            def T(s):
                pe.wait_ge(xn_ready, s + 1)
                if not is_at(s, 0):
                    pe.wait_ge(t_split, s)
                for k in range(KD):
                    mm = pe.transpose(t_ps[:, k * P:(k + 1) * P], xn[:, k * P:(k + 1) * P], ident[:, :])
                mm.then_inc(t_done, 1)

            def H1(s, i):
                pe.wait_ge(t_split, s + 1)
                if not is_at(s, 0):
                    pe.wait_ge(xq_copied, s)
                for k in range(KD):
                    for part in range(2):
                        mm = pe.matmul(h_ps[:, :], xt[part][:, k * P:(k + 1) * P], h3[:, k, 0:D],
                                       start=(k == 0 and part == 0), stop=(k == KD - 1 and part == 1))
                mm.then_inc(h_done, 1)

            def Q(s, i):
                pe.wait_ge(xq_ready, s + 1)
                for k in range(KD):
                    mm = pe.transpose(turned_view[:, k * P:(k + 1) * P], xq[:, k * P:(k + 1) * P], ident_b[:, :])
                mm.then_inc(turned, 1)

            def U(n, half):
                pe.wait_ge(xq_copied, GT * n + GT)
                for m in (2 * half, 2 * half + 1):
                    if not (is_at(n, 0) and m < 2):
                        pe.wait_ge(relu_done, M * n + m - 1)
                    for j in range(2):
                        o = 2 * m + j
                        for k in range(KD):
                            mm = pe.matmul(up_ps[m % 2][:, j * 256:(j + 1) * 256], up3[:, k, o * P:(o + 1) * P],
                                           xqT[:, k, :], start=(k == 0), stop=(k == KD - 1))
                    mm.then_inc(up_done, 1)

            def W(s, i, n):
                for half in range(2):
                    pe.wait_ge(u_ready[half], n + 1)
                if not is_at(s, 0):
                    pe.wait_ge(y2_done, s)
                for m in range(M):
                    for k in range(2):
                        for part in range(2):
                            at = k * 256 + i * P
                            mm = pe.matmul(w_ps[m // 2][:, m % 2 * 256:(m % 2 + 1) * 256],
                                           u[part][:, m, at:at + P], h3[:, k, 0:256],
                                           start=(k == 0 and part == 0), stop=(k == 1 and part == 1))
                    if m % 2:
                        mm.then_inc(w_done, 1)

            def D1(s, i):
                pe.wait_ge(q2_ready, s + 1)
                if not is_at(s, 0):
                    pe.wait_ge(q2_copied, s)
                for k in range(KF):
                    mm = pe.transpose(turn2_ps[:, k * P:(k + 1) * P], q2[:, k * P:(k + 1) * P], ident_b[:, :])
                mm.then_inc(turned2, 1)

            def D2(s, i, n):
                pe.wait_ge(q2_copied, s + 1)
                if not is_at(s, 0):
                    pe.wait_ge(result_ready, s)
                for k in range(KF):
                    mm = pe.matmul(down_ps[:, :], q2T[:, k, :], down3[:, k, :], start=(k == 0), stop=(k == KF - 1))
                mm.then_inc(down_done, 1)

            over_windows(pe, T, H1, nothing, Q, U, nothing, nothing, W, nothing, nothing, D1, D2)


def decoder_layer(nc, d, out):
    attT = nc.dram_tensor("attT", (STEPS, P, 2, CHUNK), F32, kind="Internal").ap()
    x1 = nc.dram_tensor("x1", (TOKENS, D), F32, kind="Internal").ap()
    with ExitStack() as ctx:
        X = ctx.enter_context(nc.sbuf_tensor("X", [P, TILES, D], F32))
        ident = ctx.enter_context(nc.sbuf_tensor("ident", [P, P], F32))
        LOADS = 4
        x_loaded = [ctx.enter_context(nc.semaphore(f"x_loaded{i}")) for i in range(LOADS)]
        consts_loaded = ctx.enter_context(nc.semaphore("consts_loaded"))
        head_loaded = [ctx.enter_context(nc.semaphore(f"head_loaded{i}")) for i in range(2)]
        head_raw = [ctx.enter_context(nc.sbuf_tensor(f"head_raw{i}", [P, TOKENS], F32)) for i in range(2)]
        context_loaded = [ctx.enter_context(nc.semaphore(f"context_loaded{c}")) for c in range(CHUNKS)]

        with ExitStack() as phase:
            w_raw = {n: phase.enter_context(nc.sbuf_tensor("raw_" + n, [P, 1024], F32)) for n in "qkv"}
            raw_loaded = {n: ctx.enter_context(nc.semaphore("raw_loaded_" + n)) for n in "qkv"}

            with nc.Block() as block:
                @block.sync
                def _(sp):
                    for i in range(LOADS):
                        rows = slice(i * TOKENS // LOADS, (i + 1) * TOKENS // LOADS)
                        sp.dma_start(X[:, i * TILES // LOADS:(i + 1) * TILES // LOADS, :],
                                     d["x"][rows, :].rearrange("(t p) n -> p t n", p=P)).then_inc(x_loaded[i], 16)
                        if i == 0:
                            sp.dma_start(ident[:, :], d["ident"]).then_inc(consts_loaded, 16)
                    for n in "qkv":
                        sp.dma_start(w_raw[n][:, :], d["w" + n][0]).then_inc(raw_loaded[n], 16)
                    sp.wait_ge(consts_loaded, 16)

            xT = [phase.enter_context(nc.sbuf_tensor("xT_" + n, [P, KD, TOKENS], F32R)) for n in ("hi", "lo")]
            layernorm_transposed(nc, X, x_loaded, LOADS, ident, "l1_", *xT)
            segment_attention(nc, X, ident, xT, w_raw, raw_loaded, d, consts_loaded, attT, head_raw, head_loaded)

        with ExitStack() as phase:
            def sb(name, shape, dt=F32):
                return phase.enter_context(nc.sbuf_tensor("t_" + name, shape, dt))

            def parts(name, shape):
                return sb(name + "_hi", shape, F32R), sb(name + "_lo", shape, F32R)

            qc = parts("qc", [P, QC, TOKENS])
            attention_output(nc, X, d, ident, attT, x1, qc, head_raw, head_loaded, context_loaded)
            reuse_semaphores(nc)
            raw_r = sb("raw_r", [P, QC, P])
            semaphores = {n: ctx.enter_context(nc.semaphore("x_" + n)) for n in
                          ("raw_loaded", "raw_r_loaded", "x1_loaded")}
            T = {"ident": ident, "context_loaded": context_loaded, **semaphores, "qc": qc, "raw_r": raw_r,
                 "raw": head_raw[0][:, :].rearrange("p (h n) -> p h n", h=2),
                 "prob": head_raw[1][:, :].rearrange("p (t h k) -> p t h k", t=CT, h=2),
                 "cos": sb("cos", [P, KEYS]), "sin": sb("sin", [P, KEYS]),
                 "mask": sb("mask", [P, TILES, KEYS], BF16), "kvT": parts("kvT", [P, TOKENS]),
                 "kv": parts("kv", [P, TILES, P]), "kr": parts("kr", [P, SEQS, 2, KEYS])}
            latents(nc, d, T, X, x1)
            cross_attention(nc, X, d, T)

        with ExitStack() as phase:
            def sb(name, shape, dt=F32):
                return phase.enter_context(nc.sbuf_tensor("g_" + name, shape, dt))

            F = {"mv": sb("mv", [P, TILES, 2]), "rstd": sb("rstd", [P, TILES]),
                 "shift": sb("shift", [P, TILES]), "magic": sb("magic", [P, 1]),
                 "scale_w": sb("scale_w", [P, 2]), "h": sb("h", [P, KD * D], F32R),
                 "t": [sb("up_t", [P, D * FF // P], BF16), sb("down_t", [P, D * FF // P], BF16)]}
            ternary_weights(nc, X, d, F)
            feed_forward(nc, X, d, F, ident, out)


def lay_out(inputs):
    f = {k: np.asarray(v) for k, v in inputs.items()}
    a = {"x": f["x"].reshape(TOKENS, D)}
    a["ident"] = np.eye(P, dtype=np.float32)
    s = np.arange(P)
    a["causal"] = np.where(s[None, :] <= s[:, None], 0.0, NEG).astype(np.float32)
    a["betas"] = f["L0_attn_betas"].reshape(HEADS, P).T
    for n in "qkv":
        a["w" + n] = f["L0_attn_W" + n].reshape(KD, P, PAIRS, 256).transpose(2, 1, 0, 3).reshape(PAIRS, P, 1024)
    a["wo"] = f["L0_attn_Wo"].reshape(HEADS, P, D).transpose(1, 0, 2)
    def rows(w, n):
        return w.reshape(n, P, -1).transpose(1, 0, 2)

    def filled(w):
        return np.concatenate([w, w[P:]])

    a["ctxT"] = f["ctx_2048"].reshape(CHUNKS, CHUNK, KD, P).transpose(0, 3, 2, 1)
    kr = f["L0_xattn_W_kr"].reshape(P, 2, 1, 32)
    a["wkv"] = np.concatenate([rows(f["L0_xattn_W_kvc"], KD), np.repeat(kr, 2, 2).reshape(P, 1, P)], 1)
    a["wdq"] = rows(np.ascontiguousarray(filled(f["L0_xattn_W_dq"].T).T), KD)
    a["ids"] = f["itok_BxS_0_1023"].reshape(TILES, P).T
    a["kio"] = np.broadcast_to(np.arange(KEYS, dtype=np.float32), (P, KEYS))
    freq = np.float32(1.0) / np.float32(10000.0) ** (np.arange(32, dtype=np.float32) / np.float32(32))
    ang = (np.arange(KEYS, dtype=np.float32)[:, None] * freq).T
    a["cos"] = np.tile(np.cos(ang), (4, 1))
    a["sin"] = np.concatenate([np.tile(-np.sin(ang), (2, 1)), np.tile(np.sin(ang), (2, 1))])
    head_of_row = np.arange(P) // 32 % 2
    a["rows_of"] = np.stack([head_of_row == 0, head_of_row == 1], 1).astype(np.float32)
    uq = filled(f["L0_xattn_W_uq"]).reshape(QC * P, PAIRS, 2, P).transpose(1, 3, 2, 0)
    uk = f["L0_xattn_W_uk"].reshape(P, PAIRS, 2, P).transpose(1, 3, 2, 0)
    uv = f["L0_xattn_W_uv"].reshape(P, PAIRS, 2, P).transpose(1, 3, 2, 0)
    wo = f["L0_xattn_W_o"].reshape(PAIRS, 2, P, D).transpose(0, 2, 1, 3)
    a["xw"] = np.concatenate([uq, uk, uv, wo], 3)
    qr = filled(f["L0_xattn_W_qr"]).reshape(QC, P, PAIRS, 2, 2, 32)
    a["xwr"] = qr.transpose(2, 1, 0, 4, 3, 5).reshape(PAIRS, P, QC, P)
    a["up"] = rows(f["L0_ffn_w_up"].T, KD).reshape(P, -1)
    a["down"] = rows(f["L0_ffn_w_down"].T, KF).reshape(P, -1)
    sylvester = np.ones((1, 1), np.float32)
    while len(sylvester) < D:
        sylvester = np.block([[sylvester, sylvester], [sylvester, -sylvester]])
    a["hadamard"] = rows(sylvester, KD).reshape(P, -1)
    return {k: np.ascontiguousarray(v) for k, v in a.items()}


def kernel(**inputs):
    import concourse.bacc as _bacc
    from concourse.bass_utils import run_bass_kernel_spmd as _run

    nc = _bacc.Bacc("TRN2", target_bir_lowering=False, num_devices=1, dynamic_dma_scratch_size=1024)
    arrays = lay_out(inputs)
    d = {k: nc.dram_tensor("in_" + k, v.shape, mybir.dt.from_np(v.dtype), kind="ExternalInput").ap()
         for k, v in arrays.items()}
    out = nc.dram_tensor("out_x", (TOKENS, D), F32, kind="ExternalOutput").ap()
    decoder_layer(nc, d, out)
    r = _run(nc, [{"in_" + k: v for k, v in arrays.items()}], core_ids=[0])
    return r.results[0]["out_x"].reshape(8, 256, D)
```
